# Optimizing a Trainium2 kernel written in Bass

```python
import numpy as np
import jax
import jax.numpy as jnp

def _softmax(x, axis=-1):
    return jax.nn.softmax(x, axis=axis)

def _gelu(x):
    return jax.nn.gelu(x, approximate=True)

def _silu(x):
    return jax.nn.silu(x)

def _sigmoid(x):
    return jax.nn.sigmoid(x)

def _layernorm(x, axis=-1, eps=1e-05):
    m = jnp.mean(x, axis=axis, keepdims=True)
    v = jnp.var(x, axis=axis, keepdims=True)
    return (x - m) / jnp.sqrt(v + eps)

def _scatter_add(tgt, idx, src, axis=0):
    return tgt.at[idx].add(src)

def _segment_sum(src, seg, n):
    return jax.ops.segment_sum(src, seg, n)
kernel_name = 'mk_gnn_preln_d4_gnn_r64_176454'

def setup_inputs(seed: int=0):
    np.random.seed(seed)
    _w = jnp.asarray

    def _rec_inputs():
        import jax
        import jax.numpy as jnp
        _gk = jax.random.key(seed)
        x = -0.000202 + 1 * jax.random.normal(jax.random.fold_in(_gk, 1), (50000, 128), jnp.float32)
        src = jax.random.randint(jax.random.fold_in(_gk, 2), (25000,), 0, 50000, jnp.int32)
        dst = jax.random.randint(jax.random.fold_in(_gk, 3), (25000,), 0, 50000, jnp.int32)
        _o = jnp.argsort(dst, stable=True)
        src = src[_o]
        dst = dst[_o]
        edge_attr_64 = -7.08334e-05 + 0.999895 * jax.random.normal(jax.random.fold_in(_gk, 11), (25000, 64), jnp.float32)
        edge_weight = jax.random.uniform(jax.random.fold_in(_gk, 13), (25000,), jnp.float32, 0.0, 0.999999)
        return (x, src, dst, edge_attr_64, edge_weight)
    x, src, dst, edge_attr_64, edge_weight = _rec_inputs()

    def _L0_gnn_setup():
        import jax, jax.numpy as jnp
        import numpy as np
        N_NODES = 50000
        N_HEDGES = 10000
        NNZ = 9375
        D = 128

        def _hconv(x, W, b, src, dst):
            x = x @ W
            ones = jnp.ones(src.shape, x.dtype)
            deg_n = jax.ops.segment_sum(ones, src, num_segments=N_NODES)
            deg_e = jax.ops.segment_sum(ones, dst, num_segments=N_HEDGES)
            Dinv = jnp.where(deg_n > 0, 1.0 / deg_n, 0.0)
            Binv = jnp.where(deg_e > 0, 1.0 / deg_e, 0.0)
            he = Binv[:, None] * jax.ops.segment_sum(x[src], dst, num_segments=N_HEDGES)
            out = Dinv[:, None] * jax.ops.segment_sum(he[dst], src, num_segments=N_NODES)
            return out + b
        key = jax.random.key(seed)
        k = jax.random.split(key, 6)
        x = jax.random.normal(k[0], (N_NODES, D), jnp.float32)
        src = jax.random.randint(k[1], (NNZ,), 0, N_NODES, dtype=jnp.int32)
        dst = jax.random.randint(k[2], (NNZ,), 0, N_HEDGES, dtype=jnp.int32)
        edge_index = jnp.stack([src, dst], axis=0)
        scale = 1.0 / np.sqrt(D)
        W1 = jax.random.normal(k[3], (D, D), jnp.float32) * scale
        W2 = jax.random.normal(k[4], (D, D), jnp.float32) * scale
        b1 = jnp.zeros((D,), jnp.float32)
        b2 = jnp.zeros((D,), jnp.float32)
        return {'x': x, 'edge_index': edge_index, 'W1': W1, 'b1': b1, 'W2': W2, 'b2': b2}
    _L0_gnn_all = _L0_gnn_setup()
    _L0_gnn_in = {k: v for k, v in _L0_gnn_all.items() if k in ('W1', 'b1', 'W2', 'b2')}
    del _L0_gnn_all

    def _L1_gnn_setup():
        import jax, jax.numpy as jnp
        import numpy as np
        import math
        N_NODES = 100000
        N_EDGES = 25000
        DIM = 128
        key = jax.random.key(seed)
        ks = jax.random.split(key, 6)
        x = jax.random.normal(ks[0], (N_NODES, DIM), dtype=jnp.float32)
        edge_index = jax.random.randint(ks[1], (2, N_EDGES), 0, N_NODES, dtype=jnp.int64)
        limit = 0.1 * math.sqrt(6.0 / (DIM + DIM))
        Wqk = jax.random.uniform(ks[2], (DIM, DIM), dtype=jnp.float32, minval=-limit, maxval=limit)
        Wv = jax.random.uniform(ks[3], (DIM, DIM), dtype=jnp.float32, minval=-limit, maxval=limit)
        Wo = jax.random.uniform(ks[4], (DIM, DIM), dtype=jnp.float32, minval=-limit, maxval=limit)
        return {'x': x, 'edge_index': edge_index, 'Wqk': Wqk, 'bqk': jnp.zeros((DIM,), jnp.float32), 'Wv': Wv, 'bv': jnp.zeros((DIM,), jnp.float32), 'Wo': Wo, 'bo': jnp.zeros((DIM,), jnp.float32), 'gamma': jnp.ones((DIM,), jnp.float32), 'beta': jnp.zeros((DIM,), jnp.float32)}
    _L1_gnn_all = _L1_gnn_setup()
    _L1_gnn_in = {k: v for k, v in _L1_gnn_all.items() if k in ('Wqk', 'bqk', 'Wv', 'bv', 'Wo', 'bo', 'gamma', 'beta')}
    del _L1_gnn_all

    def _L2_gnn_setup():
        import jax, jax.numpy as jnp
        import numpy as np
        N, E = (50000, 9375)
        NODE_DIM, EDGE_DIM, MSG_DIM = (128, 64, 128)
        key = jax.random.key(seed)
        ks = jax.random.split(key, 8)
        s = 0.05
        return {'node_features': jax.random.normal(ks[0], (N, NODE_DIM), jnp.float32), 'edge_features': jax.random.normal(ks[1], (E, EDGE_DIM), jnp.float32), 'edge_index': jax.random.randint(ks[2], (2, E), 0, N, jnp.int32), 'We1': jax.random.normal(ks[3], (2 * NODE_DIM + EDGE_DIM, 32), jnp.float32) * s, 'be1': jnp.zeros((32,), jnp.float32), 'We2': jax.random.normal(ks[4], (32, MSG_DIM), jnp.float32) * s, 'be2': jnp.zeros((MSG_DIM,), jnp.float32), 'Wn1': jax.random.normal(ks[5], (NODE_DIM + MSG_DIM, 64), jnp.float32) * s, 'bn1': jnp.zeros((64,), jnp.float32), 'Wn2': jax.random.normal(ks[6], (64, MSG_DIM), jnp.float32) * s, 'bn2': jnp.zeros((MSG_DIM,), jnp.float32)}
    _L2_gnn_all = _L2_gnn_setup()
    _L2_gnn_in = {k: v for k, v in _L2_gnn_all.items() if k in ('We1', 'be1', 'We2', 'be2', 'Wn1', 'bn1', 'Wn2', 'bn2')}
    del _L2_gnn_all

    def _L3_gnn_setup():
        import jax, jax.numpy as jnp
        import numpy as np
        N_NODES = 100000
        N_EDGES = 25000
        D_IN = 128
        D_OUT = 128
        BN_EPS = 1e-05
        key = jax.random.key(seed)
        ks = jax.random.split(key, 6)
        x = jax.random.normal(ks[0], (N_NODES, D_IN), dtype=jnp.float32)
        edge_index = jax.random.randint(ks[1], (2, N_EDGES), 0, N_NODES, dtype=jnp.int32)
        edge_weight = jax.random.uniform(ks[2], (N_EDGES,), dtype=jnp.float32)
        W = jax.random.normal(ks[3], (D_IN, D_OUT), dtype=jnp.float32) / np.sqrt(D_IN)
        b = jax.random.normal(ks[4], (D_OUT,), dtype=jnp.float32) * 0.01
        gamma = jnp.ones((D_OUT,), dtype=jnp.float32)
        beta = jnp.zeros((D_OUT,), dtype=jnp.float32)
        return {'x': x, 'edge_index': edge_index, 'edge_weight': edge_weight, 'W': W, 'b': b, 'gamma': gamma, 'beta': beta}
    _L3_gnn_all = _L3_gnn_setup()
    _L3_gnn_in = {k: v for k, v in _L3_gnn_all.items() if k in ('W', 'b', 'gamma', 'beta')}
    del _L3_gnn_all
    return {'x': x, 'src': src, 'dst': dst, 'edge_attr_64': edge_attr_64, 'edge_weight': edge_weight, 'L0_gnn_W1': _L0_gnn_in['W1'], 'L0_gnn_b1': _L0_gnn_in['b1'], 'L0_gnn_W2': _L0_gnn_in['W2'], 'L0_gnn_b2': _L0_gnn_in['b2'], 'L1_gnn_Wqk': _L1_gnn_in['Wqk'], 'L1_gnn_bqk': _L1_gnn_in['bqk'], 'L1_gnn_Wv': _L1_gnn_in['Wv'], 'L1_gnn_bv': _L1_gnn_in['bv'], 'L1_gnn_Wo': _L1_gnn_in['Wo'], 'L1_gnn_bo': _L1_gnn_in['bo'], 'L1_gnn_gamma': _L1_gnn_in['gamma'], 'L1_gnn_beta': _L1_gnn_in['beta'], 'L2_gnn_We1': _L2_gnn_in['We1'], 'L2_gnn_be1': _L2_gnn_in['be1'], 'L2_gnn_We2': _L2_gnn_in['We2'], 'L2_gnn_be2': _L2_gnn_in['be2'], 'L2_gnn_Wn1': _L2_gnn_in['Wn1'], 'L2_gnn_bn1': _L2_gnn_in['bn1'], 'L2_gnn_Wn2': _L2_gnn_in['Wn2'], 'L2_gnn_bn2': _L2_gnn_in['bn2'], 'L3_gnn_W': _L3_gnn_in['W'], 'L3_gnn_b': _L3_gnn_in['b'], 'L3_gnn_gamma': _L3_gnn_in['gamma'], 'L3_gnn_beta': _L3_gnn_in['beta']}

def reference(x, src, dst, edge_attr_64, edge_weight, L0_gnn_W1, L0_gnn_b1, L0_gnn_W2, L0_gnn_b2, L1_gnn_Wqk, L1_gnn_bqk, L1_gnn_Wv, L1_gnn_bv, L1_gnn_Wo, L1_gnn_bo, L1_gnn_gamma, L1_gnn_beta, L2_gnn_We1, L2_gnn_be1, L2_gnn_We2, L2_gnn_be2, L2_gnn_Wn1, L2_gnn_bn1, L2_gnn_Wn2, L2_gnn_bn2, L3_gnn_W, L3_gnn_b, L3_gnn_gamma, L3_gnn_beta):
    import jax
    import jax.numpy as jnp

    def _L0_gnn_ref(x, edge_index, W1, b1, W2, b2):
        import jax, jax.numpy as jnp
        import numpy as np
        N_NODES = 50000
        N_HEDGES = 10000
        NNZ = 9375
        D = 128

        def _hconv(x, W, b, src, dst):
            x = x @ W
            ones = jnp.ones(src.shape, x.dtype)
            deg_n = jax.ops.segment_sum(ones, src, num_segments=N_NODES)
            deg_e = jax.ops.segment_sum(ones, dst, num_segments=N_HEDGES)
            Dinv = jnp.where(deg_n > 0, 1.0 / deg_n, 0.0)
            Binv = jnp.where(deg_e > 0, 1.0 / deg_e, 0.0)
            he = Binv[:, None] * jax.ops.segment_sum(x[src], dst, num_segments=N_HEDGES)
            out = Dinv[:, None] * jax.ops.segment_sum(he[dst], src, num_segments=N_NODES)
            return out + b
        src, dst = (edge_index[0], edge_index[1])
        h = _hconv(x, W1, b1, src, dst)
        h = jax.nn.relu(h)
        return _hconv(h, W2, b2, src, dst)

    def _L1_gnn_ref(x, edge_index, Wqk, bqk, Wv, bv, Wo, bo, gamma, beta):
        import jax, jax.numpy as jnp
        import numpy as np
        import math
        N_NODES = 100000
        N_EDGES = 25000
        DIM = 128
        N, D = x.shape
        qk = x @ Wqk + bqk
        v = x @ Wv + bv
        src = edge_index[0]
        dst = edge_index[1]
        scores = jnp.sum(qk[dst] * qk[src], axis=-1) / jnp.sqrt(jnp.float32(D))
        scores = jnp.clip(scores, -5.0, 5.0)
        m = jax.ops.segment_max(scores, dst, num_segments=N)
        e = jnp.exp(scores - m[dst])
        s = jax.ops.segment_sum(e, dst, num_segments=N)
        attn = e / s[dst]
        out = jax.ops.segment_sum(attn[:, None] * v[src], dst, num_segments=N)
        out = out @ Wo + bo
        h = out + x
        mu = jnp.mean(h, axis=-1, keepdims=True)
        var = jnp.mean(jnp.square(h - mu), axis=-1, keepdims=True)
        return gamma * (h - mu) / jnp.sqrt(var + 1e-05) + beta

    def _L2_gnn_ref(node_features, edge_features, edge_index, We1, be1, We2, be2, Wn1, bn1, Wn2, bn2):
        import jax, jax.numpy as jnp
        import numpy as np
        N, E = (50000, 9375)
        NODE_DIM, EDGE_DIM, MSG_DIM = (128, 64, 128)
        src, dst = (edge_index[0], edge_index[1])
        src_f = node_features[src]
        dst_f = node_features[dst]
        edge_in = jnp.concatenate([src_f, dst_f, edge_features], axis=1)
        h = jax.nn.relu(edge_in @ We1 + be1)
        edge_msg = jax.nn.relu(h @ We2 + be2)
        node_in = jnp.concatenate([dst_f, edge_msg], axis=1)
        h2 = jax.nn.relu(node_in @ Wn1 + bn1)
        node_msg = jax.nn.relu(h2 @ Wn2 + bn2)
        agg = jax.ops.segment_sum(node_msg, dst, num_segments=node_features.shape[0])
        return node_features + agg

    def _L3_gnn_ref(x, edge_index, edge_weight, W, b, gamma, beta):
        import jax, jax.numpy as jnp
        import numpy as np
        N_NODES = 100000
        N_EDGES = 25000
        D_IN = 128
        D_OUT = 128
        BN_EPS = 1e-05
        n = x.shape[0]
        self_loops = jnp.arange(n, dtype=edge_index.dtype)
        row = jnp.concatenate([edge_index[0], self_loops])
        col = jnp.concatenate([edge_index[1], self_loops])
        ew = jnp.concatenate([edge_weight, jnp.ones((n,), x.dtype)])
        deg = jax.ops.segment_sum(jnp.ones_like(ew), row, num_segments=n)
        dinv = jnp.where(deg > 0, jax.lax.rsqrt(deg), 0.0)
        norm = dinv[row] * dinv[col] * ew
        h = x @ W + b
        msgs = norm[:, None] * h[row]
        out = jax.ops.segment_sum(msgs, col, num_segments=n)
        mean = jnp.mean(out, axis=0)
        var = jnp.mean(jnp.square(out - mean), axis=0)
        out = (out - mean) * jax.lax.rsqrt(var + BN_EPS) * gamma + beta
        return jax.nn.relu(out)
    edge_index = jnp.stack([src, dst])
    h = jnp.maximum(_layernorm(x, axis=-1), 0.0)
    x = x + _L0_gnn_ref(h, edge_index, L0_gnn_W1, L0_gnn_b1, L0_gnn_W2, L0_gnn_b2)
    h = jnp.maximum(_layernorm(x, axis=-1), 0.0)
    x = x + _L1_gnn_ref(h, edge_index, L1_gnn_Wqk, L1_gnn_bqk, L1_gnn_Wv, L1_gnn_bv, L1_gnn_Wo, L1_gnn_bo, L1_gnn_gamma, L1_gnn_beta)
    h = jnp.maximum(_layernorm(x, axis=-1), 0.0)
    x = x + _L2_gnn_ref(h, edge_attr_64, edge_index, L2_gnn_We1, L2_gnn_be1, L2_gnn_We2, L2_gnn_be2, L2_gnn_Wn1, L2_gnn_bn1, L2_gnn_Wn2, L2_gnn_bn2)
    h = jnp.maximum(_layernorm(x, axis=-1), 0.0)
    x = x + _L3_gnn_ref(h, edge_index, edge_weight, L3_gnn_W, L3_gnn_b, L3_gnn_gamma, L3_gnn_beta)
    return x

_drawn_inputs = setup_inputs


def setup_inputs(seed=0):
    import zlib

    import numpy as np

    out = dict(_drawn_inputs(seed))
    spreads = {'L0_gnn_b1': (0.0, 0.45),
     'L0_gnn_b2': (0.0, 0.1),
     'L1_gnn_bqk': (0.0, 2.0),
     'L1_gnn_bv': (0.0, 0.8),
     'L1_gnn_bo': (0.0, 0.29),
     'L1_gnn_gamma': (1.0, 0.2),
     'L1_gnn_beta': (0.0, 0.355),
     'L2_gnn_be1': (0.0, 2.0),
     'L2_gnn_be2': (0.0, 2.0),
     'L2_gnn_bn1': (0.0, 2.0),
     'L2_gnn_bn2': (0.0, 0.322),
     'L3_gnn_gamma': (1.0, 0.6),
     'L3_gnn_beta': (0.0, 0.36)}
    factors = {'edge_attr_64': 8.0,
     'L1_gnn_Wqk': 8.0,
     'L1_gnn_Wv': 8.0,
     'L1_gnn_Wo': 8.0,
     'L2_gnn_We1': 8.0,
     'L2_gnn_We2': 8.0,
     'L2_gnn_Wn1': 2.688,
     'L3_gnn_b': 64.0,
     'edge_weight': 3.575}
    for name, (base, spread) in spreads.items():
        noise = np.random.default_rng([zlib.crc32(name.encode()), seed]).standard_normal(out[name].shape)
        drawn = base * np.exp(spread * noise) if base else spread * noise
        out[name] = jnp.asarray(drawn.astype(out[name].dtype))
    for name, factor in factors.items():
        out[name] = (out[name] * factor).astype(out[name].dtype)
    return out
```

```python
from contextlib import ExitStack, contextmanager

import concourse.bass as bass
from concourse import mybir

F32 = mybir.dt.float32
BF16 = mybir.dt.bfloat16
I32 = mybir.dt.int32
ALU = mybir.AluOpType
ACT = mybir.ActivationFunctionType
AX_X = mybir.AxisListType.X

P = 128
D = 128
N = 50000
E = 25000
HEDGES = 10000
G = 4
NT = 200
EP = NT * P
NGE = NT // G
LOW_STEP = 2 * G * P
NHI, NLO = 196, 256
HB = NHI // 2
NN = NHI * NLO
NGN = NN // (P * G)
XW = 136
TW = 132
RW = 260
EPS = 1e-5
M_DINV, M_CHIGH, M_GINV, M_INDEX, M_BINV, M_GINV2, M_BARE, M_Q = range(8)
K_ID = 0
K_AFTER = K_ID + P
K_IOTA = K_AFTER + P
K_NODE = K_IOTA + NLO
K_EDGE = K_NODE + 2 * NLO
K_LAST = K_EDGE + NT
K_DUMP = K_LAST + 1
K_ONE = K_DUMP + 1
K_ROW1 = K_ONE + P
K_COLS = K_ROW1 + P


def pipeline(eng, n, parts, slots=2):
    deep = max(lag for _, lag in parts)
    looped = (n - deep) // slots * slots

    def step(k):
        for part, lag in parts:
            if 0 <= k - lag < n:
                part(k - lag, (k - lag) % slots)

    for k in range(deep):
        step(k)
    with eng.Fori(0, looped - slots + 1, slots) as i:
        for k in range(deep, deep + slots):
            for part, lag in parts:
                part(i + (k - lag), (k - lag) % slots)
    for k in range(deep + looped, n + deep):
        step(k)


def bounded(eng, count, part):
    with eng.Fori(0, count - 1, 2) as i:
        part(i, 0)
        part(i + 1, 1)


def build(nc, t, debug):
    root = ExitStack()
    with root:
        def dram(name, shape):
            return nc.dram_tensor(name, shape, F32, kind="ExternalOutput" if debug else "Internal").ap()

        meta_d = dram("meta_d", (NN, 8))
        sum1_d = dram("sum1_d", (NN + P, D))
        x1_d = dram("x1_d", (NN + P, XW))
        he_d = dram("he_d", (EP + P, D))
        att_d = dram("att_d", (EP, TW))
        xd_d = dram("xd_d", (EP, XW))
        x2_d = dram("x2_d", (NN + EP, D))
        r_d = dram("r_d", (NN + EP, RW))

        stage = [0]

        def sb(name, shape, dt=F32, ctx=root):
            return ctx.enter_context(nc.sbuf_tensor(f"{name}_{stage[0]}", shape, dt))

        def sem(name):
            return nc.alloc_semaphore(f"{name}_{stage[0]}")

        @contextmanager
        def phase():
            stage[0] += 1
            with nc.cleanup_on_exit(), ExitStack() as c:
                yield c

        K = sb("K", [P, K_COLS])
        ident = K[:, K_ID:K_ID + P]
        after = K[:, K_AFTER:K_AFTER + P]
        last_row = K[:, K_LAST:K_LAST + 1]
        dump_row = K[:, K_DUMP:K_DUMP + 1]
        edge_no = K[:, K_EDGE:K_EDGE + NT]
        ones = K[:, K_ONE:K_ONE + P]
        srcF = sb("srcF", [P, NT])
        dstF = sb("dstF", [P, NT + 1])
        ew = sb("ew", [P, NT])
        srcI = sb("srcI", [P, NT], I32)
        dstI = sb("dstI", [P, NT], I32)
        low = sb("low", [P, NT])
        seg_end = sb("seg_end", [P, NT])
        out_row = sb("out_row", [P, NT], I32)
        he_index = sb("he_index", [P, NT], I32)
        meta_src = sb("meta_src", [P, NT, 8])
        meta_dst = sb("meta_dst", [P, NT, 8])
        table_src = sb("table_src", [P, NT], I32)
        table_dst = sb("table_dst", [P, NT], I32)
        ginv_dst = sb("ginv_dst", [P, NT])
        he_last = [sb("he_last0", [P, D]), sb("he_last1", [P, D])]
        low_groups = sb("low_groups", [P, 1], I32)
        minus_half = sb("minus_half", [P, 16])
        W = {n: sb("w_" + n, [P, D]) for n in
             ("W1", "W2", "Wvo", "We1a", "We1b", "We1c", "We2", "Wn1a", "Wn1b", "Wn2", "W3")}
        Wscore = sb("Wscore", [P, D + 1])
        urow = sb("urow", [1, 2 * TW])
        R = {n: sb("r_" + n, [P, D]) for n in ("b1", "b2", "bo", "bvo", "gamma", "beta", "bgamma", "bbeta", "b3")}
        C = {n: sb("c_" + n, [P, 1]) for n in ("be1", "be2", "bn1", "bqk", "bv")}
        wb = sb("wb", [2, D])
        gram1 = sb("gram1", [P, D + 2])
        gram2 = sb("gram2", [2, D + 2])
        bank = [root.enter_context(nc.psum_tensor(f"bank{i}", [P, 512], F32)) for i in range(8)]
        passed = {n: sem("passed_" + n) for n in ("pool", "dve", "act", "pe", "sp")}

        def hold(name, eng, s, value):
            eng.wait_ge(s, value)
            eng.sem_inc(passed[name], 1)

        def rows_of(table, g, width, first=0):
            return table[bass.ds(g * (G * P) + first, G * P), 0:width].rearrange("(j p) f -> p j f", p=P)

        def node_rows_of(table, g, width):
            return table[bass.ds(g * (G * P), G * P), 0:width].rearrange("(p j) f -> p j f", p=P)

        with phase() as c:
            rows = sb("rows", [NT // 2, 3, 2, P], I32, c)
            rowsF = sb("rowsF", [NT // 2, 4, 2, P], F32, c)
            zeros = sb("zeros", [P, 28 * D], F32, c)
            wq, wv, wo, wqT, wvT = (sb(f"ld_{n}", [P, D], F32, c) for n in ("q", "v", "o", "qT", "vT"))
            tmpF, nextF, high = (sb(n, [P, NT], F32, c) for n in ("tmpF", "nextF", "high"))
            tmpI = sb("tmpI", [P, NT], I32, c)
            split = {n: sb("sp_" + n, [P, NT], F32, c) for n in ("hs", "ls", "hd", "ld")}
            cnt = sb("cnt", [P, 1], F32, c)
            iota = sb("iota_b", [P, NLO], BF16, c)
            hot_s = sb("hot_s", [P, 2, NHI + 2 * NLO], BF16, c)
            hot_d = sb("hot_d", [P, 2, NHI + NLO], BF16, c)
            deg = {n: sb("deg_" + n, [HB, 2 * NLO], F32, c) for n in ("s", "h", "d")}
            a = {n: sb("a_" + n, [HB, 2 * NLO], F32, c) for n in ("x", "y", "z", "w", "half")}
            totals = sb("totals", [HB, 2], F32, c)
            meta = sb("meta", [HB, 2 * NLO, 8], F32, c)
            loads, zeroed, zero_ready, vec, columns_ps, columns_in, weights_ps, hot_ready, hot_used, \
                counts_ps, deg_ready, pow_done, totals_ready, offsets_ps, meta_ready, meta_out, act_link = (sem(n) for n in (
                    "loads", "zeroed", "zero_ready", "vec", "columns_ps", "columns_in", "weights_ps", "hot_ready",
                    "hot_used", "counts_ps", "deg_ready", "pow_done", "totals_ready", "offsets_ps", "meta_ready",
                    "meta_out", "act_link"))

            def as_col(ap):
                return ap.rearrange("(n a) -> n a", a=1)

            plan = [(K[:, :], t["consts"])]
            plan += [(rows[:, k, :, :], t[n].rearrange("(a r p) -> r a p", a=2, p=P)) for k, n in
                     enumerate(("src", "dst", "next_dst"))]
            plan += [(rowsF[:, 3, :, :], t["edge_weight"].rearrange("(a r p) -> r a p", a=2, p=P))]
            plan += [(wq[:, :], t["L1_gnn_Wqk"]), (wv[:, :], t["L1_gnn_Wv"]), (wo[:, :], t["L1_gnn_Wo"]),
                     (W["W1"][:, :], t["L0_gnn_W1"]), (W["W2"][:, :], t["L0_gnn_W2"]), (W["W3"][:, :], t["L3_gnn_W"]),
                     (W["We1a"][:, 0:32], t["L2_gnn_We1"][0:D, :]), (W["We1b"][:, 0:32], t["L2_gnn_We1"][D:2 * D, :]),
                     (W["We1c"][0:64, 0:32], t["L2_gnn_We1"][2 * D:2 * D + 64, :]), (W["We2"][0:32, :], t["L2_gnn_We2"]),
                     (W["Wn1a"][:, 0:64], t["L2_gnn_Wn1"][0:D, :]), (W["Wn1b"][:, 0:64], t["L2_gnn_Wn1"][D:2 * D, :]),
                     (W["Wn2"][0:64, :], t["L2_gnn_Wn2"]),
                     (W["Wn2"][64:65, :], t["L2_gnn_bn2"].rearrange("(a n) -> a n", a=1)),
                     (C["be1"][0:32, :], as_col(t["L2_gnn_be1"])), (C["be2"][:, :], as_col(t["L2_gnn_be2"])),
                     (C["bn1"][0:64, :], as_col(t["L2_gnn_bn1"])), (C["bqk"][:, :], as_col(t["L1_gnn_bqk"])),
                     (C["bv"][:, :], as_col(t["L1_gnn_bv"])),
                     (wb[0:1, :], t["L3_gnn_b"].rearrange("(a n) -> a n", a=1)),
                     (wb[1:2, :], t["consts"][0:1, K_ROW1:K_ROW1 + P])]
            plan += [(R[dst][:, :], t[n].partition_broadcast(P)) for dst, n in
                     (("b1", "L0_gnn_b1"), ("b2", "L0_gnn_b2"), ("bo", "L1_gnn_bo"), ("gamma", "L1_gnn_gamma"),
                      ("beta", "L1_gnn_beta"), ("bgamma", "L3_gnn_gamma"), ("bbeta", "L3_gnn_beta"), ("b3", "L3_gnn_b"))]
            count = [0]

            with nc.Block() as block:
                @block.sync
                def _(sp):
                    for dst, src in plan:
                        sp.dma_start(dst, src).then_inc(loads, 16)
                    sp.wait_ge(zero_ready, 1)
                    for k in range(NN // (P * 28)):
                        sp.dma_start(sum1_d[k * P * 28:(k + 1) * P * 28, :].rearrange("(p r) f -> p (r f)", p=P),
                                     zeros[:, :]).then_inc(zeroed, 16)
                    for k in range(EP // (P * 25)):
                        sp.dma_start(he_d[k * P * 25:(k + 1) * P * 25, :].rearrange("(p r) f -> p (r f)", p=P),
                                     zeros[:, 0:25 * D]).then_inc(zeroed, 16)
                    for part in (sum1_d[NN:NN + P, :], he_d[EP:EP + P, :]):
                        sp.dma_start(part, zeros[:, 0:D]).then_inc(zeroed, 16)
                    sp.dma_start(x1_d[NN:NN + P, :], zeros[:, 0:XW]).then_inc(zeroed, 16)
                    sp.wait_ge(meta_ready, 1)
                    sp.dma_start(meta_d.rearrange("(a p l) m -> p a (l m)", a=2, p=HB),
                                 meta[:, :, :].rearrange("p (a l) m -> p a (l m)", a=2)).then_inc(meta_out, 16)
                    sp.wait_ge(meta_out, 16)
                    sp.wait_ge(zeroed, 16 * (NN // (P * 28) + EP // (P * 25) + 3))

                @block.gpsimd
                def _(pool):
                    nc.gpsimd.memset(zeros[:, :], 0.0).then_inc(zero_ready, 1)
                    nc.gpsimd.memset(minus_half[:, :], -0.5)
                    nc.gpsimd.memset(a["half"][:, :], -0.5).then_inc(pow_done, 1)
                    pool.wait_ge(pow_done, 1)
                    pool.wait_ge(deg_ready, 1)
                    nc.gpsimd.tensor_tensor(a["w"][:, :], a["w"][:, :], a["half"][:, :], ALU.pow).then_inc(pow_done, 1)

                @block.tensor
                def _(pe):
                    pe.wait_ge(loads, 16 * len(plan))
                    nc.tensor.transpose(bank[4][:, 0:D], wq[:, :], ident)
                    nc.tensor.transpose(bank[4][:, D:2 * D], wv[:, :], ident).then_inc(weights_ps, 1)
                    pe.wait_ge(columns_in, 1)
                    for k in range(4):
                        for b in range(2):
                            last = nc.tensor.transpose(bank[k][:, b * (NT // 2):(b + 1) * (NT // 2)], rowsF[:, k, b, :],
                                                       K[0:NT // 2, K_ID:K_ID + NT // 2])
                    last.then_inc(columns_ps, 1)
                    pe.wait_ge(act_link, 1)
                    nc.tensor.matmul(bank[5][:, 0:D], wqT[:, :], wqT[:, :], start=True, stop=True)
                    nc.tensor.matmul(bank[5][:, D:D + 1], wqT[:, :], C["bqk"][:, :], start=True, stop=True)
                    nc.tensor.matmul(bank[6][0:1, 0:D], C["bqk"][:, :], wqT[:, :], start=True, stop=True)
                    nc.tensor.matmul(bank[6][0:1, D:D + 1], C["bqk"][:, :], C["bqk"][:, :], start=True, stop=True)
                    nc.tensor.matmul(bank[7][:, 0:D], wvT[:, :], wo[:, :], start=True, stop=True)
                    nc.tensor.matmul(bank[7][:, D:2 * D], C["bv"][:, :].to_broadcast([P, P]), wo[:, :], start=True,
                                     stop=True).then_inc(weights_ps, 1)
                    pe.wait_ge(columns_in, 3)
                    nc.tensor.matmul(bank[4][:, 0:1], ones, cnt[:, :], start=True, stop=True).then_inc(weights_ps, 1)

                    def counts(g, s):
                        pe.wait_ge(hot_ready, g + 1)
                        for b in range(2):
                            nc.tensor.matmul(bank[b][0:HB, :], hot_s[:, s, b * HB:(b + 1) * HB],
                                             hot_s[:, s, NHI:], start=False, stop=False, skip_group_check=True)
                            last = nc.tensor.matmul(bank[2 + b][0:HB, 0:NLO], hot_d[:, s, b * HB:(b + 1) * HB],
                                                    hot_d[:, s, NHI:], start=False, stop=False, skip_group_check=True)
                        last.then_inc(hot_used, 1)
                    pipeline(pe, NT, [(counts, 0)])
                    pe.wait_ge(totals_ready, 1)
                    nc.tensor.matmul(bank[4][0:HB, 0:2], K[0:HB, K_AFTER:K_AFTER + HB], totals[:, :], start=True, stop=True)
                    nc.tensor.matmul(bank[4][0:HB, 2:3], ones[0:HB, 0:HB], totals[:, 0:1], start=True,
                                     stop=True).then_inc(offsets_ps, 1)

                @block.scalar
                def _(act):
                    act.wait_ge(weights_ps, 1)
                    nc.scalar.activation(wqT[:, :], bank[4][:, 0:D], ACT.Copy)
                    nc.scalar.activation(wvT[:, :], bank[4][:, D:2 * D], ACT.Copy).then_inc(act_link, 1)
                    act.wait_ge(weights_ps, 2)
                    nc.scalar.activation(Wscore[:, :], bank[5][:, 0:D + 1], ACT.Copy)
                    for j in range(2):
                        nc.scalar.activation(urow[:, j * TW:j * TW + D + 1], bank[6][0:1, 0:D + 1], ACT.Copy)
                    nc.scalar.activation(W["Wvo"][:, :], bank[7][:, 0:D], ACT.Copy).then_inc(act_link, 1)

                @block.vector
                def _(dve):
                    def link(ins):
                        count[0] += 1
                        ins.then_inc(vec, 1)
                        dve.wait_ge(vec, count[0])

                    dve.wait_ge(loads, 16 * len(plan))
                    nc.vector.tensor_copy(rowsF[:, 0:3, :, :], rows[:, :, :, :]).then_inc(columns_in, 1)
                    dve.wait_ge(columns_ps, 1)
                    for k, dst in enumerate((srcF[:, :], dstF[:, 1:NT + 1], nextF[:, :], ew[:, :])):
                        link(nc.vector.tensor_copy(dst, bank[k][:, 0:NT]))
                    for k in range(4):
                        link(nc.vector.memset(bank[k][:, :], 0.0))
                    link(nc.vector.memset(dstF[:, 0:1], -1.0))
                    link(nc.vector.tensor_copy(srcI[:, :], srcF[:, :]))
                    link(nc.vector.tensor_copy(dstI[:, :], dstF[:, 1:NT + 1]))
                    for whole, hi, lo in ((srcI, "hs", "ls"), (dstI, "hd", "ld")):
                        link(nc.vector.tensor_single_scalar(tmpI[:, :], whole[:, :], 8, ALU.arith_shift_right))
                        link(nc.vector.tensor_copy(split[hi][:, :], tmpI[:, :]))
                        link(nc.vector.tensor_single_scalar(tmpI[:, :], whole[:, :], NLO - 1, ALU.bitwise_and))
                        link(nc.vector.tensor_copy(split[lo][:, :], tmpI[:, :]))
                    link(nc.vector.tensor_scalar(high[:, :], dstF[:, 1:NT + 1], float(HEDGES), None, ALU.is_ge))
                    link(nc.vector.tensor_scalar(low[:, :], dstF[:, 1:NT + 1], float(HEDGES), None, ALU.is_lt))
                    link(nc.vector.tensor_copy(iota[:, :], K[:, K_IOTA:K_IOTA + NLO]))
                    link(nc.vector.tensor_reduce(cnt[:, :], low[:, :], AX_X, ALU.add))
                    link(nc.vector.tensor_tensor(seg_end[:, :], dstF[:, 1:NT + 1], nextF[:, :], ALU.not_equal))
                    link(nc.vector.tensor_scalar(tmpF[:, :], edge_no, float(NN), None, ALU.add))
                    link(nc.vector.tensor_tensor(nextF[:, :], dstF[:, 1:NT + 1], tmpF[:, :], ALU.subtract))
                    link(nc.vector.tensor_tensor(nextF[:, :], nextF[:, :], seg_end[:, :], ALU.mult))
                    link(nc.vector.tensor_tensor(nextF[:, :], nextF[:, :], tmpF[:, :], ALU.add))
                    link(nc.vector.tensor_copy(out_row[:, :], nextF[:, :]))
                    link(nc.vector.tensor_scalar(tmpF[:, :], dstF[:, 1:NT + 1], float(N), None, ALU.is_lt))
                    link(nc.vector.tensor_tensor(seg_end[:, :], seg_end[:, :], tmpF[:, :], ALU.mult))
                    for m in (meta_src, meta_dst):
                        link(nc.vector.memset(m[:, :, :], 0.0))
                    dve.wait_ge(act_link, 2)
                    nc.vector.tensor_tensor(R["bvo"][:, :], bank[7][:, D:2 * D], R["bo"][:, :], ALU.add).then_inc(columns_in, 2)
                    dve.wait_ge(weights_ps, 3)
                    link(nc.vector.tensor_scalar(cnt[:, :], bank[4][:, 0:1], 1.0, float(LOW_STEP - 1), ALU.max, ALU.add))
                    link(nc.vector.tensor_copy(low_groups[:, :], cnt[:, :]))
                    link(nc.vector.tensor_single_scalar(low_groups[:, :], low_groups[:, :], 10, ALU.arith_shift_right))
                    link(nc.vector.tensor_copy(cnt[:, :], low_groups[:, :]))
                    link(nc.vector.tensor_scalar(cnt[:, :], cnt[:, :], 2.0, None, ALU.mult))
                    link(nc.vector.tensor_copy(low_groups[:, :], cnt[:, :]))

                    dve.sem_inc(hot_used, 2)

                    def hots(g, s):
                        at = bass.ds(g, 1)
                        dve.wait_ge(hot_used, g + 1)
                        for out, hi, lo in ((hot_s, "hs", "ls"), (hot_d, "hd", "ld")):
                            nc.vector.tensor_scalar(out[:, s, 0:NHI], iota[:, 0:NHI], split[hi][:, at], None, ALU.is_equal)
                            nc.vector.tensor_scalar(out[:, s, NHI:NHI + NLO], iota[:, :], split[lo][:, at], None,
                                                    ALU.is_equal)
                        nc.vector.tensor_scalar(hot_s[:, s, NHI + NLO:NHI + 2 * NLO], iota[:, :], split["ls"][:, at],
                                                high[:, at], ALU.is_equal, ALU.mult).then_inc(hot_ready, 1)
                    pipeline(dve, NT, [(hots, 0)])

                    dve.wait_ge(hot_used, NT + 2)
                    for b in range(2):
                        cols = slice(b * NLO, (b + 1) * NLO)
                        link(nc.vector.tensor_copy(deg["s"][:, cols], bank[b][0:HB, 0:NLO]))
                        link(nc.vector.tensor_copy(deg["h"][:, cols], bank[b][0:HB, NLO:2 * NLO]))
                        link(nc.vector.tensor_copy(deg["d"][:, cols], bank[2 + b][0:HB, 0:NLO]))
                    nc.vector.tensor_scalar(a["w"][:, :], deg["s"][:, :], 1.0, None, ALU.add).then_inc(deg_ready, 1)
                    node = K[0:HB, K_NODE:K_NODE + 2 * NLO]
                    link(nc.vector.tensor_scalar(a["x"][:, :], deg["s"][:, :], 1.0, None, ALU.max))
                    link(nc.vector.reciprocal(a["x"][:, :], a["x"][:, :]))
                    link(nc.vector.tensor_scalar(a["y"][:, :], deg["s"][:, :], 1.0, None, ALU.min))
                    link(nc.vector.tensor_tensor(a["x"][:, :], a["x"][:, :], a["y"][:, :], ALU.mult))
                    link(nc.vector.tensor_copy(meta[:, :, M_DINV], a["x"][:, :]))
                    link(nc.vector.tensor_tensor(meta[:, :, M_CHIGH], a["x"][:, :], deg["h"][:, :], ALU.mult))
                    link(nc.vector.tensor_scalar(a["x"][:, :], deg["d"][:, :], 1.0, None, ALU.max))
                    link(nc.vector.reciprocal(meta[:, :, M_BINV], a["x"][:, :]))
                    link(nc.vector.memset(a["y"][:, :], 1.0))
                    for b in range(2):
                        cols = slice(b * NLO, (b + 1) * NLO)
                        link(nc.vector.tensor_tensor_scan(a["z"][:, cols], a["y"][:, cols], deg["d"][:, cols], 0.0,
                                                          ALU.mult, ALU.add))
                        link(nc.vector.tensor_copy(totals[:, b:b + 1], a["z"][:, (b + 1) * NLO - 1:(b + 1) * NLO]))
                    dve.sem_inc(totals_ready, 1)
                    dve.wait_ge(offsets_ps, 1)
                    link(nc.vector.tensor_copy(a["x"][:, 0:3], bank[4][0:HB, 0:3]))
                    link(nc.vector.tensor_tensor(a["x"][:, 1:2], a["x"][:, 1:2], a["x"][:, 2:3], ALU.add))
                    for b in range(2):
                        cols = slice(b * NLO, (b + 1) * NLO)
                        link(nc.vector.tensor_scalar(a["z"][:, cols], a["z"][:, cols], a["x"][:, b:b + 1], None, ALU.add))
                    link(nc.vector.tensor_scalar(a["z"][:, :], a["z"][:, :], float(NN - 1), None, ALU.add))
                    link(nc.vector.tensor_tensor(a["z"][:, :], a["z"][:, :], node, ALU.subtract))
                    link(nc.vector.tensor_scalar(a["y"][:, :], deg["d"][:, :], 1.0, None, ALU.min))
                    link(nc.vector.tensor_tensor(a["z"][:, :], a["z"][:, :], a["y"][:, :], ALU.mult))
                    link(nc.vector.tensor_tensor(meta[:, :, M_INDEX], a["z"][:, :], node, ALU.add))
                    link(nc.vector.tensor_scalar(a["x"][:, :], node, float(N), None, ALU.is_lt))
                    link(nc.vector.tensor_scalar(a["y"][:, :], a["y"][:, :], -1.0, 1.0, ALU.mult, ALU.add))
                    link(nc.vector.tensor_tensor(a["x"][:, :], a["x"][:, :], a["y"][:, :], ALU.mult))
                    link(nc.vector.tensor_copy(meta[:, :, M_BARE], a["x"][:, :]))
                    dve.wait_ge(pow_done, 2)
                    link(nc.vector.tensor_copy(meta[:, :, M_GINV], a["w"][:, :]))
                    link(nc.vector.tensor_tensor(a["w"][:, :], a["w"][:, :], a["w"][:, :], ALU.mult))
                    link(nc.vector.tensor_copy(meta[:, :, M_GINV2], a["w"][:, :]))
                    nc.vector.tensor_tensor(meta[:, :, M_Q], a["w"][:, :], a["x"][:, :], ALU.mult).then_inc(meta_ready, 1)

        with phase() as c:
            xin = sb("xin", [P, 2, 8, D], F32, c)
            min_ = sb("min", [P, 2, 8, 8], F32, c)
            xout = sb("xout", [P, 2, 8, XW], F32, c)
            in_sem = [sem("xt_in0"), sem("xt_in1")]
            x_added, m_copied = sem("xt_added"), sem("xt_meta")
            out_sem = [sem("xt_out0"), sem("xt_out1")]
            chunk = 8 * P
            nch = NN // chunk

            with nc.Block() as block:
                @block.sync
                def _(sp):
                    sp.sem_inc(x_added, 2)
                    sp.sem_inc(m_copied, 2)

                    def load(g, s):
                        sp.wait_ge(x_added, g + 1)
                        sp.dma_start(xin[:, s, :, :], t["x"][bass.ds(g * chunk, chunk), :].rearrange("(p j) f -> p j f", p=P)).then_inc(in_sem[s], 16)
                        sp.wait_ge(m_copied, g + 1)
                        sp.dma_start(min_[:, s, :, :], meta_d[bass.ds(g * chunk, chunk), :].rearrange("(p j) f -> p j f", p=P)).then_inc(in_sem[s], 16)
                    pipeline(sp, nch, [(load, 0)])

                @block.vector
                def _(dve):
                    for s in range(2):
                        dve.sem_inc(out_sem[s], 16)

                    def add(g, s):
                        dve.wait_ge(in_sem[s], (g - s) * 16 + 32)
                        dve.wait_ge(out_sem[s], (g - s) * 8 + 16)
                        nc.vector.tensor_tensor(xout[:, s, :, 0:D], xin[:, s, :, :],
                                                R["b2"][:, :].unsqueeze(1).to_broadcast([P, 8, D]), ALU.add).then_inc(x_added, 1)
                        nc.vector.tensor_copy(xout[:, s, :, D:XW], min_[:, s, :, :]).then_inc(m_copied, 1)
                    pipeline(dve, nch, [(add, 0)])

                @block.scalar
                def _(act):
                    def store(g, s):
                        act.wait_ge(m_copied, g + 3)
                        act.dma_start(x1_d[bass.ds(g * chunk, chunk), :].rearrange("(p j) f -> p j f", p=P), xout[:, s, :, :]).then_inc(out_sem[s], 16)
                    pipeline(act, nch, [(store, 0)])
                    for s in range(2):
                        act.wait_ge(out_sem[s], 16 * ((nch + 1 - s) // 2) + 16)
        def layer_sums(dve, tiles, st, tmp, neg, var, link, ready, g):
            n = len(tiles)
            for j, x in enumerate(tiles):
                last = nc.vector.bn_stats(st[:, j, :], x)
            last.then_inc(link, 1)
            dve.wait_ge(link, g * 4 + 1)
            nc.vector.tensor_tensor(tmp[:, 0, 0:n], st[:, 0:n, 1], st[:, 0:n, 4], ALU.add)
            nc.vector.tensor_tensor(tmp[:, 1, 0:n], st[:, 0:n, 1], st[:, 0:n, 4], ALU.subtract)
            nc.vector.tensor_tensor(tmp[:, 2, 0:n], st[:, 0:n, 2], st[:, 0:n, 5], ALU.add).then_inc(link, 1)
            dve.wait_ge(link, g * 4 + 2)
            nc.vector.tensor_scalar(neg, tmp[:, 0, 0:n], -0.5, None, ALU.mult)
            nc.vector.tensor_tensor(tmp[:, 1, 0:n], tmp[:, 1, 0:n], tmp[:, 1, 0:n], ALU.mult).then_inc(link, 1)
            dve.wait_ge(link, g * 4 + 3)
            nc.vector.scalar_tensor_tensor(out=tmp[:, 2, 0:n], in0=tmp[:, 1, 0:n], scalar=D / 4.0, in1=tmp[:, 2, 0:n],
                                           op0=ALU.mult, op1=ALU.add).then_inc(link, 1)
            dve.wait_ge(link, g * 4 + 4)
            nc.vector.tensor_scalar(var, tmp[:, 2, 0:n], 1.0 / D, EPS, ALU.mult, ALU.add).then_inc(ready, 1)

        def layer_scale(pool, neg, var, rs, nb, n, summed, link, ready, g):
            pool.wait_ge(summed, g + 1)
            nc.gpsimd.tensor_tensor(rs, var, minus_half[:, 0:n], ALU.pow).then_inc(link, 1)
            pool.wait_ge(link, g + 1)
            nc.gpsimd.tensor_tensor(nb, neg, rs, ALU.mult).then_inc(ready, 1)

        def gather(pool, out, table, index, s):
            pool.indirect_dma_start(out=out, out_offset=None, in_=table,
                                    in_offset=bass.IndirectOffsetOnAxis(ap=index, axis=0)).then_inc(s, 16)

        def groups_of_low(eng):
            return eng.value_load(low_groups[0:1, 0:1], min_val=2, max_val=NGE)

        def hyperedges(conv):
            with phase() as c:
                ix = sb("ix", [P, 2, 2 * G], I32, c)
                col = sb("col", [P, 2, G + 1], F32, c)
                rows = sb("rows", [P, 2, G, D], F32, c)
                ms, md = (sb(n, [P, 2, G, 8], F32, c) for n in ("ms", "md"))
                st = sb("st", [P, G, 6], F32, c)
                tmp = sb("tmp", [P, 3, G], F32, c)
                neg, var, rs, nb = (sb(n, [P, 2, G], F32, c) for n in ("neg", "var", "rs", "nb"))
                h = sb("h", [P, 2, G, D], F32, c)
                same, carry, sumT, out = (sb(n, [P, 2, G, P], F32, c) for n in ("same", "carry", "sumT", "out"))
                whole = sb("whole", [P, 2, G, D], F32, c)
                cols_ready, pool_link, summed, scaled, link, h_ready, bc_ps, same_ready, sumT_ps, sumT_in, he_ps, \
                    whole_in, out_ready, meta_kept, front = (sem(f"he_{n}") for n in (
                        "cols_ready", "pool_link", "summed", "scaled", "link", "h_ready", "bc_ps", "same_ready",
                        "sumT_ps", "sumT_in", "he_ps", "whole_in", "out_ready", "meta_kept", "front"))
                rows_in = [sem("he_rows_in0"), sem("he_rows_in1")]
                stored = [sem("he_stored0"), sem("he_stored1")]
                bc, sT, hps = bank[0], bank[1], [bank[2], bank[3]]
                weight = W["W1"] if conv == 0 else W["W2"]
                n_in = 16 * G * (3 if conv == 0 else 1)

                with nc.Block() as block:
                    @block.gpsimd
                    def _(pool):
                        n = groups_of_low(pool)

                        def part(g, s):
                            hold("pool", pool, stored[s], (g - s) * 8 + 16)
                            nc.gpsimd.tensor_copy(ix[:, s, 0:G], srcI[:, bass.ds(g * G, G)])
                            if conv == 0:
                                nc.gpsimd.tensor_copy(ix[:, s, G:2 * G], dstI[:, bass.ds(g * G, G)])
                            else:
                                nc.gpsimd.tensor_copy(ms[:, s, :, :], meta_src[:, bass.ds(g * G, G), :])
                                nc.gpsimd.tensor_copy(md[:, s, :, :], meta_dst[:, bass.ds(g * G, G), :])
                            nc.gpsimd.tensor_copy(col[:, s, :], dstF[:, bass.ds(g * G, G + 1)]).then_inc(cols_ready, 1)
                            hold("pool", pool, cols_ready, g + 1)
                            for j in range(G):
                                gather(pool, rows[:, s, j, :], t["x"] if conv == 0 else sum1_d, ix[:, s, j:j + 1], rows_in[s])
                                if conv == 0:
                                    gather(pool, ms[:, s, j, :], meta_d, ix[:, s, j:j + 1], rows_in[s])
                                    gather(pool, md[:, s, j, :], meta_d, ix[:, s, G + j:G + j + 1], rows_in[s])
                            if conv == 0:
                                layer_scale(pool, neg[:, s, :], var[:, s, :], rs[:, s, :], nb[:, s, :], G, summed,
                                            pool_link, scaled, g)
                        bounded(pool, n, part)

                    @block.vector
                    def _(dve):
                        n = groups_of_low(dve)
                        nc.vector.memset(whole[:, 1, G - 1, :], 0.0).then_inc(whole_in, 1)

                        def part(g, s):
                            dve.wait_ge(rows_in[s], ((g - s) // 2) * n_in + n_in)
                            if conv == 0:
                                layer_sums(dve, [rows[:, s, j, :] for j in range(G)], st, tmp, neg[:, s, :], var[:, s, :],
                                           link, summed, g)
                                nc.vector.tensor_copy(meta_src[:, bass.ds(g * G, G), :], ms[:, s, :, :])
                                nc.vector.tensor_copy(meta_dst[:, bass.ds(g * G, G), :], md[:, s, :, :])
                            else:
                                for j in range(G):
                                    last = nc.vector.scalar_tensor_tensor(
                                        out=rows[:, s, j, :], in0=rows[:, s, j, :], scalar=ms[:, s, j, M_DINV:M_DINV + 1],
                                        in1=R["b1"][:, :], op0=ALU.mult, op1=ALU.add)
                                last.then_inc(link, 1)
                                dve.wait_ge(link, g + 1)
                                for j in range(G):
                                    last = nc.vector.scalar_tensor_tensor(
                                        out=rows[:, s, j, :], in0=he_last[0][:, :], scalar=ms[:, s, j, M_CHIGH:M_CHIGH + 1],
                                        in1=rows[:, s, j, :], op0=ALU.mult, op1=ALU.add)
                                last.then_inc(scaled, 1)
                            dve.wait_ge(bc_ps, g + 1)
                            for j in range(G):
                                nc.vector.tensor_scalar(same[:, s, j, :], bc[:, j * P:(j + 1) * P], col[:, s, j + 1:j + 2],
                                                        None, ALU.is_equal)
                                last = nc.vector.tensor_scalar(carry[:, s, j, :], bc[:, j * P:(j + 1) * P], col[:, s, j:j + 1],
                                                               last_row, ALU.is_equal, ALU.mult)
                            last.then_inc(same_ready, 1)
                            dve.wait_ge(whole_in, g * G + G + 1)
                            for j in range(G):
                                last = nc.vector.tensor_scalar(out[:, s, j, :], whole[:, s, j, :],
                                                               md[:, s, j, M_BINV:M_BINV + 1], None, ALU.mult)
                            last.then_inc(out_ready, 1)
                        bounded(dve, n, part)

                    @block.scalar
                    def _(act):
                        act.preload_act_table(ACT.Relu)
                        n = groups_of_low(act)

                        def part(g, s):
                            act.wait_ge(scaled, g + 1)
                            if conv == 0:
                                for j in range(G):
                                    last = nc.scalar.activation(h[:, s, j, :], rows[:, s, j, :], ACT.Relu,
                                                                bias=nb[:, s, j:j + 1], scale=rs[:, s, j:j + 1])
                            else:
                                last = nc.scalar.activation(h[:, s, :, :], rows[:, s, :, :], ACT.Relu)
                            last.then_inc(h_ready, 1)
                            act.wait_ge(sumT_ps, g + 1)
                            nc.scalar.activation(sumT[:, s, :, :], sT[:, :].rearrange("p (j f) -> p j f", j=G),
                                                 ACT.Copy).then_inc(sumT_in, 1)
                            for j in range(G):
                                act.wait_ge(he_ps, g * G + j + 1)
                                nc.scalar.activation(whole[:, s, j, :], hps[j % 2][:, 0:D], ACT.Copy).then_inc(whole_in, 1)
                        bounded(act, n, part)

                    @block.tensor
                    def _(pe):
                        n = groups_of_low(pe)
                        pe.sem_inc(same_ready, 1)

                        def part(g, s):
                            pe.wait_ge(cols_ready, g + 1)
                            pe.wait_ge(same_ready, g + 1)
                            for j in range(G):
                                last = nc.tensor.transpose(bc[:, j * P:(j + 1) * P],
                                                           col[:, s, j + 1:j + 2].to_broadcast([P, P]), ident)
                            last.then_inc(bc_ps, 1)
                            pe.wait_ge(h_ready, g + 1)
                            pe.wait_ge(same_ready, g + 2)
                            for j in range(G):
                                last = nc.tensor.matmul(sT[:, j * P:(j + 1) * P], h[:, s, j, :], same[:, s, j, :],
                                                        start=True, stop=True)
                            last.then_inc(sumT_ps, 1)
                            pe.wait_ge(sumT_in, g + 1)
                            for j in range(G):
                                before = whole[:, s, j - 1, :] if j else whole[:, 1 - s, G - 1, :]
                                nc.tensor.matmul(hps[j % 2][:, 0:D], sumT[:, s, j, :], weight[:, :], start=True, stop=False)
                                pe.wait_ge(whole_in, g * G + j + 1)
                                nc.tensor.matmul(hps[j % 2][:, 0:D], carry[:, s, j, :], before, start=False,
                                                 stop=True).then_inc(he_ps, 1)
                        bounded(pe, n, part)

                    @block.sync
                    def _(sp):
                        n = groups_of_low(sp)
                        for s in range(2):
                            sp.sem_inc(stored[s], 16)

                        def part(g, s):
                            sp.wait_ge(out_ready, g + 1)
                            sp.dma_start(rows_of(he_d, g, D), out[:, s, :, :]).then_inc(stored[s], 16)
                            hold("sp", sp, stored[s], (g - s) * 8 + 32)
                        bounded(sp, n, part)

        def last_hyperedge(conv):
            with phase() as c:
                m = sb("m", [P, 8], F32, c)
                v = sb("v", [P, 4], F32, c)
                vi = sb("vi", [P, 1], I32, c)
                e = sb("e", [P, NT], F32, c)
                m_in, link, v_ready, row_in = (sem(f"last_{n}") for n in ("m_in", "link", "v_ready", "row_in"))
                with nc.Block() as block:
                    @block.sync
                    def _(sp):
                        sp.dma_start(m[:, :], meta_d[HEDGES - 1, :].partition_broadcast(P)).then_inc(m_in, 16)

                    @block.vector
                    def _(dve):
                        k = [0]

                        def chain(ins):
                            k[0] += 1
                            ins.then_inc(link, 1)
                            dve.wait_ge(link, k[0])

                        dve.wait_ge(m_in, 16)
                        chain(nc.vector.tensor_scalar(v[:, 0:1], m[:, M_INDEX:M_INDEX + 1], float(NN), None, ALU.is_ge))
                        chain(nc.vector.tensor_scalar(v[:, 1:2], m[:, M_INDEX:M_INDEX + 1], float(-NN - EP), None, ALU.add))
                        chain(nc.vector.tensor_tensor(v[:, 2:3], v[:, 0:1], v[:, 1:2], ALU.mult))
                        chain(nc.vector.tensor_scalar(v[:, 3:4], v[:, 2:3], float(EP), None, ALU.add))
                        nc.vector.tensor_copy(vi[:, :], v[:, 3:4]).then_inc(v_ready, 1)
                        if conv == 0:
                            chain(nc.vector.tensor_tensor(e[:, :], meta_dst[:, :, M_INDEX], edge_no, ALU.subtract))
                            chain(nc.vector.tensor_scalar(e[:, :], e[:, :], float(-NN), None, ALU.add))
                            chain(nc.vector.tensor_tensor(e[:, :], e[:, :], low[:, :], ALU.mult))
                            chain(nc.vector.tensor_tensor(e[:, :], e[:, :], edge_no, ALU.add))
                            chain(nc.vector.tensor_copy(he_index[:, :], e[:, :]))

                    @block.gpsimd
                    def _(pool):
                        pool.wait_ge(v_ready, 1)
                        gather(pool, he_last[conv][:, :], he_d, vi[:, :], row_in)
                        pool.wait_ge(row_in, 16)

        def to_sources(conv):
            with phase() as c:
                width = D if conv == 0 else XW
                ix = sb("ix", [P, 2, G], I32, c)
                col = sb("col", [P, 2, G], F32, c)
                lo = sb("lo", [P, 2, G], F32, c)
                dinv = sb("dinv", [P, 2, G], F32, c)
                rows = sb("rows", [P, 2, G, D], F32, c)
                same = sb("same", [P, 2, G, P], F32, c)
                junk = sb("junk", [P, P], F32, c)
                later = sb("later", [P, 3, G], F32, c)
                to = sb("to", [P, 2, G], I32, c)
                add = sb("add", [P, 2, G, width], F32, c)
                cols_ready, bc_ps, same_ready, comb_ps, add_ready, to_ready, link, added, cleared, comb_free = (
                    sem(f"ts_{n}") for n in ("cols_ready", "bc_ps", "same_ready", "comb_ps", "add_ready", "to_ready",
                                             "link", "added", "cleared", "comb_free"))
                rows_in = [sem("ts_rows_in0"), sem("ts_rows_in1")]
                bc, comb = bank[0], bank[1]
                table = sum1_d if conv == 0 else x1_d

                with nc.Block() as block:
                    @block.gpsimd
                    def _(pool):
                        n = groups_of_low(pool)
                        nc.gpsimd.memset(add[:, :, :, :], 0.0).then_inc(cleared, 1)

                        def part(g, s):
                            nc.gpsimd.tensor_copy(ix[:, s, :], he_index[:, bass.ds(g * G, G)])
                            nc.gpsimd.tensor_copy(col[:, s, :], srcF[:, bass.ds(g * G, G)])
                            nc.gpsimd.tensor_copy(dinv[:, s, :], meta_src[:, bass.ds(g * G, G), M_DINV])
                            nc.gpsimd.tensor_copy(lo[:, s, :], low[:, bass.ds(g * G, G)]).then_inc(cols_ready, 1)
                            hold("pool", pool, cols_ready, g + 1)
                            for j in range(G):
                                gather(pool, rows[:, s, j, :], he_d, ix[:, s, j:j + 1], rows_in[s])
                            hold("pool", pool, to_ready, g + 1)
                            hold("pool", pool, add_ready, g + 1)
                            for j in range(G):
                                pool.indirect_dma_start(out=table, out_offset=bass.IndirectOffsetOnAxis(ap=to[:, s, j:j + 1], axis=0),
                                                        in_=add[:, s, j, :], in_offset=None, compute_op=ALU.add).then_inc(added, 16)
                                hold("pool", pool, added, (g * G + j) * 16 + 16)
                        bounded(pool, n, part)

                    @block.tensor
                    def _(pe):
                        n = groups_of_low(pe)

                        def part(g, s):
                            pe.wait_ge(cols_ready, g + 1)
                            for j in range(G):
                                last = nc.tensor.transpose(bc[:, j * P:(j + 1) * P], col[:, s, j:j + 1].to_broadcast([P, P]), ident)
                            last.then_inc(bc_ps, 1)
                            pe.wait_ge(same_ready, g + 1)
                            hold("pe", pe, rows_in[s], (g - s) * (8 * G) + 16 * G)
                            for j in range(G):
                                last = nc.tensor.matmul(comb[:, j * P:(j + 1) * P], same[:, s, j, :], rows[:, s, j, :],
                                                        start=True, stop=True)
                            last.then_inc(comb_ps, 1)
                        bounded(pe, n, part)

                    @block.vector
                    def _(dve):
                        n = groups_of_low(dve)

                        def part(g, s):
                            dve.wait_ge(bc_ps, g + 1)
                            for j in range(G):
                                nc.vector.tensor_scalar(same[:, s, j, :], bc[:, j * P:(j + 1) * P], col[:, s, j:j + 1],
                                                        lo[:, s, j:j + 1], ALU.is_equal, ALU.mult)
                                last = nc.vector.scalar_tensor_tensor(out=junk[:, :], in0=bc[:, j * P:(j + 1) * P],
                                                                      scalar=col[:, s, j:j + 1], in1=after, op0=ALU.is_equal,
                                                                      op1=ALU.mult, accum_out=later[:, 0, j:j + 1])
                                last.then_inc(link, 1)
                                dve.wait_ge(link, g * (G + 3) + j + 1)
                            dve.sem_inc(same_ready, 1)
                            nc.vector.tensor_scalar(later[:, 1, :], later[:, 0, :], 1.0, None, ALU.min)
                            nc.vector.tensor_scalar(later[:, 2, :], col[:, s, :], -1.0, dump_row, ALU.mult, ALU.add).then_inc(link, 1)
                            dve.wait_ge(link, g * (G + 3) + G + 1)
                            nc.vector.tensor_tensor(later[:, 1, :], later[:, 1, :], later[:, 2, :], ALU.mult).then_inc(link, 1)
                            dve.wait_ge(link, g * (G + 3) + G + 2)
                            nc.vector.tensor_tensor(later[:, 2, :], later[:, 1, :], col[:, s, :], ALU.add).then_inc(link, 1)
                            dve.wait_ge(link, g * (G + 3) + G + 3)
                            nc.vector.tensor_copy(to[:, s, :], later[:, 2, :]).then_inc(to_ready, 1)
                            dve.wait_ge(to_ready, g + 1)
                        bounded(dve, n, part)

                    @block.scalar
                    def _(act):
                        act.preload_act_table(ACT.Copy)
                        act.wait_ge(cleared, 1)
                        n = groups_of_low(act)

                        def part(g, s):
                            act.wait_ge(comb_ps, g + 1)
                            for j in range(G):
                                if conv == 0:
                                    last = nc.scalar.activation(add[:, s, j, 0:D], comb[:, j * P:(j + 1) * P], ACT.Copy)
                                else:
                                    last = nc.scalar.activation(add[:, s, j, 0:D], comb[:, j * P:(j + 1) * P], ACT.Copy,
                                                                scale=dinv[:, s, j:j + 1])
                            last.then_inc(add_ready, 1)
                        bounded(act, n, part)

        for conv in range(2):
            hyperedges(conv)
            last_hyperedge(conv)
            to_sources(conv)
        S = 4

        def slot_count(g, s, dmas):
            return (g - s) * (16 // S * dmas) + 16 * dmas

        with phase() as c:
            ix = sb("ix", [P, S, 2 * G], I32, c)
            col = sb("col", [P, S, G + 1], F32, c)
            xs, xd = (sb(n, [P, S, G, XW], F32, c) for n in ("xs", "xd"))
            st = sb("st", [P, 2 * G, 6], F32, c)
            tmp = sb("tmp", [P, 3, 2 * G], F32, c)
            neg, var, rs, nb = (sb(n, [P, S, 2 * G], F32, c) for n in ("neg", "var", "rs", "nb"))
            hs = sb("hs", [P, S, G, TW], F32, c)
            hd = sb("hd", [P, S, G, D], F32, c)
            hdT = sb("hdT", [P, S, G * P], F32, c)
            junk = sb("junk", [P, D + 1], F32, c)
            score, e = (sb(n, [P, S, G], F32, c) for n in ("score", "e"))
            same, carry = (sb(n, [P, S, G, P], F32, c) for n in ("same", "carry"))
            sums = sb("sums", [P, S, G, TW], F32, c)
            cols_ready, pool_link, summed, scaled, link, he_link, h_ready, hdT_ps, hdT_in, r_ps, clip_link, score_ready, \
                e_ready, bc_ps, same_ready, sum_ps, sum_in, ones_set = (sem(f"at_{n}") for n in (
                    "cols_ready", "pool_link", "summed", "scaled", "link", "he_link", "h_ready", "hdT_ps", "hdT_in",
                    "r_ps", "clip_link", "score_ready", "e_ready", "bc_ps", "same_ready", "sum_ps", "sum_in", "ones_set"))
            rows_in = [sem(f"at_rows_in{s}") for s in range(S)]
            stored = [sem(f"at_stored{s}") for s in range(S)]
            tp, rp, bcp, sp_ = bank[0], [bank[1], bank[2]], [bank[3], bank[4]], [bank[5], bank[6]]

            with nc.Block() as block:
                @block.gpsimd
                def _(pool):
                    def rows(g, s):
                        hold("pool", pool, stored[s], slot_count(g, s, 2))
                        nc.gpsimd.tensor_copy(ix[:, s, 0:G], srcI[:, bass.ds(g * G, G)])
                        nc.gpsimd.tensor_copy(ix[:, s, G:2 * G], dstI[:, bass.ds(g * G, G)])
                        nc.gpsimd.tensor_copy(col[:, s, :], dstF[:, bass.ds(g * G, G + 1)]).then_inc(cols_ready, 1)
                        hold("pool", pool, cols_ready, g + 1)
                        for j in range(G):
                            gather(pool, xs[:, s, j, :], x1_d, ix[:, s, j:j + 1], rows_in[s])
                            gather(pool, xd[:, s, j, :], x1_d, ix[:, s, G + j:G + j + 1], rows_in[s])

                    def scale(g, s):
                        layer_scale(pool, neg[:, s, :], var[:, s, :], rs[:, s, :], nb[:, s, :], 2 * G, summed, pool_link,
                                    scaled, g)
                    pipeline(pool, NGE, [(rows, 0), (scale, 1)], S)

                @block.vector
                def _(dve):
                    nc.vector.memset(hs[:, :, :, D:D + 1], 1.0).then_inc(ones_set, 1)
                    nc.vector.memset(sums[:, S - 1, G - 1, :], 0.0).then_inc(sum_in, 1)
                    dve.sem_inc(score_ready, 1)

                    def stats(g, s):
                        dve.wait_ge(rows_in[s], slot_count(g, s, 2 * G))
                        for x in (xs, xd):
                            for j in range(G):
                                last = nc.vector.scalar_tensor_tensor(
                                    out=x[:, s, j, 0:D], in0=he_last[1][:, :], scalar=x[:, s, j, D + M_CHIGH:D + M_CHIGH + 1],
                                    in1=x[:, s, j, 0:D], op0=ALU.mult, op1=ALU.add)
                        nc.vector.tensor_copy(table_src[:, bass.ds(g * G, G)], xs[:, s, :, D + M_INDEX])
                        nc.vector.tensor_copy(table_dst[:, bass.ds(g * G, G)], xd[:, s, :, D + M_INDEX])
                        nc.vector.tensor_copy(ginv_dst[:, bass.ds(g * G, G)], xd[:, s, :, D + M_GINV])
                        last.then_inc(he_link, 1)
                        dve.wait_ge(he_link, g + 1)
                        layer_sums(dve, [x[:, s, j, 0:D] for x in (xs, xd) for j in range(G)], st, tmp, neg[:, s, :],
                                   var[:, s, :], link, summed, g)

                    def scores(g, s):
                        dve.wait_ge(r_ps, g + 1)
                        for j in range(G):
                            last = nc.vector.scalar_tensor_tensor(
                                out=junk[:, :], in0=rp[j // 2][:, (j % 2) * TW:(j % 2) * TW + D + 1], scalar=float(D) ** -0.5,
                                in1=hs[:, s, j, 0:D + 1], op0=ALU.mult, op1=ALU.mult, accum_out=score[:, s, j:j + 1])
                            last.then_inc(clip_link, 1)
                            dve.wait_ge(clip_link, g * G + j + 1)
                        nc.vector.tensor_scalar(score[:, s, :], score[:, s, :], 5.0, -5.0, ALU.min, ALU.max).then_inc(score_ready, 1)

                    def sames(g, s):
                        dve.wait_ge(e_ready, g + 1)
                        dve.wait_ge(bc_ps, g + 1)
                        for j in range(G):
                            bc = bcp[s % 2][:, j * P:(j + 1) * P]
                            nc.vector.tensor_scalar(same[:, s, j, :], bc, col[:, s, j + 1:j + 2], e[:, s, j:j + 1],
                                                    ALU.is_equal, ALU.mult)
                            last = nc.vector.tensor_scalar(carry[:, s, j, :], bc, col[:, s, j:j + 1], last_row,
                                                           ALU.is_equal, ALU.mult)
                        last.then_inc(same_ready, 1)
                    pipeline(dve, NGE, [(sames, 2), (stats, 0), (scores, 1)], S)

                @block.scalar
                def _(act):
                    act.preload_act_table(ACT.Exp)
                    act.wait_ge(ones_set, 1)

                    def relus(g, s):
                        act.wait_ge(scaled, g + 1)
                        for j in range(G):
                            nc.scalar.activation(hd[:, s, j, :], xd[:, s, j, 0:D], ACT.Relu, bias=nb[:, s, G + j:G + j + 1],
                                                 scale=rs[:, s, G + j:G + j + 1])
                        for j in range(G):
                            last = nc.scalar.activation(hs[:, s, j, 0:D], xs[:, s, j, 0:D], ACT.Relu, bias=nb[:, s, j:j + 1],
                                                        scale=rs[:, s, j:j + 1])
                        last.then_inc(h_ready, 1)
                        act.wait_ge(hdT_ps, g + 1)
                        nc.scalar.activation(hdT[:, s, :], tp[:, :], ACT.Copy).then_inc(hdT_in, 1)

                    def exps(g, s):
                        act.wait_ge(score_ready, g + 2)
                        nc.scalar.activation(e[:, s, :], score[:, s, :], ACT.Exp).then_inc(e_ready, 1)

                    def copies(g, s):
                        for j in range(G):
                            act.wait_ge(sum_ps, g * G + j + 1)
                            nc.scalar.activation(sums[:, s, j, 0:D + 1], sp_[j % 2][:, 0:D + 1], ACT.Copy).then_inc(sum_in, 1)
                    pipeline(act, NGE, [(relus, 0), (exps, 1), (copies, 1)], S)

                @block.tensor
                def _(pe):
                    pe.wait_ge(ones_set, 1)

                    def products(g, s):
                        pe.wait_ge(h_ready, g + 1)
                        for j in range(G):
                            last = nc.tensor.transpose(tp[:, j * P:(j + 1) * P], hd[:, s, j, :], ident)
                        last.then_inc(hdT_ps, 1)
                        pe.wait_ge(cols_ready, g + 1)
                        for j in range(G):
                            last = nc.tensor.transpose(bcp[s % 2][:, j * P:(j + 1) * P],
                                                       col[:, s, j + 1:j + 2].to_broadcast([P, P]), ident)
                        last.then_inc(bc_ps, 1)
                        pe.wait_ge(score_ready, g + 1)
                        pe.wait_ge(hdT_in, g + 1)
                        for j in range(G):
                            r = rp[j // 2][:, (j % 2) * TW:(j % 2) * TW + D + 1]
                            nc.tensor.matmul(r, hdT[:, s, j * P:(j + 1) * P], Wscore[:, :], start=True, stop=False)
                            last = nc.tensor.matmul(r, ones[0:1, :], urow[:, 0:D + 1], start=False, stop=True)
                        last.then_inc(r_ps, 1)

                    def totals_(g, s):
                        pe.wait_ge(same_ready, g + 1)
                        for j in range(G):
                            before = sums[:, s, j - 1, 0:D + 1] if j else sums[:, (s - 1) % S, G - 1, 0:D + 1]
                            out = sp_[j % 2][:, 0:D + 1]
                            nc.tensor.matmul(out, same[:, s, j, :], hs[:, s, j, 0:D + 1], start=True, stop=False)
                            pe.wait_ge(sum_in, g * G + j + 1)
                            nc.tensor.matmul(out, carry[:, s, j, :], before, start=False, stop=True).then_inc(sum_ps, 1)
                    pipeline(pe, NGE, [(products, 0), (totals_, 1)], S)

                @block.sync
                def _(sp):
                    for s in range(S):
                        sp.sem_inc(stored[s], 32)

                    def store(g, s):
                        sp.wait_ge(summed, g + 1)
                        sp.dma_start(rows_of(xd_d, g, XW), xd[:, s, :, :]).then_inc(stored[s], 16)
                        sp.wait_ge(sum_in, g * G + G + 1)
                        sp.dma_start(rows_of(att_d, g, D + 1), sums[:, s, :, 0:D + 1]).then_inc(stored[s], 16)
                    pipeline(sp, NGE, [(store, 0)], S)
                    for s in range(S):
                        sp.wait_ge(stored[s], 32 * ((NGE - s + S - 1) // S) + 32)

        def update(edges):
            n = NGE if edges else NGN
            with phase() as c:
                x1 = sb("x1", [P, S, G, XW], F32, c)
                h = sb("h", [P, S, G, D], F32, c)
                x2 = sb("x2", [P, S, G, D], F32, c)
                st = sb("st", [P, 4, G, 6], F32, c)
                tmp = sb("tmp", [P, 4, 3, G], F32, c)
                neg, var, rs, nb = (sb(k, [P, 4, S, G], F32, c) for k in ("neg", "var", "rs", "nb"))
                norms = 2 if edges else 4
                summed, scaled, link, pool_link = ([sem(f"up_{k}{i}") for i in range(norms)] for k in (
                    "summed", "scaled", "link", "pool_link"))
                x_ready, h_ready, hb_link, z_ready, x2_link, x2_ready = (sem(f"up_{k}") for k in (
                    "x_ready", "h_ready", "hb_link", "z_ready", "x2_link", "x2_ready"))
                rows_in = [sem(f"up_rows_in{s}") for s in range(S)]
                stored = [sem(f"up_stored{s}") for s in range(S)]
                if edges:
                    att = sb("att", [P, S, G, TW], F32, c)
                    attT = sb("attT", [P, S, G * P], F32, c)
                    rden = sb("rden", [P, S, G], F32, c)
                    attT_ps, attT_in, o_ps, rden_ready, o_used = (sem(f"up_{k}") for k in (
                        "attT_ps", "attT_in", "o_ps", "rden_ready", "o_used"))
                else:
                    h2 = sb("h2", [P, S, G, D], F32, c)
                    r = sb("r", [P, S, G, RW], F32, c)
                    u = sb("u", [P, S, G, D + 2], F32, c)
                    h2_ready, x3_ready, h3_ready, u_ready, gram_done, gram_zero = (sem(f"up_{k}") for k in (
                        "h2_ready", "x3_ready", "h3_ready", "u_ready", "gram_done", "gram_zero"))
                n_in, n_out = (2 if edges else 1), (1 if edges else 2)

                with nc.Block() as block:
                    @block.sync
                    def _(sp):
                        for s in range(S):
                            sp.sem_inc(stored[s], 16 * n_out)

                        def load(g, s):
                            sp.wait_ge(stored[s], slot_count(g, s, n_out))
                            if edges:
                                sp.dma_start(x1[:, s, :, :], rows_of(xd_d, g, XW)).then_inc(rows_in[s], 16)
                                sp.dma_start(att[:, s, :, 0:D + 1], rows_of(att_d, g, D + 1)).then_inc(rows_in[s], 16)
                            else:
                                sp.dma_start(x1[:, s, :, :], node_rows_of(x1_d, g, XW)).then_inc(rows_in[s], 16)

                        def store(g, s):
                            sp.wait_ge(x2_ready, g + 1)
                            if edges:
                                sp.dma_start(rows_of(x2_d, g, D, NN), x2[:, s, :, :]).then_inc(stored[s], 16)
                            else:
                                sp.dma_start(node_rows_of(x2_d, g, D), x2[:, s, :, :]).then_inc(stored[s], 16)

                        def store_r(g, s):
                            sp.wait_ge(gram_done, g + 1)
                            sp.dma_start(node_rows_of(r_d, g, RW), r[:, s, :, :]).then_inc(stored[s], 16)
                        pipeline(sp, n, [(load, 0), (store, 2)] if edges else [(load, 0), (store, 2), (store_r, 3)], S)
                        for s in range(S):
                            sp.wait_ge(stored[s], 16 * n_out * ((n - s + S - 1) // S) + 16 * n_out)

                    @block.gpsimd
                    def _(pool):
                        def scale(i):
                            def part(g, s):
                                layer_scale(pool, neg[:, i, s, :], var[:, i, s, :], rs[:, i, s, :], nb[:, i, s, :], G,
                                            summed[i], pool_link[i], scaled[i], g)
                            return part
                        pipeline(pool, n, [(scale(i), i) for i in reversed(range(norms))], S)

                    @block.vector
                    def _(dve):
                        if edges:
                            dve.sem_inc(o_used, 2)
                        else:
                            nc.vector.memset(bank[0][:, :], 0.0)
                            nc.vector.memset(bank[1][:, :], 0.0).then_inc(gram_zero, 1)
                            nc.vector.memset(r[:, :, :, 2 * D:2 * D + 1], 1.0)
                            nc.vector.memset(r[:, :, :, 2 * D + 2:RW], 0.0)

                        def sums_of(i, tiles, g, s):
                            layer_sums(dve, tiles, st[:, i, :, :], tmp[:, i, :, :], neg[:, i, s, :], var[:, i, s, :],
                                       link[i], summed[i], g)

                        def first(g, s):
                            dve.wait_ge(rows_in[s], slot_count(g, s, n_in))
                            if edges:
                                nc.vector.reciprocal(rden[:, s, :], att[:, s, :, D]).then_inc(rden_ready, 1)
                            else:
                                for j in range(G):
                                    last = nc.vector.scalar_tensor_tensor(
                                        out=x1[:, s, j, 0:D], in0=he_last[1][:, :],
                                        scalar=x1[:, s, j, D + M_CHIGH:D + M_CHIGH + 1], in1=x1[:, s, j, 0:D],
                                        op0=ALU.mult, op1=ALU.add)
                                last.then_inc(x_ready, 1)
                                dve.wait_ge(x_ready, g + 1)
                            sums_of(0, [x1[:, s, j, 0:D] for j in range(G)], g, s)

                        def second(g, s):
                            dve.wait_ge(h_ready, g + 1)
                            row = R["bvo"] if edges else R["bo"]
                            if edges:
                                dve.wait_ge(o_ps, g + 1)
                                dve.wait_ge(rden_ready, g + 1)
                                for j in range(G):
                                    last = nc.vector.scalar_tensor_tensor(
                                        out=h[:, s, j, :], in0=bank[2 + s % 2][:, j * P:(j + 1) * P], scalar=rden[:, s, j:j + 1],
                                        in1=h[:, s, j, :], op0=ALU.mult, op1=ALU.add)
                                last.then_inc(o_used, 1)
                                dve.wait_ge(o_used, g + 3)
                            nc.vector.tensor_tensor(h[:, s, :, :], h[:, s, :, :],
                                                    row[:, :].unsqueeze(1).to_broadcast([P, G, D]), ALU.add).then_inc(hb_link, 1)
                            dve.wait_ge(hb_link, g + 1)
                            sums_of(1, [h[:, s, j, :] for j in range(G)], g, s)

                        def third(g, s):
                            dve.wait_ge(z_ready, g + 1)
                            nc.vector.tensor_tensor(x2[:, s, :, :], h[:, s, :, :],
                                                    R["gamma"][:, :].unsqueeze(1).to_broadcast([P, G, D]), ALU.mult)
                            nc.vector.tensor_tensor(x1[:, s, :, 0:D], x1[:, s, :, 0:D],
                                                    R["beta"][:, :].unsqueeze(1).to_broadcast([P, G, D]), ALU.add).then_inc(x2_link, 1)
                            dve.wait_ge(x2_link, g + 1)
                            nc.vector.tensor_tensor(x2[:, s, :, :], x2[:, s, :, :], x1[:, s, :, 0:D], ALU.add).then_inc(x2_ready, 1)
                            if not edges:
                                dve.wait_ge(x2_ready, g + 1)
                                sums_of(2, [x2[:, s, j, :] for j in range(G)], g, s)

                        def fourth(g, s):
                            dve.wait_ge(h2_ready, g + 1)
                            nc.vector.tensor_tensor(r[:, s, :, 0:D], x2[:, s, :, :], h2[:, s, :, :], ALU.add)
                            nc.vector.tensor_copy(r[:, s, :, 2 * D + 1], x1[:, s, :, D + M_GINV])
                            nc.vector.tensor_copy(u[:, s, :, D], x1[:, s, :, D + M_Q])
                            nc.vector.tensor_copy(u[:, s, :, D + 1], x1[:, s, :, D + M_BARE]).then_inc(x3_ready, 1)
                            dve.wait_ge(x3_ready, g + 1)
                            sums_of(3, [r[:, s, j, 0:D] for j in range(G)], g, s)
                        pipeline(dve, n, [(third, 2), (second, 1), (first, 0)] if edges else
                                 [(fourth, 3), (third, 2), (second, 1), (first, 0)], S)
                        if not edges:
                            dve.wait_ge(gram_done, n)
                            nc.vector.tensor_copy(gram1[:, :], bank[0][:, 0:D + 2])
                            nc.vector.tensor_copy(gram2[:, :], bank[1][0:2, 0:D + 2])

                    @block.scalar
                    def _(act):
                        act.preload_act_table(ACT.Relu)

                        def normed(i, out, x, func, ready):
                            def part(g, s):
                                act.wait_ge(scaled[i], g + 1)
                                for j in range(G):
                                    last = nc.scalar.activation(out(s, j), x(s, j), func, bias=nb[:, i, s, j:j + 1],
                                                                scale=rs[:, i, s, j:j + 1])
                                last.then_inc(ready, 1)
                            return part

                        def transposed(g, s):
                            act.wait_ge(attT_ps, g + 1)
                            nc.scalar.activation(attT[:, s, :], bank[s % 2][:, :], ACT.Copy).then_inc(attT_in, 1)

                        def weighted(g, s):
                            act.wait_ge(h3_ready, g + 1)
                            for j in range(G):
                                last = nc.scalar.activation(u[:, s, j, 0:D], r[:, s, j, D:2 * D], ACT.Copy,
                                                            scale=x1[:, s, j, D + M_Q:D + M_Q + 1])
                            last.then_inc(u_ready, 1)

                        h1 = normed(0, lambda s, j: h[:, s, j, :], lambda s, j: x1[:, s, j, 0:D], ACT.Relu, h_ready)
                        z = normed(1, lambda s, j: h[:, s, j, :], lambda s, j: h[:, s, j, :], ACT.Identity, z_ready)
                        if edges:
                            pipeline(act, n, [(z, 1), (transposed, 0), (h1, 0)], S)
                        else:
                            second_h = normed(2, lambda s, j: h2[:, s, j, :], lambda s, j: x2[:, s, j, :], ACT.Relu, h2_ready)
                            third_h = normed(3, lambda s, j: r[:, s, j, D:2 * D], lambda s, j: r[:, s, j, 0:D], ACT.Relu, h3_ready)
                            pipeline(act, n, [(third_h, 3), (weighted, 3), (second_h, 2), (z, 1), (h1, 0)], S)

                    @block.tensor
                    def _(pe):
                        def outputs(g, s):
                            pe.wait_ge(rows_in[s], slot_count(g, s, n_in))
                            for j in range(G):
                                last = nc.tensor.transpose(bank[s % 2][:, j * P:(j + 1) * P], att[:, s, j, 0:D], ident)
                            last.then_inc(attT_ps, 1)
                            pe.wait_ge(attT_in, g + 1)
                            pe.wait_ge(o_used, g + 1)
                            for j in range(G):
                                last = nc.tensor.matmul(bank[2 + s % 2][:, j * P:(j + 1) * P], attT[:, s, j * P:(j + 1) * P],
                                                        W["Wvo"][:, :], start=True, stop=True)
                            last.then_inc(o_ps, 1)

                        def moments(g, s):
                            pe.wait_ge(u_ready, g + 1)
                            for j in range(G):
                                nc.tensor.matmul(bank[0][:, 0:D + 2], u[:, s, j, 0:D], u[:, s, j, :], start=False,
                                                 stop=False, skip_group_check=True)
                                last = nc.tensor.matmul(bank[1][0:2, 0:D + 2], u[:, s, j, D:D + 2], u[:, s, j, :],
                                                        start=False, stop=False, skip_group_check=True)
                            last.then_inc(gram_done, 1)
                        if not edges:
                            pe.wait_ge(gram_zero, 1)
                        pipeline(pe, n, [(outputs, 0)] if edges else [(moments, 0)], S)

        update(False)
        update(True)
        with phase() as c:
            ix = sb("ix", [P, S, 2 * G], I32, c)
            col = sb("col", [P, S, G + 1], F32, c)
            xs, xd = (sb(n, [P, S, G, D], F32, c) for n in ("xs", "xd"))
            ef = sb("ef", [P, S, G, 64], F32, c)
            st = sb("st", [P, 2 * G, 6], F32, c)
            tmp = sb("tmp", [P, 3, 2 * G], F32, c)
            neg, var, rs, nb = (sb(n, [P, S, 2 * G], F32, c) for n in ("neg", "var", "rs", "nb"))
            st3 = sb("st3", [P, G, 6], F32, c)
            tmp3 = sb("tmp3", [P, 3, G], F32, c)
            neg3, var3, rs3, nb3 = (sb(n, [P, S, G], F32, c) for n in ("neg3", "var3", "rs3", "nb3"))
            hs, hd = (sb(n, [P, S, G, D], F32, c) for n in ("hs", "hd"))
            hsT, hdT = (sb(n, [P, 2, G * P], F32, c) for n in ("hsT", "hdT"))
            efT = sb("efT", [64, 2, G * P], F32, c)
            hid = sb("hid", [32, 2, G * P], F32, c)
            msg = sb("msg", [P, 2, G * P], F32, c)
            nhid = sb("nhid", [65, 2, G * P], F32, c)
            nmsg = sb("nmsg", [P, 2, G, D], F32, c)
            same, carry = (sb(n, [P, 2, G, P], F32, c) for n in ("same", "carry"))
            sums = sb("sums", [P, S, G, D], F32, c)
            r = sb("r", [P, S, G, RW], F32, c)
            cols_ready, pool_link, pool_link3, summed, scaled, link, summed3, scaled3, link3, h_ready, hT_ps, hsT_in, hdT_in, \
                hid_ps, hid_in, msg_ps, msg_in, nhid_ps, nhid_in, nmsg_ps, nmsg_in, bc_ps, same_ready, sum_ps, sum_in, \
                set_up, r_link, x3_ready, h3_ready, efT_in = (sem(f"mlp_{n}") for n in (
                    "cols_ready", "pool_link", "pool_link3", "summed", "scaled", "link", "summed3", "scaled3", "link3",
                    "h_ready", "hT_ps", "hsT_in", "hdT_in", "hid_ps", "hid_in", "msg_ps", "msg_in", "nhid_ps", "nhid_in",
                    "nmsg_ps", "nmsg_in", "bc_ps", "same_ready", "sum_ps", "sum_in", "set_up", "r_link", "x3_ready",
                    "h3_ready", "efT_in"))
            rows_in = [sem(f"mlp_rows_in{s}") for s in range(S)]
            ef_loaded = [sem(f"mlp_ef_in{s}") for s in range(S)]
            stored = [sem(f"mlp_stored{s}") for s in range(S)]
            hs_p, hd_p, ef_p, hid_p, msg_p, nmsg_p = bank[0], bank[1], bank[2], bank[3], bank[4], bank[5]
            sum_p = [bank[6], bank[7]]

            with nc.Block() as block:
                @block.gpsimd
                def _(pool):
                    def rows(g, s):
                        hold("pool", pool, stored[s], slot_count(g, s, 1))
                        nc.gpsimd.tensor_copy(ix[:, s, 0:G], table_src[:, bass.ds(g * G, G)])
                        nc.gpsimd.tensor_copy(ix[:, s, G:2 * G], table_dst[:, bass.ds(g * G, G)])
                        nc.gpsimd.tensor_copy(col[:, s, :], dstF[:, bass.ds(g * G, G + 1)]).then_inc(cols_ready, 1)
                        hold("pool", pool, cols_ready, g + 1)
                        for j in range(G):
                            gather(pool, xs[:, s, j, :], x2_d, ix[:, s, j:j + 1], rows_in[s])
                            gather(pool, xd[:, s, j, :], x2_d, ix[:, s, G + j:G + j + 1], rows_in[s])

                    def scale(g, s):
                        layer_scale(pool, neg[:, s, :], var[:, s, :], rs[:, s, :], nb[:, s, :], 2 * G, summed, pool_link,
                                    scaled, g)

                    def scale3(g, s):
                        layer_scale(pool, neg3[:, s, :], var3[:, s, :], rs3[:, s, :], nb3[:, s, :], G, summed3, pool_link3,
                                    scaled3, g)
                    pipeline(pool, NGE, [(rows, 0), (scale, 1), (scale3, 3)], S)

                @block.sync
                def _(sp):
                    for s in range(S):
                        sp.sem_inc(stored[s], 16)

                    def load(g, s):
                        sp.wait_ge(stored[s], slot_count(g, s, 1))
                        sp.dma_start(ef[:, s, :, :], rows_of(t["edge_attr_64"], g, 64)).then_inc(ef_loaded[s], 16)

                    def store(g, s):
                        sp.wait_ge(h3_ready, g + 1)
                        sp.dma_start(rows_of(r_d, g, RW, NN), r[:, s, :, :]).then_inc(stored[s], 16)
                    pipeline(sp, NGE, [(load, 0), (store, 3)], S)
                    for s in range(S):
                        sp.wait_ge(stored[s], 16 * ((NGE - s + S - 1) // S) + 16)

                @block.vector
                def _(dve):
                    nc.vector.memset(nhid[64:65, :, :], 1.0)
                    nc.vector.memset(r[:, :, :, 2 * D:2 * D + 1], 1.0)
                    nc.vector.memset(r[:, :, :, 2 * D + 2:RW], 0.0)
                    nc.vector.memset(sums[:, S - 1, G - 1, :], 0.0).then_inc(sum_in, 1)
                    dve.sem_inc(set_up, 1)
                    dve.sem_inc(same_ready, 1)

                    def stats(g, s):
                        dve.wait_ge(rows_in[s], slot_count(g, s, 2 * G))
                        layer_sums(dve, [x[:, s, j, :] for x in (xs, xd) for j in range(G)], st, tmp, neg[:, s, :],
                                   var[:, s, :], link, summed, g)

                    def to_sbuf(g, s):
                        dve.wait_ge(hT_ps, g + 1)
                        nc.vector.tensor_copy(hdT[:, s % 2, :], hd_p[:, :]).then_inc(hdT_in, 1)
                        nc.vector.tensor_copy(efT[:, s % 2, :], ef_p[0:64, :]).then_inc(efT_in, 1)

                    def sames(g, s):
                        dve.wait_ge(bc_ps, g + 1)
                        for j in range(G):
                            bc = ef_p[:, j * P:(j + 1) * P]
                            nc.vector.tensor_scalar(same[:, s % 2, j, :], bc, col[:, s, j + 1:j + 2], None, ALU.is_equal)
                            last = nc.vector.tensor_scalar(carry[:, s % 2, j, :], bc, col[:, s, j:j + 1], last_row,
                                                           ALU.is_equal, ALU.mult)
                        last.then_inc(same_ready, 1)

                    def x3(g, s):
                        dve.wait_ge(h_ready, g + 1)
                        nc.vector.tensor_tensor(r[:, s, :, 0:D], xd[:, s, :, :], hd[:, s, :, :], ALU.add)
                        nc.vector.tensor_copy(r[:, s, :, 2 * D + 1], ginv_dst[:, bass.ds(g * G, G)]).then_inc(r_link, 1)
                        dve.wait_ge(r_link, g + 1)
                        dve.wait_ge(sum_in, g * G + G + 1)
                        nc.vector.tensor_tensor(r[:, s, :, 0:D], r[:, s, :, 0:D], sums[:, s, :, :], ALU.add).then_inc(x3_ready, 1)
                        dve.wait_ge(x3_ready, g + 1)
                        layer_sums(dve, [r[:, s, j, 0:D] for j in range(G)], st3, tmp3, neg3[:, s, :], var3[:, s, :],
                                   link3, summed3, g)
                    pipeline(dve, NGE, [(x3, 3), (to_sbuf, 1), (sames, 1), (stats, 0)], S)

                @block.scalar
                def _(act):
                    act.preload_act_table(ACT.Relu)
                    act.wait_ge(set_up, 1)

                    def relus(g, s):
                        act.wait_ge(scaled, g + 1)
                        for k, (x, h) in enumerate(((xs, hs), (xd, hd))):
                            for j in range(G):
                                last = nc.scalar.activation(h[:, s, j, :], x[:, s, j, :], ACT.Relu,
                                                            bias=nb[:, s, k * G + j:k * G + j + 1],
                                                            scale=rs[:, s, k * G + j:k * G + j + 1])
                        last.then_inc(h_ready, 1)

                    def hsT_copy(g, s):
                        act.wait_ge(hT_ps, g + 1)
                        nc.scalar.activation(hsT[:, s % 2, :], hs_p[:, :], ACT.Copy).then_inc(hsT_in, 1)

                    def biased(out, ps, bias, ready_in, ready_out):
                        def part(g, s):
                            act.wait_ge(ready_in, g + 1)
                            if bias is None:
                                nc.scalar.activation(out(s % 2), ps, ACT.Relu).then_inc(ready_out, 1)
                            else:
                                nc.scalar.activation(out(s % 2), ps, ACT.Relu, bias=bias).then_inc(ready_out, 1)
                        return part

                    hidden = biased(lambda s: hid[:, s, :], hid_p[0:32, :], C["be1"][0:32, :], hid_ps, hid_in)
                    message = biased(lambda s: msg[:, s, :], msg_p[:, :], C["be2"][:, :], msg_ps, msg_in)
                    nhidden = biased(lambda s: nhid[0:64, s, :], hid_p[0:64, :], C["bn1"][0:64, :], nhid_ps, nhid_in)
                    nmessage = biased(lambda s: nmsg[:, s, :, :].rearrange("p j f -> p (j f)"), nmsg_p[:, :], None, nmsg_ps, nmsg_in)

                    def copies(g, s):
                        for j in range(G):
                            act.wait_ge(sum_ps, g * G + j + 1)
                            nc.scalar.activation(sums[:, s, j, :], sum_p[j % 2][:, 0:D], ACT.Copy).then_inc(sum_in, 1)

                    def h3(g, s):
                        act.wait_ge(scaled3, g + 1)
                        for j in range(G):
                            last = nc.scalar.activation(r[:, s, j, D:2 * D], r[:, s, j, 0:D], ACT.Relu,
                                                        bias=nb3[:, s, j:j + 1], scale=rs3[:, s, j:j + 1])
                        last.then_inc(h3_ready, 1)
                    pipeline(act, NGE, [(h3, 3), (hidden, 1), (relus, 0), (message, 1), (hsT_copy, 0), (copies, 2),
                                        (nhidden, 1), (nmessage, 1)], S)

                @block.tensor
                def _(pe):
                    pe.wait_ge(sum_in, 1)
                    pe.wait_ge(set_up, 1)

                    def transposes(g, s):
                        pe.wait_ge(h_ready, g + 1)
                        pe.wait_ge(same_ready, g + 1)
                        hold("pe", pe, ef_loaded[s], slot_count(g, s, 1))
                        for j in range(G):
                            nc.tensor.transpose(ef_p[0:64, j * P:(j + 1) * P], ef[:, s, j, :], ident)
                        for x, p in ((hs, hs_p), (hd, hd_p)):
                            for j in range(G):
                                last = nc.tensor.transpose(p[:, j * P:(j + 1) * P], x[:, s, j, :], ident)
                        last.then_inc(hT_ps, 1)

                    def hidden(g, s):
                        pe.wait_ge(efT_in, g + 1)
                        pe.wait_ge(cols_ready, g + 1)
                        for j in range(G):
                            last = nc.tensor.transpose(ef_p[:, j * P:(j + 1) * P], col[:, s, j + 1:j + 2].to_broadcast([P, P]), ident)
                        last.then_inc(bc_ps, 1)
                        pe.wait_ge(hsT_in, g + 1)
                        nc.tensor.matmul(hid_p[0:32, :], W["We1a"][:, 0:32], hsT[:, s % 2, :], start=True, stop=False)
                        pe.wait_ge(hdT_in, g + 1)
                        nc.tensor.matmul(hid_p[0:32, :], W["We1b"][:, 0:32], hdT[:, s % 2, :], start=False, stop=False)
                        nc.tensor.matmul(hid_p[0:32, :], W["We1c"][0:64, 0:32], efT[:, s % 2, :], start=False,
                                         stop=True).then_inc(hid_ps, 1)

                    def message(g, s):
                        pe.wait_ge(hid_in, g + 1)
                        nc.tensor.matmul(msg_p[:, :], W["We2"][0:32, :], hid[:, s % 2, :], start=True, stop=True).then_inc(msg_ps, 1)

                    def nhidden(g, s):
                        nc.tensor.matmul(hid_p[0:64, :], W["Wn1a"][:, 0:64], hdT[:, s % 2, :], start=True, stop=False)
                        pe.wait_ge(msg_in, g + 1)
                        nc.tensor.matmul(hid_p[0:64, :], W["Wn1b"][:, 0:64], msg[:, s % 2, :], start=False,
                                         stop=True).then_inc(nhid_ps, 1)

                    def nmessage(g, s):
                        pe.wait_ge(nhid_in, g + 1)
                        for j in range(G):
                            last = nc.tensor.matmul(nmsg_p[:, j * P:(j + 1) * P], nhid[:, s % 2, j * P:(j + 1) * P],
                                                    W["Wn2"][0:65, :], start=True, stop=True)
                        last.then_inc(nmsg_ps, 1)

                    def totals_(g, s):
                        pe.wait_ge(same_ready, g + 2)
                        pe.wait_ge(nmsg_in, g + 1)
                        for j in range(G):
                            before = sums[:, s, j - 1, :] if j else sums[:, (s - 1) % S, G - 1, :]
                            out = sum_p[j % 2][:, 0:D]
                            nc.tensor.matmul(out, same[:, s % 2, j, :], nmsg[:, s % 2, j, :], start=True, stop=False)
                            pe.wait_ge(sum_in, g * G + j + 1)
                            nc.tensor.matmul(out, carry[:, s % 2, j, :], before, start=False, stop=True).then_inc(sum_ps, 1)
                    pipeline(pe, NGE, [(hidden, 1), (message, 1), (transposes, 0), (totals_, 2), (nhidden, 1), (nmessage, 1)], S)

        with phase() as c:
            ix = sb("ix", [P, S, 2 * G], I32, c)
            col = sb("col", [P, S, G + 1], F32, c)
            cw = sb("cw", [P, S, G, 2], F32, c)
            rs_, rd = (sb(n, [P, S, G, RW], F32, c) for n in ("rs_", "rd"))
            wt, rg, q = (sb(n, [P, S, G], F32, c) for n in ("wt", "rg", "q"))
            same, carry = (sb(n, [P, S, G, P], F32, c) for n in ("same", "carry"))
            sums = sb("sums", [P, S, G, TW], F32, c)
            u = sb("u", [P, S, G, D + 2], F32, c)
            cols_ready, wt_ready, rg_link, bc_ps, same_ready, sum_ps, sum_in, w_ready, u_ready, gram_done, gram_zero, ones_set, \
                q_link = (sem(f"gc_{n}") for n in (
                    "cols_ready", "wt_ready", "rg_link", "bc_ps", "same_ready", "sum_ps", "sum_in", "w_ready", "u_ready",
                    "gram_done", "gram_zero", "ones_set", "q_link"))
            src_in, dst_in, scattered = ([sem(f"gc_{n}{s}") for s in range(S)] for n in ("src_in", "dst_in", "scattered"))
            bcp, sum_p = [bank[2], bank[3]], [bank[4], bank[5]]

            with nc.Block() as block:
                @block.gpsimd
                def _(pool):
                    def written(g, s):
                        hold("pool", pool, scattered[s], slot_count(g, s, G))
                        hold("pool", pool, u_ready, g + 1)

                    def rows(g, s):
                        nc.gpsimd.tensor_copy(ix[:, s, 0:G], table_src[:, bass.ds(g * G, G)])
                        nc.gpsimd.tensor_copy(ix[:, s, G:2 * G], out_row[:, bass.ds(g * G, G)])
                        nc.gpsimd.tensor_copy(cw[:, s, :, 0], ew[:, bass.ds(g * G, G)])
                        nc.gpsimd.tensor_copy(cw[:, s, :, 1], seg_end[:, bass.ds(g * G, G)])
                        nc.gpsimd.tensor_copy(col[:, s, :], dstF[:, bass.ds(g * G, G + 1)]).then_inc(cols_ready, 1)
                        hold("pool", pool, cols_ready, g + 1)
                        for j in range(G):
                            gather(pool, rs_[:, s, j, :], r_d, ix[:, s, j:j + 1], src_in[s])

                    def scatter(g, s):
                        hold("pool", pool, w_ready, g + 1)
                        for j in range(G):
                            pool.indirect_dma_start(out=r_d, out_offset=bass.IndirectOffsetOnAxis(ap=ix[:, s, G + j:G + j + 1], axis=0),
                                                    in_=rd[:, s, j, :], in_offset=None).then_inc(scattered[s], 16)
                    pipeline(pool, NGE, [(written, S), (rows, 0), (scatter, 2)], S)

                @block.sync
                def _(sp):
                    def load(g, s):
                        sp.wait_ge(cols_ready, g + 1)
                        sp.dma_start(rd[:, s, :, :], rows_of(r_d, g, RW, NN)).then_inc(dst_in[s], 16)
                    pipeline(sp, NGE, [(load, 0)], S)

                @block.vector
                def _(dve):
                    nc.vector.memset(bank[0][:, :], 0.0)
                    nc.vector.memset(bank[1][:, :], 0.0).then_inc(gram_zero, 1)
                    nc.vector.memset(sums[:, S - 1, G - 1, :], 0.0).then_inc(sum_in, 1)

                    def sames(g, s):
                        dve.wait_ge(cols_ready, g + 1)
                        dve.wait_ge(src_in[s], slot_count(g, s, G))
                        nc.vector.tensor_tensor(wt[:, s, :], rs_[:, s, :, 2 * D + 1], cw[:, s, :, 0], ALU.mult).then_inc(wt_ready, 1)
                        dve.wait_ge(dst_in[s], slot_count(g, s, 1))
                        nc.vector.reciprocal(rg[:, s, :], rd[:, s, :, 2 * D + 1])
                        nc.vector.tensor_tensor(q[:, s, :], rd[:, s, :, 2 * D + 1], rd[:, s, :, 2 * D + 1], ALU.mult).then_inc(rg_link, 1)
                        dve.wait_ge(rg_link, g + 1)
                        nc.vector.tensor_tensor(q[:, s, :], q[:, s, :], cw[:, s, :, 1], ALU.mult).then_inc(q_link, 1)
                        dve.wait_ge(q_link, g + 1)
                        dve.wait_ge(bc_ps, g + 1)
                        for j in range(G):
                            bc = bcp[s % 2][:, j * P:(j + 1) * P]
                            nc.vector.tensor_scalar(same[:, s, j, :], bc, col[:, s, j + 1:j + 2], wt[:, s, j:j + 1],
                                                    ALU.is_equal, ALU.mult)
                            last = nc.vector.tensor_scalar(carry[:, s, j, :], bc, col[:, s, j:j + 1], last_row,
                                                           ALU.is_equal, ALU.mult)
                        last.then_inc(same_ready, 1)

                    def own(g, s):
                        nc.vector.tensor_copy(u[:, s, :, D + 1], cw[:, s, :, 1])
                        dve.wait_ge(sum_in, g * G + G + 1)
                        for j in range(G):
                            last = nc.vector.scalar_tensor_tensor(
                                out=rd[:, s, j, D:2 * D + 1], in0=sums[:, s, j, 0:D + 1], scalar=rg[:, s, j:j + 1],
                                in1=rd[:, s, j, D:2 * D + 1], op0=ALU.mult, op1=ALU.add)
                        last.then_inc(w_ready, 1)
                    pipeline(dve, NGE, [(sames, 0), (own, 1)], S)
                    dve.wait_ge(gram_done, NGE)
                    nc.vector.tensor_tensor(gram1[:, :], gram1[:, :], bank[0][:, 0:D + 2], ALU.add)
                    nc.vector.tensor_tensor(gram2[:, :], gram2[:, :], bank[1][0:2, 0:D + 2], ALU.add)

                @block.scalar
                def _(act):
                    act.preload_act_table(ACT.Copy)
                    
                    def copies(g, s):
                        for j in range(G):
                            act.wait_ge(sum_ps, g * G + j + 1)
                            nc.scalar.activation(sums[:, s, j, 0:D + 1], sum_p[j % 2][:, 0:D + 1], ACT.Copy).then_inc(sum_in, 1)

                    def weighted(g, s):
                        act.wait_ge(w_ready, g + 1)
                        for j in range(G):
                            last = nc.scalar.activation(u[:, s, j, 0:D + 1], rd[:, s, j, D:2 * D + 1], ACT.Copy,
                                                        scale=q[:, s, j:j + 1])
                        last.then_inc(u_ready, 1)
                    pipeline(act, NGE, [(copies, 0), (weighted, 1)], S)

                @block.tensor
                def _(pe):
                    pe.wait_ge(gram_zero, 1)

                    def broadcasts(g, s):
                        pe.wait_ge(cols_ready, g + 1)
                        for j in range(G):
                            last = nc.tensor.transpose(bcp[s % 2][:, j * P:(j + 1) * P],
                                                       col[:, s, j + 1:j + 2].to_broadcast([P, P]), ident)
                        last.then_inc(bc_ps, 1)

                    def totals_(g, s):
                        pe.wait_ge(same_ready, g + 1)
                        for j in range(G):
                            before = sums[:, s, j - 1, 0:D + 1] if j else sums[:, (s - 1) % S, G - 1, 0:D + 1]
                            out = sum_p[j % 2][:, 0:D + 1]
                            nc.tensor.matmul(out, same[:, s, j, :], rs_[:, s, j, D:2 * D + 1], start=True, stop=False)
                            pe.wait_ge(sum_in, g * G + j + 1)
                            nc.tensor.matmul(out, carry[:, s, j, :], before, start=False, stop=True).then_inc(sum_ps, 1)

                    def moments(g, s):
                        pe.wait_ge(u_ready, g + 1)
                        for j in range(G):
                            nc.tensor.matmul(bank[0][:, 0:D + 2], u[:, s, j, 0:D], u[:, s, j, :], start=False, stop=False,
                                             skip_group_check=True)
                            last = nc.tensor.matmul(bank[1][0:2, 0:D + 2], u[:, s, j, D:D + 2], u[:, s, j, :], start=False,
                                                    stop=False, skip_group_check=True)
                        last.then_inc(gram_done, 1)
                    pipeline(pe, NGE, [(broadcasts, 0), (totals_, 1), (moments, 2)], S)

        Wbn = sb("Wbn", [P, D])
        bbn = sb("bbn", [P, D])
        tbn = sb("tbn", [P, D])
        with phase() as c:
            y1, z1, var_, sc, half = (sb(n, [P, D], F32, c) for n in ("y1", "z1", "var_", "sc", "half"))
            y2, z2 = (sb(n, [2, D], F32, c) for n in ("y2", "z2"))
            mean = sb("mean", [P, D], F32, c)
            y_ps, z_ready, e_ps, link, var_ready, pow_done = (sem(f"bn_{n}") for n in ("y_ps", "z_ready", "e_ps", "link", "var_ready", "pow_done"))
            with nc.Block() as block:
                @block.tensor
                def _(pe):
                    nc.tensor.matmul(bank[0][:, 0:D], gram1[:, 0:D], W["W3"][:, :], start=True, stop=False)
                    nc.tensor.matmul(bank[0][:, 0:D], gram2[:, 0:D], wb[:, :], start=False, stop=True)
                    nc.tensor.matmul(bank[1][0:2, 0:D], gram1[:, D:D + 2], W["W3"][:, :], start=True, stop=False)
                    nc.tensor.matmul(bank[1][0:2, 0:D], gram2[:, D:D + 2], wb[:, :], start=False, stop=True).then_inc(y_ps, 1)
                    pe.wait_ge(z_ready, 1)
                    nc.tensor.matmul(bank[2][:, 0:D], ones, z1[:, :], start=True, stop=False)
                    nc.tensor.matmul(bank[2][:, 0:D], ones[0:2, :], z2[:, :], start=False, stop=True)
                    nc.tensor.matmul(bank[3][:, 0:D], K[0:2, K_ROW1:K_ROW1 + P], y2[:, :], start=True, stop=True).then_inc(e_ps, 1)

                @block.gpsimd
                def _(pool):
                    nc.gpsimd.memset(half[:, :], -0.5).then_inc(pow_done, 1)
                    pool.wait_ge(pow_done, 1)
                    pool.wait_ge(var_ready, 1)
                    nc.gpsimd.tensor_tensor(sc[:, :], var_[:, :], half[:, :], ALU.pow).then_inc(pow_done, 1)

                @block.vector
                def _(dve):
                    k = [0]

                    def chain(ins):
                        k[0] += 1
                        ins.then_inc(link, 1)
                        dve.wait_ge(link, k[0])

                    dve.wait_ge(y_ps, 1)
                    chain(nc.vector.tensor_tensor(z1[:, :], W["W3"][:, :], bank[0][:, 0:D], ALU.mult))
                    chain(nc.vector.tensor_copy(y2[:, :], bank[1][0:2, 0:D]))
                    nc.vector.tensor_tensor(z2[:, :], wb[:, :], y2[:, :], ALU.mult).then_inc(z_ready, 1)
                    dve.wait_ge(e_ps, 1)
                    chain(nc.vector.tensor_scalar(mean[:, :], bank[3][:, 0:D], 1.0 / N, None, ALU.mult))
                    chain(nc.vector.tensor_tensor(z1[:, :], mean[:, :], mean[:, :], ALU.mult))
                    chain(nc.vector.tensor_scalar(y1[:, :], bank[2][:, 0:D], 1.0 / N, EPS, ALU.mult, ALU.add))
                    chain(nc.vector.tensor_tensor(y1[:, :], y1[:, :], z1[:, :], ALU.subtract))
                    nc.vector.tensor_scalar(var_[:, :], y1[:, :], EPS, None, ALU.max).then_inc(var_ready, 1)
                    dve.wait_ge(pow_done, 2)
                    chain(nc.vector.tensor_tensor(sc[:, :], sc[:, :], R["bgamma"][:, :], ALU.mult))
                    chain(nc.vector.tensor_tensor(Wbn[:, :], W["W3"][:, :], sc[:, :], ALU.mult))
                    chain(nc.vector.tensor_tensor(bbn[:, :], R["b3"][:, :], sc[:, :], ALU.mult))
                    chain(nc.vector.tensor_tensor(z1[:, :], mean[:, :], sc[:, :], ALU.mult))
                    chain(nc.vector.tensor_tensor(tbn[:, :], R["bbeta"][:, :], z1[:, :], ALU.subtract))

        with phase() as c:
            r = sb("r", [P, S, G, RW], F32, c)
            wT = sb("wT", [P, S, G * P], F32, c)
            y = sb("y", [P, S, G, D], F32, c)
            g2 = sb("g2", [P, S, G], F32, c)
            wT_ps, wT_in, y_ps, y_used, link, link2, y_ready = (sem(f"out_{n}") for n in (
                "wT_ps", "wT_in", "y_ps", "y_used", "link", "link2", "y_ready"))
            rows_in = [sem(f"out_rows_in{s}") for s in range(S)]
            stored = [sem(f"out_stored{s}") for s in range(S)]

            with nc.Block() as block:
                @block.sync
                def _(sp):
                    for s in range(S):
                        sp.sem_inc(stored[s], 16)

                    def load(g, s):
                        sp.wait_ge(stored[s], slot_count(g, s, 1))
                        sp.dma_start(r[:, s, :, :], node_rows_of(r_d, g, RW)).then_inc(rows_in[s], 16)
                    pipeline(sp, NGN, [(load, 0)], S)

                @block.tensor
                def _(pe):
                    def transposes(g, s):
                        pe.wait_ge(rows_in[s], slot_count(g, s, 1))
                        for j in range(G):
                            last = nc.tensor.transpose(bank[s % 2][:, j * P:(j + 1) * P], r[:, s, j, D:2 * D], ident)
                        last.then_inc(wT_ps, 1)

                    def products(g, s):
                        pe.wait_ge(wT_in, g + 1)
                        pe.wait_ge(y_used, g + 1)
                        for j in range(G):
                            last = nc.tensor.matmul(bank[2 + s % 2][:, j * P:(j + 1) * P], wT[:, s, j * P:(j + 1) * P],
                                                    Wbn[:, :], start=True, stop=True)
                        last.then_inc(y_ps, 1)
                    pipeline(pe, NGN, [(transposes, 0), (products, 1)], S)

                @block.scalar
                def _(act):
                    act.preload_act_table(ACT.Copy)

                    def to_sbuf(g, s):
                        act.wait_ge(wT_ps, g + 1)
                        nc.scalar.activation(wT[:, s, :], bank[s % 2][:, :], ACT.Copy).then_inc(wT_in, 1)

                    def store(g, s):
                        act.wait_ge(y_ready, g + 1)
                        act.dma_start(node_rows_of(t["out"], g, D), y[:, s, :, :]).then_inc(stored[s], 16)
                    pipeline(act, NGN, [(to_sbuf, 0), (store, 2)], S)
                    for s in range(S):
                        act.wait_ge(stored[s], 16 * ((NGN - s + S - 1) // S) + 16)

                @block.vector
                def _(dve):
                    dve.sem_inc(y_used, 2)

                    def part(g, s):
                        dve.wait_ge(y_ps, g + 1)
                        for j in range(G):
                            last = nc.vector.scalar_tensor_tensor(
                                out=y[:, s, j, :], in0=bbn[:, :], scalar=r[:, s, j, 2 * D:2 * D + 1],
                                in1=bank[2 + s % 2][:, j * P:(j + 1) * P], op0=ALU.mult, op1=ALU.add)
                        last.then_inc(y_used, 1)
                        nc.vector.tensor_tensor(g2[:, s, :], r[:, s, :, 2 * D + 1], r[:, s, :, 2 * D + 1], ALU.mult).then_inc(link, 1)
                        dve.wait_ge(link, g + 1)
                        for j in range(G):
                            last = nc.vector.scalar_tensor_tensor(out=y[:, s, j, :], in0=y[:, s, j, :], scalar=g2[:, s, j:j + 1],
                                                                  in1=tbn[:, :], op0=ALU.mult, op1=ALU.add)
                        last.then_inc(link2, 1)
                        dve.wait_ge(link2, g + 1)
                        nc.vector.scalar_tensor_tensor(out=y[:, s, :, :], in0=y[:, s, :, :], scalar=0.0, in1=r[:, s, :, 0:D],
                                                       op0=ALU.max, op1=ALU.add).then_inc(y_ready, 1)
                    pipeline(dve, NGN, [(part, 0)], S)
    return


_FLOATS = ["x", "edge_attr_64", "L0_gnn_W1", "L0_gnn_b1", "L0_gnn_W2", "L0_gnn_b2", "L1_gnn_Wqk", "L1_gnn_bqk",
           "L1_gnn_Wv", "L1_gnn_bv", "L1_gnn_Wo", "L1_gnn_bo", "L1_gnn_gamma", "L1_gnn_beta", "L2_gnn_We1",
           "L2_gnn_be1", "L2_gnn_We2", "L2_gnn_be2", "L2_gnn_Wn1", "L2_gnn_bn1", "L2_gnn_Wn2", "L2_gnn_bn2",
           "L3_gnn_W", "L3_gnn_b", "L3_gnn_gamma", "L3_gnn_beta"]
DEBUG = False


def constants():
    import numpy as np

    k = np.zeros((P, K_COLS), np.float32)
    p = np.arange(P)
    k[:, K_ID:K_ID + P] = np.eye(P)
    k[:, K_AFTER:K_AFTER + P] = p[None, :] > p[:, None]
    k[:, K_IOTA:K_IOTA + NLO] = np.arange(NLO)
    for b in range(2):
        k[:HB, K_NODE + b * NLO:K_NODE + (b + 1) * NLO] = (b * HB + np.arange(HB))[:, None] * NLO + np.arange(NLO)
    k[:, K_EDGE:K_EDGE + NT] = np.arange(NT) * P + p[:, None]
    k[P - 1, K_LAST] = 1
    k[:, K_DUMP] = NN + p
    k[:, K_ONE:K_ONE + P] = 1
    k[1, K_ROW1:K_ROW1 + P] = 1
    return k


def kernel(**inputs):
    import numpy as np
    import concourse.bacc as bacc
    from concourse.bass_utils import run_bass_kernel_spmd

    def padded(v, rows, fill):
        v = np.asarray(v)
        out = np.full((rows,) + v.shape[1:], fill, v.dtype)
        out[:len(v)] = v
        return out

    arrays = {n: np.ascontiguousarray(np.asarray(inputs[n])) for n in _FLOATS}
    arrays["x"] = padded(arrays["x"], NN, 0)
    arrays["edge_attr_64"] = padded(arrays["edge_attr_64"], EP, 0)
    arrays["src"] = padded(inputs["src"], EP, N)
    arrays["dst"] = padded(inputs["dst"], EP, N)
    arrays["next_dst"] = padded(arrays["dst"][1:], EP, N + 1)
    arrays["edge_weight"] = padded(inputs["edge_weight"], EP, 0)
    arrays["consts"] = constants()
    nc = bacc.Bacc("TRN2", target_bir_lowering=False, num_devices=1)
    t = {n: nc.dram_tensor(n, a.shape, mybir.dt.from_np(a.dtype), kind="ExternalInput").ap() for n, a in arrays.items()}
    t["out"] = nc.dram_tensor("out", (NN, D), F32, kind="ExternalOutput").ap()
    build(nc, t, DEBUG)
    r = run_bass_kernel_spmd(nc, [arrays], core_ids=[0])
    return r.results[0]["out"][:N]
```

```python
from contextlib import ExitStack, contextmanager

import concourse.bass as bass
from concourse import mybir

F32 = mybir.dt.float32
BF16 = mybir.dt.bfloat16
I32 = mybir.dt.int32
ALU = mybir.AluOpType
ACT = mybir.ActivationFunctionType
AX_X = mybir.AxisListType.X

P = 128
D = 128
N = 50000
E = 25000
HEDGES = 10000
G = 4
NT = 200
EP = NT * P
NGE = NT // G
LOW_STEP = 2 * G * P
NHI, NLO = 196, 256
HB = NHI // 2
NN = NHI * NLO
NGN = NN // (P * G)
XW = 136
TW = 132
RW = 260
EPS = 1e-5
M_DINV, M_CHIGH, M_GINV, M_INDEX, M_BINV, M_GINV2, M_BARE, M_Q = range(8)
K_ID = 0
K_AFTER = K_ID + P
K_IOTA = K_AFTER + P
K_NODE = K_IOTA + NLO
K_EDGE = K_NODE + 2 * NLO
K_LAST = K_EDGE + NT
K_DUMP = K_LAST + 1
K_ONE = K_DUMP + 1
K_ROW1 = K_ONE + P
K_COLS = K_ROW1 + P


def pipeline(eng, n, parts, slots=2):
    parts = [(p + (0,))[:3] for p in parts]
    deep = max(lag for _, lag, _ in parts)
    looped = (n - deep) // slots * slots

    def step(k):
        for part, lag, more in parts:
            if 0 <= k - lag < n + more:
                part(k - lag, (k - lag) % slots)

    for k in range(deep):
        step(k)
    with eng.Fori(0, looped - slots + 1, slots) as i:
        for k in range(deep, deep + slots):
            for part, lag, _ in parts:
                part(i + (k - lag), (k - lag) % slots)
    for k in range(deep + looped, max(n + lag + more for _, lag, more in parts)):
        step(k)


def bounded(eng, count, part):
    with eng.Fori(0, count - 1, 2) as i:
        part(i, 0)
        part(i + 1, 1)


def build(nc, t, debug):
    root = ExitStack()
    with root:
        def dram(name, shape):
            return nc.dram_tensor(name, shape, F32, kind="ExternalOutput" if debug else "Internal").ap()

        meta_d = dram("meta_d", (NN, 8))
        sum1_d = dram("sum1_d", (NN + P, D))
        x1_d = dram("x1_d", (NN + P, XW))
        he_d = dram("he_d", (EP + P, D))
        x2_d = dram("x2_d", (NN + EP, D))
        r_d = dram("r_d", (NN + EP, RW))

        stage = [0]

        def sb(name, shape, dt=F32, ctx=root):
            return ctx.enter_context(nc.sbuf_tensor(f"{name}_{stage[0]}", shape, dt))

        def sem(name):
            return nc.alloc_semaphore(f"{name}_{stage[0]}")

        @contextmanager
        def phase():
            stage[0] += 1
            with nc.cleanup_on_exit(), ExitStack() as c:
                yield c

        K = sb("K", [P, K_COLS])
        ident = K[:, K_ID:K_ID + P]
        after = K[:, K_AFTER:K_AFTER + P]
        last_row = K[:, K_LAST:K_LAST + 1]
        dump_row = K[:, K_DUMP:K_DUMP + 1]
        edge_no = K[:, K_EDGE:K_EDGE + NT]
        ones = K[:, K_ONE:K_ONE + P]
        srcF = sb("srcF", [P, NT])
        dstF = sb("dstF", [P, NT + 1])
        ew = sb("ew", [P, NT])
        srcI = sb("srcI", [P, NT], I32)
        dstI = sb("dstI", [P, NT], I32)
        low = sb("low", [P, NT])
        seg_end = sb("seg_end", [P, NT])
        out_row = sb("out_row", [P, NT], I32)
        he_index = sb("he_index", [P, NT], I32)
        meta_src = sb("meta_src", [P, NT, 8])
        meta_dst = sb("meta_dst", [P, NT, 8])
        table_src = sb("table_src", [P, NT], I32)
        table_dst = sb("table_dst", [P, NT], I32)
        ginv_dst = sb("ginv_dst", [P, NT])
        he_last = [sb("he_last0", [P, D]), sb("he_last1", [P, D])]
        low_groups = sb("low_groups", [P, 1], I32)
        minus_half = sb("minus_half", [P, 16])
        W = {n: sb("w_" + n, [P, D]) for n in
             ("W1", "W2", "Wvo", "We1a", "We1b", "We1c", "We2", "Wn1a", "Wn1b", "Wn2", "W3")}
        Wscore = sb("Wscore", [P, D + 1])
        urow = sb("urow", [1, 2 * TW])
        R = {n: sb("r_" + n, [P, D]) for n in ("b1", "b2", "bo", "bvo", "gamma", "beta", "bgamma", "bbeta", "b3")}
        C = {n: sb("c_" + n, [P, 1]) for n in ("be1", "be2", "bn1", "bqk", "bv")}
        wb = sb("wb", [2, D])
        gram1 = sb("gram1", [P, D + 2])
        gram2 = sb("gram2", [2, D + 2])
        bank = [root.enter_context(nc.psum_tensor(f"bank{i}", [P, 512], F32)) for i in range(8)]
        passed = {n: sem("passed_" + n) for n in ("pool", "dve", "act", "pe", "sp")}

        def hold(name, eng, s, value):
            eng.wait_ge(s, value)
            eng.sem_inc(passed[name], 1)

        def rows_of(table, g, width, first=0):
            return table[bass.ds(g * (G * P) + first, G * P), 0:width].rearrange("(j p) f -> p j f", p=P)

        def node_rows_of(table, g, width):
            return table[bass.ds(g * (G * P), G * P), 0:width].rearrange("(p j) f -> p j f", p=P)

        with phase() as c:
            rows = sb("rows", [NT // 2, 3, 2, P], I32, c)
            rowsF = sb("rowsF", [NT // 2, 4, 2, P], F32, c)
            zeros = sb("zeros", [P, 28 * D], F32, c)
            wq, wv, wo, wqT, wvT = (sb(f"ld_{n}", [P, D], F32, c) for n in ("q", "v", "o", "qT", "vT"))
            tmpF, nextF, high = (sb(n, [P, NT], F32, c) for n in ("tmpF", "nextF", "high"))
            tmpI = sb("tmpI", [P, NT], I32, c)
            split = {n: sb("sp_" + n, [P, NT], F32, c) for n in ("hs", "ls", "hd", "ld")}
            cnt = sb("cnt", [P, 1], F32, c)
            iota = sb("iota_b", [P, NLO], BF16, c)
            hot_s = sb("hot_s", [P, 2, NHI + 2 * NLO], BF16, c)
            hot_d = sb("hot_d", [P, 2, NHI + NLO], BF16, c)
            deg = {n: sb("deg_" + n, [HB, 2 * NLO], F32, c) for n in ("s", "h", "d")}
            a = {n: sb("a_" + n, [HB, 2 * NLO], F32, c) for n in ("x", "y", "z", "w", "half")}
            totals = sb("totals", [HB, 2], F32, c)
            meta = sb("meta", [HB, 2 * NLO, 8], F32, c)
            loads, zeroed, zero_ready, vec, columns_ps, columns_in, weights_ps, hot_ready, hot_used, \
                counts_ps, deg_ready, pow_done, totals_ready, offsets_ps, meta_ready, meta_out, act_link = (sem(n) for n in (
                    "loads", "zeroed", "zero_ready", "vec", "columns_ps", "columns_in", "weights_ps", "hot_ready",
                    "hot_used", "counts_ps", "deg_ready", "pow_done", "totals_ready", "offsets_ps", "meta_ready",
                    "meta_out", "act_link"))

            def as_col(ap):
                return ap.rearrange("(n a) -> n a", a=1)

            plan = [(K[:, :], t["consts"])]
            plan += [(rows[:, k, :, :], t[n].rearrange("(a r p) -> r a p", a=2, p=P)) for k, n in
                     enumerate(("src", "dst", "next_dst"))]
            plan += [(rowsF[:, 3, :, :], t["edge_weight"].rearrange("(a r p) -> r a p", a=2, p=P))]
            plan += [(wq[:, :], t["L1_gnn_Wqk"]), (wv[:, :], t["L1_gnn_Wv"]), (wo[:, :], t["L1_gnn_Wo"]),
                     (W["W1"][:, :], t["L0_gnn_W1"]), (W["W2"][:, :], t["L0_gnn_W2"]), (W["W3"][:, :], t["L3_gnn_W"]),
                     (W["We1a"][:, 0:32], t["L2_gnn_We1"][0:D, :]), (W["We1b"][:, 0:32], t["L2_gnn_We1"][D:2 * D, :]),
                     (W["We1c"][0:64, 0:32], t["L2_gnn_We1"][2 * D:2 * D + 64, :]), (W["We2"][0:32, :], t["L2_gnn_We2"]),
                     (W["Wn1a"][:, 0:64], t["L2_gnn_Wn1"][0:D, :]), (W["Wn1b"][:, 0:64], t["L2_gnn_Wn1"][D:2 * D, :]),
                     (W["Wn2"][0:64, :], t["L2_gnn_Wn2"]),
                     (W["Wn2"][64:65, :], t["L2_gnn_bn2"].rearrange("(a n) -> a n", a=1)),
                     (C["be1"][0:32, :], as_col(t["L2_gnn_be1"])), (C["be2"][:, :], as_col(t["L2_gnn_be2"])),
                     (C["bn1"][0:64, :], as_col(t["L2_gnn_bn1"])), (C["bqk"][:, :], as_col(t["L1_gnn_bqk"])),
                     (C["bv"][:, :], as_col(t["L1_gnn_bv"])),
                     (wb[0:1, :], t["L3_gnn_b"].rearrange("(a n) -> a n", a=1)),
                     (wb[1:2, :], t["consts"][0:1, K_ROW1:K_ROW1 + P])]
            plan += [(R[dst][:, :], t[n].partition_broadcast(P)) for dst, n in
                     (("b1", "L0_gnn_b1"), ("b2", "L0_gnn_b2"), ("bo", "L1_gnn_bo"), ("gamma", "L1_gnn_gamma"),
                      ("beta", "L1_gnn_beta"), ("bgamma", "L3_gnn_gamma"), ("bbeta", "L3_gnn_beta"), ("b3", "L3_gnn_b"))]
            count = [0]

            with nc.Block() as block:
                @block.sync
                def _(sp):
                    for dst, src in plan:
                        sp.dma_start(dst, src).then_inc(loads, 16)
                    sp.wait_ge(zero_ready, 1)
                    for k in range(NN // (P * 28)):
                        sp.dma_start(sum1_d[k * P * 28:(k + 1) * P * 28, :].rearrange("(p r) f -> p (r f)", p=P),
                                     zeros[:, :]).then_inc(zeroed, 16)
                    for k in range(EP // (P * 25)):
                        sp.dma_start(he_d[k * P * 25:(k + 1) * P * 25, :].rearrange("(p r) f -> p (r f)", p=P),
                                     zeros[:, 0:25 * D]).then_inc(zeroed, 16)
                    for part in (sum1_d[NN:NN + P, :], he_d[EP:EP + P, :]):
                        sp.dma_start(part, zeros[:, 0:D]).then_inc(zeroed, 16)
                    sp.dma_start(x1_d[NN:NN + P, :], zeros[:, 0:XW]).then_inc(zeroed, 16)
                    sp.wait_ge(meta_ready, 1)
                    sp.dma_start(meta_d.rearrange("(a p l) m -> p a (l m)", a=2, p=HB),
                                 meta[:, :, :].rearrange("p (a l) m -> p a (l m)", a=2)).then_inc(meta_out, 16)
                    sp.wait_ge(meta_out, 16)
                    sp.wait_ge(zeroed, 16 * (NN // (P * 28) + EP // (P * 25) + 3))

                @block.gpsimd
                def _(pool):
                    nc.gpsimd.memset(zeros[:, :], 0.0).then_inc(zero_ready, 1)
                    nc.gpsimd.memset(minus_half[:, :], -0.5)
                    nc.gpsimd.memset(a["half"][:, :], -0.5).then_inc(pow_done, 1)
                    pool.wait_ge(pow_done, 1)
                    pool.wait_ge(deg_ready, 1)
                    nc.gpsimd.tensor_tensor(a["w"][:, :], a["w"][:, :], a["half"][:, :], ALU.pow).then_inc(pow_done, 1)

                @block.tensor
                def _(pe):
                    pe.wait_ge(loads, 16 * len(plan))
                    nc.tensor.transpose(bank[4][:, 0:D], wq[:, :], ident)
                    nc.tensor.transpose(bank[4][:, D:2 * D], wv[:, :], ident).then_inc(weights_ps, 1)
                    pe.wait_ge(columns_in, 1)
                    for k in range(4):
                        for b in range(2):
                            last = nc.tensor.transpose(bank[k][:, b * (NT // 2):(b + 1) * (NT // 2)], rowsF[:, k, b, :],
                                                       K[0:NT // 2, K_ID:K_ID + NT // 2])
                    last.then_inc(columns_ps, 1)
                    pe.wait_ge(act_link, 1)
                    nc.tensor.matmul(bank[5][:, 0:D], wqT[:, :], wqT[:, :], start=True, stop=True)
                    nc.tensor.matmul(bank[5][:, D:D + 1], wqT[:, :], C["bqk"][:, :], start=True, stop=True)
                    nc.tensor.matmul(bank[6][0:1, 0:D], C["bqk"][:, :], wqT[:, :], start=True, stop=True)
                    nc.tensor.matmul(bank[6][0:1, D:D + 1], C["bqk"][:, :], C["bqk"][:, :], start=True, stop=True)
                    nc.tensor.matmul(bank[7][:, 0:D], wvT[:, :], wo[:, :], start=True, stop=True)
                    nc.tensor.matmul(bank[7][:, D:2 * D], C["bv"][:, :].to_broadcast([P, P]), wo[:, :], start=True,
                                     stop=True).then_inc(weights_ps, 1)
                    pe.wait_ge(columns_in, 3)
                    nc.tensor.matmul(bank[4][:, 0:1], ones, cnt[:, :], start=True, stop=True).then_inc(weights_ps, 1)

                    def counts(g, s):
                        pe.wait_ge(hot_ready, g + 1)
                        for b in range(2):
                            nc.tensor.matmul(bank[b][0:HB, :], hot_s[:, s, b * HB:(b + 1) * HB],
                                             hot_s[:, s, NHI:], start=False, stop=False, skip_group_check=True)
                            last = nc.tensor.matmul(bank[2 + b][0:HB, 0:NLO], hot_d[:, s, b * HB:(b + 1) * HB],
                                                    hot_d[:, s, NHI:], start=False, stop=False, skip_group_check=True)
                        last.then_inc(hot_used, 1)
                    pipeline(pe, NT, [(counts, 0)])
                    pe.wait_ge(totals_ready, 1)
                    nc.tensor.matmul(bank[4][0:HB, 0:2], K[0:HB, K_AFTER:K_AFTER + HB], totals[:, :], start=True, stop=True)
                    nc.tensor.matmul(bank[4][0:HB, 2:3], ones[0:HB, 0:HB], totals[:, 0:1], start=True,
                                     stop=True).then_inc(offsets_ps, 1)

                @block.scalar
                def _(act):
                    act.wait_ge(weights_ps, 1)
                    nc.scalar.activation(wqT[:, :], bank[4][:, 0:D], ACT.Copy)
                    nc.scalar.activation(wvT[:, :], bank[4][:, D:2 * D], ACT.Copy).then_inc(act_link, 1)
                    act.wait_ge(weights_ps, 2)
                    nc.scalar.activation(Wscore[:, :], bank[5][:, 0:D + 1], ACT.Copy)
                    for j in range(2):
                        nc.scalar.activation(urow[:, j * TW:j * TW + D + 1], bank[6][0:1, 0:D + 1], ACT.Copy)
                    nc.scalar.activation(W["Wvo"][:, :], bank[7][:, 0:D], ACT.Copy).then_inc(act_link, 1)

                @block.vector
                def _(dve):
                    def link(ins):
                        count[0] += 1
                        ins.then_inc(vec, 1)
                        dve.wait_ge(vec, count[0])

                    dve.wait_ge(loads, 16 * len(plan))
                    nc.vector.tensor_copy(rowsF[:, 0:3, :, :], rows[:, :, :, :]).then_inc(columns_in, 1)
                    dve.wait_ge(columns_ps, 1)
                    for k, dst in enumerate((srcF[:, :], dstF[:, 1:NT + 1], nextF[:, :], ew[:, :])):
                        link(nc.vector.tensor_copy(dst, bank[k][:, 0:NT]))
                    for k in range(4):
                        link(nc.vector.memset(bank[k][:, :], 0.0))
                    link(nc.vector.memset(dstF[:, 0:1], -1.0))
                    link(nc.vector.tensor_copy(srcI[:, :], srcF[:, :]))
                    link(nc.vector.tensor_copy(dstI[:, :], dstF[:, 1:NT + 1]))
                    for whole, hi, lo in ((srcI, "hs", "ls"), (dstI, "hd", "ld")):
                        link(nc.vector.tensor_single_scalar(tmpI[:, :], whole[:, :], 8, ALU.arith_shift_right))
                        link(nc.vector.tensor_copy(split[hi][:, :], tmpI[:, :]))
                        link(nc.vector.tensor_single_scalar(tmpI[:, :], whole[:, :], NLO - 1, ALU.bitwise_and))
                        link(nc.vector.tensor_copy(split[lo][:, :], tmpI[:, :]))
                    link(nc.vector.tensor_scalar(high[:, :], dstF[:, 1:NT + 1], float(HEDGES), None, ALU.is_ge))
                    link(nc.vector.tensor_scalar(low[:, :], dstF[:, 1:NT + 1], float(HEDGES), None, ALU.is_lt))
                    link(nc.vector.tensor_copy(iota[:, :], K[:, K_IOTA:K_IOTA + NLO]))
                    link(nc.vector.tensor_reduce(cnt[:, :], low[:, :], AX_X, ALU.add))
                    link(nc.vector.tensor_tensor(seg_end[:, :], dstF[:, 1:NT + 1], nextF[:, :], ALU.not_equal))
                    link(nc.vector.tensor_scalar(tmpF[:, :], edge_no, float(NN), None, ALU.add))
                    link(nc.vector.tensor_tensor(nextF[:, :], dstF[:, 1:NT + 1], tmpF[:, :], ALU.subtract))
                    link(nc.vector.tensor_tensor(nextF[:, :], nextF[:, :], seg_end[:, :], ALU.mult))
                    link(nc.vector.tensor_tensor(nextF[:, :], nextF[:, :], tmpF[:, :], ALU.add))
                    link(nc.vector.tensor_copy(out_row[:, :], nextF[:, :]))
                    link(nc.vector.tensor_scalar(tmpF[:, :], dstF[:, 1:NT + 1], float(N), None, ALU.is_lt))
                    link(nc.vector.tensor_tensor(seg_end[:, :], seg_end[:, :], tmpF[:, :], ALU.mult))
                    for m in (meta_src, meta_dst):
                        link(nc.vector.memset(m[:, :, :], 0.0))
                    dve.wait_ge(act_link, 2)
                    nc.vector.tensor_tensor(R["bvo"][:, :], bank[7][:, D:2 * D], R["bo"][:, :], ALU.add).then_inc(columns_in, 2)
                    dve.wait_ge(weights_ps, 3)
                    link(nc.vector.tensor_scalar(cnt[:, :], bank[4][:, 0:1], 1.0, float(LOW_STEP - 1), ALU.max, ALU.add))
                    link(nc.vector.tensor_copy(low_groups[:, :], cnt[:, :]))
                    link(nc.vector.tensor_single_scalar(low_groups[:, :], low_groups[:, :], 10, ALU.arith_shift_right))
                    link(nc.vector.tensor_copy(cnt[:, :], low_groups[:, :]))
                    link(nc.vector.tensor_scalar(cnt[:, :], cnt[:, :], 2.0, None, ALU.mult))
                    link(nc.vector.tensor_copy(low_groups[:, :], cnt[:, :]))

                    dve.sem_inc(hot_used, 2)

                    def hots(g, s):
                        at = bass.ds(g, 1)
                        dve.wait_ge(hot_used, g + 1)
                        for out, hi, lo in ((hot_s, "hs", "ls"), (hot_d, "hd", "ld")):
                            nc.vector.tensor_scalar(out[:, s, 0:NHI], iota[:, 0:NHI], split[hi][:, at], None, ALU.is_equal)
                            nc.vector.tensor_scalar(out[:, s, NHI:NHI + NLO], iota[:, :], split[lo][:, at], None,
                                                    ALU.is_equal)
                        nc.vector.tensor_scalar(hot_s[:, s, NHI + NLO:NHI + 2 * NLO], iota[:, :], split["ls"][:, at],
                                                high[:, at], ALU.is_equal, ALU.mult).then_inc(hot_ready, 1)
                    pipeline(dve, NT, [(hots, 0)])

                    dve.wait_ge(hot_used, NT + 2)
                    for b in range(2):
                        cols = slice(b * NLO, (b + 1) * NLO)
                        link(nc.vector.tensor_copy(deg["s"][:, cols], bank[b][0:HB, 0:NLO]))
                        link(nc.vector.tensor_copy(deg["h"][:, cols], bank[b][0:HB, NLO:2 * NLO]))
                        link(nc.vector.tensor_copy(deg["d"][:, cols], bank[2 + b][0:HB, 0:NLO]))
                    nc.vector.tensor_scalar(a["w"][:, :], deg["s"][:, :], 1.0, None, ALU.add).then_inc(deg_ready, 1)
                    node = K[0:HB, K_NODE:K_NODE + 2 * NLO]
                    link(nc.vector.tensor_scalar(a["x"][:, :], deg["s"][:, :], 1.0, None, ALU.max))
                    link(nc.vector.reciprocal(a["x"][:, :], a["x"][:, :]))
                    link(nc.vector.tensor_scalar(a["y"][:, :], deg["s"][:, :], 1.0, None, ALU.min))
                    link(nc.vector.tensor_tensor(a["x"][:, :], a["x"][:, :], a["y"][:, :], ALU.mult))
                    link(nc.vector.tensor_copy(meta[:, :, M_DINV], a["x"][:, :]))
                    link(nc.vector.tensor_tensor(meta[:, :, M_CHIGH], a["x"][:, :], deg["h"][:, :], ALU.mult))
                    link(nc.vector.tensor_scalar(a["x"][:, :], deg["d"][:, :], 1.0, None, ALU.max))
                    link(nc.vector.reciprocal(meta[:, :, M_BINV], a["x"][:, :]))
                    link(nc.vector.memset(a["y"][:, :], 1.0))
                    for b in range(2):
                        cols = slice(b * NLO, (b + 1) * NLO)
                        link(nc.vector.tensor_tensor_scan(a["z"][:, cols], a["y"][:, cols], deg["d"][:, cols], 0.0,
                                                          ALU.mult, ALU.add))
                        link(nc.vector.tensor_copy(totals[:, b:b + 1], a["z"][:, (b + 1) * NLO - 1:(b + 1) * NLO]))
                    dve.sem_inc(totals_ready, 1)
                    dve.wait_ge(offsets_ps, 1)
                    link(nc.vector.tensor_copy(a["x"][:, 0:3], bank[4][0:HB, 0:3]))
                    link(nc.vector.tensor_tensor(a["x"][:, 1:2], a["x"][:, 1:2], a["x"][:, 2:3], ALU.add))
                    for b in range(2):
                        cols = slice(b * NLO, (b + 1) * NLO)
                        link(nc.vector.tensor_scalar(a["z"][:, cols], a["z"][:, cols], a["x"][:, b:b + 1], None, ALU.add))
                    link(nc.vector.tensor_scalar(a["z"][:, :], a["z"][:, :], float(NN - 1), None, ALU.add))
                    link(nc.vector.tensor_tensor(a["z"][:, :], a["z"][:, :], node, ALU.subtract))
                    link(nc.vector.tensor_scalar(a["y"][:, :], deg["d"][:, :], 1.0, None, ALU.min))
                    link(nc.vector.tensor_tensor(a["z"][:, :], a["z"][:, :], a["y"][:, :], ALU.mult))
                    link(nc.vector.tensor_tensor(meta[:, :, M_INDEX], a["z"][:, :], node, ALU.add))
                    link(nc.vector.tensor_scalar(a["x"][:, :], node, float(N), None, ALU.is_lt))
                    link(nc.vector.tensor_scalar(a["y"][:, :], a["y"][:, :], -1.0, 1.0, ALU.mult, ALU.add))
                    link(nc.vector.tensor_tensor(a["x"][:, :], a["x"][:, :], a["y"][:, :], ALU.mult))
                    link(nc.vector.tensor_copy(meta[:, :, M_BARE], a["x"][:, :]))
                    dve.wait_ge(pow_done, 2)
                    link(nc.vector.tensor_copy(meta[:, :, M_GINV], a["w"][:, :]))
                    link(nc.vector.tensor_tensor(a["w"][:, :], a["w"][:, :], a["w"][:, :], ALU.mult))
                    link(nc.vector.tensor_copy(meta[:, :, M_GINV2], a["w"][:, :]))
                    nc.vector.tensor_tensor(meta[:, :, M_Q], a["w"][:, :], a["x"][:, :], ALU.mult).then_inc(meta_ready, 1)

        with phase() as c:
            xin = sb("xin", [P, 2, 8, D], F32, c)
            min_ = sb("min", [P, 2, 8, 8], F32, c)
            xout = sb("xout", [P, 2, 8, XW], F32, c)
            in_sem = [sem("xt_in0"), sem("xt_in1")]
            x_added, m_copied = sem("xt_added"), sem("xt_meta")
            out_sem = [sem("xt_out0"), sem("xt_out1")]
            chunk = 8 * P
            nch = NN // chunk

            with nc.Block() as block:
                @block.sync
                def _(sp):
                    sp.sem_inc(x_added, 2)
                    sp.sem_inc(m_copied, 2)

                    def load(g, s):
                        sp.wait_ge(x_added, g + 1)
                        sp.dma_start(xin[:, s, :, :], t["x"][bass.ds(g * chunk, chunk), :].rearrange("(p j) f -> p j f", p=P)).then_inc(in_sem[s], 16)
                        sp.wait_ge(m_copied, g + 1)
                        sp.dma_start(min_[:, s, :, :], meta_d[bass.ds(g * chunk, chunk), :].rearrange("(p j) f -> p j f", p=P)).then_inc(in_sem[s], 16)
                    pipeline(sp, nch, [(load, 0)])

                @block.vector
                def _(dve):
                    for s in range(2):
                        dve.sem_inc(out_sem[s], 16)

                    def add(g, s):
                        dve.wait_ge(in_sem[s], (g - s) * 16 + 32)
                        dve.wait_ge(out_sem[s], (g - s) * 8 + 16)
                        nc.vector.tensor_tensor(xout[:, s, :, 0:D], xin[:, s, :, :],
                                                R["b2"][:, :].unsqueeze(1).to_broadcast([P, 8, D]), ALU.add).then_inc(x_added, 1)
                        nc.vector.tensor_copy(xout[:, s, :, D:XW], min_[:, s, :, :]).then_inc(m_copied, 1)
                    pipeline(dve, nch, [(add, 0)])

                @block.scalar
                def _(act):
                    def store(g, s):
                        act.wait_ge(m_copied, g + 3)
                        act.dma_start(x1_d[bass.ds(g * chunk, chunk), :].rearrange("(p j) f -> p j f", p=P), xout[:, s, :, :]).then_inc(out_sem[s], 16)
                    pipeline(act, nch, [(store, 0)])
                    for s in range(2):
                        act.wait_ge(out_sem[s], 16 * ((nch + 1 - s) // 2) + 16)
        def layer_sums(dve, tiles, st, tmp, neg, var, link, ready, g):
            n = len(tiles)
            for j, x in enumerate(tiles):
                last = nc.vector.bn_stats(st[:, j, :], x)
            last.then_inc(link, 1)
            dve.wait_ge(link, g * 4 + 1)
            nc.vector.tensor_tensor(tmp[:, 0, 0:n], st[:, 0:n, 1], st[:, 0:n, 4], ALU.add)
            nc.vector.tensor_tensor(tmp[:, 1, 0:n], st[:, 0:n, 1], st[:, 0:n, 4], ALU.subtract)
            nc.vector.tensor_tensor(tmp[:, 2, 0:n], st[:, 0:n, 2], st[:, 0:n, 5], ALU.add).then_inc(link, 1)
            dve.wait_ge(link, g * 4 + 2)
            nc.vector.tensor_scalar(neg, tmp[:, 0, 0:n], -0.5, None, ALU.mult)
            nc.vector.tensor_tensor(tmp[:, 1, 0:n], tmp[:, 1, 0:n], tmp[:, 1, 0:n], ALU.mult).then_inc(link, 1)
            dve.wait_ge(link, g * 4 + 3)
            nc.vector.scalar_tensor_tensor(out=tmp[:, 2, 0:n], in0=tmp[:, 1, 0:n], scalar=D / 4.0, in1=tmp[:, 2, 0:n],
                                           op0=ALU.mult, op1=ALU.add).then_inc(link, 1)
            dve.wait_ge(link, g * 4 + 4)
            nc.vector.tensor_scalar(var, tmp[:, 2, 0:n], 1.0 / D, EPS, ALU.mult, ALU.add).then_inc(ready, 1)

        def layer_scale(pool, neg, var, rs, nb, n, summed, link, ready, g):
            pool.wait_ge(summed, g + 1)
            nc.gpsimd.tensor_tensor(rs, var, minus_half[:, 0:n], ALU.pow).then_inc(link, 1)
            pool.wait_ge(link, g + 1)
            nc.gpsimd.tensor_tensor(nb, neg, rs, ALU.mult).then_inc(ready, 1)

        def layer_all(pool, st, tmp, rs, nb, n, link, ready, g):
            nc.gpsimd.tensor_tensor(tmp[:, 1, 0:n], st[:, 0:n, 1], st[:, 0:n, 4], ALU.subtract)
            nc.gpsimd.tensor_tensor(tmp[:, 0, 0:n], st[:, 0:n, 1], st[:, 0:n, 4], ALU.add)
            nc.gpsimd.tensor_tensor(tmp[:, 2, 0:n], st[:, 0:n, 2], st[:, 0:n, 5], ALU.add).then_inc(link, 1)
            pool.wait_ge(link, g * 5 + 1)
            nc.gpsimd.tensor_tensor(tmp[:, 1, 0:n], tmp[:, 1, 0:n], tmp[:, 1, 0:n], ALU.mult).then_inc(link, 1)
            nc.gpsimd.tensor_scalar(tmp[:, 0, 0:n], tmp[:, 0, 0:n], -0.5, None, ALU.mult)
            nc.gpsimd.tensor_scalar(tmp[:, 2, 0:n], tmp[:, 2, 0:n], 1.0 / D, EPS, ALU.mult, ALU.add)
            hold("pool", pool, link, g * 5 + 2)
            nc.gpsimd.tensor_scalar(tmp[:, 1, 0:n], tmp[:, 1, 0:n], 0.25, None, ALU.mult).then_inc(link, 1)
            pool.wait_ge(link, g * 5 + 3)
            nc.gpsimd.tensor_tensor(tmp[:, 2, 0:n], tmp[:, 2, 0:n], tmp[:, 1, 0:n], ALU.add).then_inc(link, 1)
            pool.wait_ge(link, g * 5 + 4)
            nc.gpsimd.tensor_tensor(rs, tmp[:, 2, 0:n], minus_half[:, 0:n], ALU.pow).then_inc(link, 1)
            pool.wait_ge(link, g * 5 + 5)
            nc.gpsimd.tensor_tensor(nb, tmp[:, 0, 0:n], rs, ALU.mult).then_inc(ready, 1)

        def gather(pool, out, table, index, s):
            pool.indirect_dma_start(out=out, out_offset=None, in_=table,
                                    in_offset=bass.IndirectOffsetOnAxis(ap=index, axis=0)).then_inc(s, 16)

        def groups_of_low(eng):
            return eng.value_load(low_groups[0:1, 0:1], min_val=2, max_val=NGE)

        def hyperedges(conv):
            with phase() as c:
                ix = sb("ix", [P, 2, 2 * G], I32, c)
                col = sb("col", [P, 2, G + 1], F32, c)
                rows = sb("rows", [P, 2, G, D], F32, c)
                ms, md = (sb(n, [P, 2, G, 8], F32, c) for n in ("ms", "md"))
                st = sb("st", [P, G, 6], F32, c)
                tmp = sb("tmp", [P, 3, G], F32, c)
                neg, var, rs, nb = (sb(n, [P, 2, G], F32, c) for n in ("neg", "var", "rs", "nb"))
                h = sb("h", [P, 2, G, D], F32, c)
                same, carry, sumT, out = (sb(n, [P, 2, G, P], F32, c) for n in ("same", "carry", "sumT", "out"))
                whole = sb("whole", [P, 2, G, D], F32, c)
                cols_ready, pool_link, summed, scaled, link, h_ready, bc_ps, same_ready, sumT_ps, sumT_in, he_ps, \
                    whole_in, out_ready, meta_kept, front = (sem(f"he_{n}") for n in (
                        "cols_ready", "pool_link", "summed", "scaled", "link", "h_ready", "bc_ps", "same_ready",
                        "sumT_ps", "sumT_in", "he_ps", "whole_in", "out_ready", "meta_kept", "front"))
                rows_in = [sem("he_rows_in0"), sem("he_rows_in1")]
                stored = [sem("he_stored0"), sem("he_stored1")]
                bc, sT, hps = bank[0], bank[1], [bank[2], bank[3]]
                weight = W["W1"] if conv == 0 else W["W2"]
                n_in = 16 * G * (3 if conv == 0 else 1)

                with nc.Block() as block:
                    @block.gpsimd
                    def _(pool):
                        n = groups_of_low(pool)

                        def part(g, s):
                            hold("pool", pool, stored[s], (g - s) * 8 + 16)
                            nc.gpsimd.tensor_copy(ix[:, s, 0:G], srcI[:, bass.ds(g * G, G)])
                            if conv == 0:
                                nc.gpsimd.tensor_copy(ix[:, s, G:2 * G], dstI[:, bass.ds(g * G, G)])
                            else:
                                nc.gpsimd.tensor_copy(ms[:, s, :, :], meta_src[:, bass.ds(g * G, G), :])
                                nc.gpsimd.tensor_copy(md[:, s, :, :], meta_dst[:, bass.ds(g * G, G), :])
                            nc.gpsimd.tensor_copy(col[:, s, :], dstF[:, bass.ds(g * G, G + 1)]).then_inc(cols_ready, 1)
                            hold("pool", pool, cols_ready, g + 1)
                            for j in range(G):
                                gather(pool, rows[:, s, j, :], t["x"] if conv == 0 else sum1_d, ix[:, s, j:j + 1], rows_in[s])
                                if conv == 0:
                                    gather(pool, ms[:, s, j, :], meta_d, ix[:, s, j:j + 1], rows_in[s])
                                    gather(pool, md[:, s, j, :], meta_d, ix[:, s, G + j:G + j + 1], rows_in[s])
                            if conv == 0:
                                layer_scale(pool, neg[:, s, :], var[:, s, :], rs[:, s, :], nb[:, s, :], G, summed,
                                            pool_link, scaled, g)
                        bounded(pool, n, part)

                    @block.vector
                    def _(dve):
                        n = groups_of_low(dve)
                        nc.vector.memset(whole[:, 1, G - 1, :], 0.0).then_inc(whole_in, 1)

                        def part(g, s):
                            dve.wait_ge(rows_in[s], ((g - s) // 2) * n_in + n_in)
                            if conv == 0:
                                layer_sums(dve, [rows[:, s, j, :] for j in range(G)], st, tmp, neg[:, s, :], var[:, s, :],
                                           link, summed, g)
                                nc.vector.tensor_copy(meta_src[:, bass.ds(g * G, G), :], ms[:, s, :, :])
                                nc.vector.tensor_copy(meta_dst[:, bass.ds(g * G, G), :], md[:, s, :, :])
                            else:
                                for j in range(G):
                                    last = nc.vector.scalar_tensor_tensor(
                                        out=rows[:, s, j, :], in0=rows[:, s, j, :], scalar=ms[:, s, j, M_DINV:M_DINV + 1],
                                        in1=R["b1"][:, :], op0=ALU.mult, op1=ALU.add)
                                last.then_inc(link, 1)
                                dve.wait_ge(link, g + 1)
                                for j in range(G):
                                    last = nc.vector.scalar_tensor_tensor(
                                        out=rows[:, s, j, :], in0=he_last[0][:, :], scalar=ms[:, s, j, M_CHIGH:M_CHIGH + 1],
                                        in1=rows[:, s, j, :], op0=ALU.mult, op1=ALU.add)
                                last.then_inc(scaled, 1)
                            dve.wait_ge(bc_ps, g + 1)
                            for j in range(G):
                                nc.vector.tensor_scalar(same[:, s, j, :], bc[:, j * P:(j + 1) * P], col[:, s, j + 1:j + 2],
                                                        None, ALU.is_equal)
                                last = nc.vector.tensor_scalar(carry[:, s, j, :], bc[:, j * P:(j + 1) * P], col[:, s, j:j + 1],
                                                               last_row, ALU.is_equal, ALU.mult)
                            last.then_inc(same_ready, 1)
                            dve.wait_ge(whole_in, g * G + G + 1)
                            for j in range(G):
                                last = nc.vector.tensor_scalar(out[:, s, j, :], whole[:, s, j, :],
                                                               md[:, s, j, M_BINV:M_BINV + 1], None, ALU.mult)
                            last.then_inc(out_ready, 1)
                        bounded(dve, n, part)

                    @block.scalar
                    def _(act):
                        act.preload_act_table(ACT.Relu)
                        n = groups_of_low(act)

                        def part(g, s):
                            act.wait_ge(scaled, g + 1)
                            if conv == 0:
                                for j in range(G):
                                    last = nc.scalar.activation(h[:, s, j, :], rows[:, s, j, :], ACT.Relu,
                                                                bias=nb[:, s, j:j + 1], scale=rs[:, s, j:j + 1])
                            else:
                                last = nc.scalar.activation(h[:, s, :, :], rows[:, s, :, :], ACT.Relu)
                            last.then_inc(h_ready, 1)
                            act.wait_ge(sumT_ps, g + 1)
                            nc.scalar.activation(sumT[:, s, :, :], sT[:, :].rearrange("p (j f) -> p j f", j=G),
                                                 ACT.Copy).then_inc(sumT_in, 1)
                            for j in range(G):
                                act.wait_ge(he_ps, g * G + j + 1)
                                nc.scalar.activation(whole[:, s, j, :], hps[j % 2][:, 0:D], ACT.Copy).then_inc(whole_in, 1)
                        bounded(act, n, part)

                    @block.tensor
                    def _(pe):
                        n = groups_of_low(pe)
                        pe.sem_inc(same_ready, 1)

                        def part(g, s):
                            pe.wait_ge(cols_ready, g + 1)
                            pe.wait_ge(same_ready, g + 1)
                            for j in range(G):
                                last = nc.tensor.transpose(bc[:, j * P:(j + 1) * P],
                                                           col[:, s, j + 1:j + 2].to_broadcast([P, P]), ident)
                            last.then_inc(bc_ps, 1)
                            pe.wait_ge(h_ready, g + 1)
                            pe.wait_ge(same_ready, g + 2)
                            for j in range(G):
                                last = nc.tensor.matmul(sT[:, j * P:(j + 1) * P], h[:, s, j, :], same[:, s, j, :],
                                                        start=True, stop=True)
                            last.then_inc(sumT_ps, 1)
                            pe.wait_ge(sumT_in, g + 1)
                            for j in range(G):
                                before = whole[:, s, j - 1, :] if j else whole[:, 1 - s, G - 1, :]
                                nc.tensor.matmul(hps[j % 2][:, 0:D], sumT[:, s, j, :], weight[:, :], start=True, stop=False)
                                pe.wait_ge(whole_in, g * G + j + 1)
                                nc.tensor.matmul(hps[j % 2][:, 0:D], carry[:, s, j, :], before, start=False,
                                                 stop=True).then_inc(he_ps, 1)
                        bounded(pe, n, part)

                    @block.sync
                    def _(sp):
                        n = groups_of_low(sp)
                        for s in range(2):
                            sp.sem_inc(stored[s], 16)

                        def part(g, s):
                            sp.wait_ge(out_ready, g + 1)
                            sp.dma_start(rows_of(he_d, g, D), out[:, s, :, :]).then_inc(stored[s], 16)
                            hold("sp", sp, stored[s], (g - s) * 8 + 32)
                        bounded(sp, n, part)

        def last_hyperedge(conv):
            with phase() as c:
                m = sb("m", [P, 8], F32, c)
                v = sb("v", [P, 4], F32, c)
                vi = sb("vi", [P, 1], I32, c)
                e = sb("e", [P, NT], F32, c)
                m_in, link, v_ready, row_in = (sem(f"last_{n}") for n in ("m_in", "link", "v_ready", "row_in"))
                with nc.Block() as block:
                    @block.sync
                    def _(sp):
                        sp.dma_start(m[:, :], meta_d[HEDGES - 1, :].partition_broadcast(P)).then_inc(m_in, 16)

                    @block.vector
                    def _(dve):
                        k = [0]

                        def chain(ins):
                            k[0] += 1
                            ins.then_inc(link, 1)
                            dve.wait_ge(link, k[0])

                        dve.wait_ge(m_in, 16)
                        chain(nc.vector.tensor_scalar(v[:, 0:1], m[:, M_INDEX:M_INDEX + 1], float(NN), None, ALU.is_ge))
                        chain(nc.vector.tensor_scalar(v[:, 1:2], m[:, M_INDEX:M_INDEX + 1], float(-NN - EP), None, ALU.add))
                        chain(nc.vector.tensor_tensor(v[:, 2:3], v[:, 0:1], v[:, 1:2], ALU.mult))
                        chain(nc.vector.tensor_scalar(v[:, 3:4], v[:, 2:3], float(EP), None, ALU.add))
                        nc.vector.tensor_copy(vi[:, :], v[:, 3:4]).then_inc(v_ready, 1)
                        if conv == 0:
                            chain(nc.vector.tensor_tensor(e[:, :], meta_dst[:, :, M_INDEX], edge_no, ALU.subtract))
                            chain(nc.vector.tensor_scalar(e[:, :], e[:, :], float(-NN), None, ALU.add))
                            chain(nc.vector.tensor_tensor(e[:, :], e[:, :], low[:, :], ALU.mult))
                            chain(nc.vector.tensor_tensor(e[:, :], e[:, :], edge_no, ALU.add))
                            chain(nc.vector.tensor_copy(he_index[:, :], e[:, :]))

                    @block.gpsimd
                    def _(pool):
                        pool.wait_ge(v_ready, 1)
                        gather(pool, he_last[conv][:, :], he_d, vi[:, :], row_in)
                        pool.wait_ge(row_in, 16)

        def to_sources(conv):
            with phase() as c:
                width = D if conv == 0 else XW
                ix = sb("ix", [P, 2, G], I32, c)
                col = sb("col", [P, 2, G], F32, c)
                lo = sb("lo", [P, 2, G], F32, c)
                dinv = sb("dinv", [P, 2, G], F32, c)
                rows = sb("rows", [P, 2, G, D], F32, c)
                same = sb("same", [P, 2, G, P], F32, c)
                junk = sb("junk", [P, P], F32, c)
                later = sb("later", [P, 3, G], F32, c)
                to = sb("to", [P, 2, G], I32, c)
                add = sb("add", [P, 2, G, width], F32, c)
                cols_ready, bc_ps, same_ready, comb_ps, add_ready, to_ready, link, added, cleared, comb_free = (
                    sem(f"ts_{n}") for n in ("cols_ready", "bc_ps", "same_ready", "comb_ps", "add_ready", "to_ready",
                                             "link", "added", "cleared", "comb_free"))
                rows_in = [sem("ts_rows_in0"), sem("ts_rows_in1")]
                bc, comb = bank[0], bank[1]
                table = sum1_d if conv == 0 else x1_d

                with nc.Block() as block:
                    @block.gpsimd
                    def _(pool):
                        n = groups_of_low(pool)
                        nc.gpsimd.memset(add[:, :, :, :], 0.0).then_inc(cleared, 1)

                        def part(g, s):
                            nc.gpsimd.tensor_copy(ix[:, s, :], he_index[:, bass.ds(g * G, G)])
                            nc.gpsimd.tensor_copy(col[:, s, :], srcF[:, bass.ds(g * G, G)])
                            nc.gpsimd.tensor_copy(dinv[:, s, :], meta_src[:, bass.ds(g * G, G), M_DINV])
                            nc.gpsimd.tensor_copy(lo[:, s, :], low[:, bass.ds(g * G, G)]).then_inc(cols_ready, 1)
                            hold("pool", pool, cols_ready, g + 1)
                            for j in range(G):
                                gather(pool, rows[:, s, j, :], he_d, ix[:, s, j:j + 1], rows_in[s])
                            hold("pool", pool, to_ready, g + 1)
                            hold("pool", pool, add_ready, g + 1)
                            for j in range(G):
                                pool.indirect_dma_start(out=table, out_offset=bass.IndirectOffsetOnAxis(ap=to[:, s, j:j + 1], axis=0),
                                                        in_=add[:, s, j, :], in_offset=None, compute_op=ALU.add).then_inc(added, 16)
                                hold("pool", pool, added, (g * G + j) * 16 + 16)
                        bounded(pool, n, part)

                    @block.tensor
                    def _(pe):
                        n = groups_of_low(pe)

                        def part(g, s):
                            pe.wait_ge(cols_ready, g + 1)
                            for j in range(G):
                                last = nc.tensor.transpose(bc[:, j * P:(j + 1) * P], col[:, s, j:j + 1].to_broadcast([P, P]), ident)
                            last.then_inc(bc_ps, 1)
                            pe.wait_ge(same_ready, g + 1)
                            hold("pe", pe, rows_in[s], (g - s) * (8 * G) + 16 * G)
                            for j in range(G):
                                last = nc.tensor.matmul(comb[:, j * P:(j + 1) * P], same[:, s, j, :], rows[:, s, j, :],
                                                        start=True, stop=True)
                            last.then_inc(comb_ps, 1)
                        bounded(pe, n, part)

                    @block.vector
                    def _(dve):
                        n = groups_of_low(dve)

                        def part(g, s):
                            dve.wait_ge(bc_ps, g + 1)
                            for j in range(G):
                                nc.vector.tensor_scalar(same[:, s, j, :], bc[:, j * P:(j + 1) * P], col[:, s, j:j + 1],
                                                        lo[:, s, j:j + 1], ALU.is_equal, ALU.mult)
                                last = nc.vector.scalar_tensor_tensor(out=junk[:, :], in0=bc[:, j * P:(j + 1) * P],
                                                                      scalar=col[:, s, j:j + 1], in1=after, op0=ALU.is_equal,
                                                                      op1=ALU.mult, accum_out=later[:, 0, j:j + 1])
                                last.then_inc(link, 1)
                                dve.wait_ge(link, g * (G + 3) + j + 1)
                            dve.sem_inc(same_ready, 1)
                            nc.vector.tensor_scalar(later[:, 1, :], later[:, 0, :], 1.0, None, ALU.min)
                            nc.vector.tensor_scalar(later[:, 2, :], col[:, s, :], -1.0, dump_row, ALU.mult, ALU.add).then_inc(link, 1)
                            dve.wait_ge(link, g * (G + 3) + G + 1)
                            nc.vector.tensor_tensor(later[:, 1, :], later[:, 1, :], later[:, 2, :], ALU.mult).then_inc(link, 1)
                            dve.wait_ge(link, g * (G + 3) + G + 2)
                            nc.vector.tensor_tensor(later[:, 2, :], later[:, 1, :], col[:, s, :], ALU.add).then_inc(link, 1)
                            dve.wait_ge(link, g * (G + 3) + G + 3)
                            nc.vector.tensor_copy(to[:, s, :], later[:, 2, :]).then_inc(to_ready, 1)
                            dve.wait_ge(to_ready, g + 1)
                        bounded(dve, n, part)

                    @block.scalar
                    def _(act):
                        act.preload_act_table(ACT.Copy)
                        act.wait_ge(cleared, 1)
                        n = groups_of_low(act)

                        def part(g, s):
                            act.wait_ge(comb_ps, g + 1)
                            for j in range(G):
                                if conv == 0:
                                    last = nc.scalar.activation(add[:, s, j, 0:D], comb[:, j * P:(j + 1) * P], ACT.Copy)
                                else:
                                    last = nc.scalar.activation(add[:, s, j, 0:D], comb[:, j * P:(j + 1) * P], ACT.Copy,
                                                                scale=dinv[:, s, j:j + 1])
                            last.then_inc(add_ready, 1)
                        bounded(act, n, part)

        for conv in range(2):
            hyperedges(conv)
            last_hyperedge(conv)
            to_sources(conv)
        S = 4

        def slot_count(g, s, dmas):
            return (g - s) * (16 // S * dmas) + 16 * dmas

        with phase() as c:
            S8 = 8
            last_norm = 6
            ix = sb("ix", [P, 4, 2 * G], I32, c)
            xs = sb("xs", [P, 4, G, XW], F32, c)
            xd = sb("xd", [P, S8, G, XW], F32, c)
            hs = sb("hs", [P, 4, G, TW], F32, c)
            hd = sb("hd", [P, S8, G, D], F32, c)
            x2 = sb("x2", [P, 4, G, D], F32, c)
            bc = sb("bc", [P, 4, G * P], I32, c)
            st = sb("st", [P, S8, 3 * G, 6], F32, c)
            tmp = sb("tmp", [P, 2, 3, 3 * G], F32, c)
            rs, nb = (sb(n, [P, S8, 3 * G], F32, c) for n in ("rs", "nb"))
            hdT, attT = (sb(n, [P, 2, G * P], F32, c) for n in ("hdT", "attT"))
            junk = sb("junk", [P, G, D + 1], F32, c)
            score, e, rden = (sb(n, [P, S8, G], F32, c) for n in ("score", "e", "rden"))
            same, carry = (sb(n, [P, 4, G, P], F32, c) for n in ("same", "carry"))
            sums = sb("sums", [P, 4, G, TW], F32, c)
            ix_ready, pool_link, summed, summed2, scaled, x_link, h_ready, hdT_ps, hdT_in, r_ps, clip_link, score_ready, \
                e_ready, same_ready, sum_ps, sum_in, set_up, attT_ps, attT_in, o_ps, o_used, rden_ready, row_link, z_ready, \
                x2_link, x2_ready = (sem(f"at_{n}") for n in (
                    "ix_ready", "pool_link", "summed", "summed2", "scaled", "x_link", "h_ready", "hdT_ps", "hdT_in", "r_ps",
                    "clip_link", "score_ready", "e_ready", "same_ready", "sum_ps", "sum_in", "set_up", "attT_ps",
                    "attT_in", "o_ps", "o_used", "rden_ready", "row_link", "z_ready", "x2_link", "x2_ready"))
            rows_in = [sem(f"at_rows_in{s}") for s in range(S8)]
            bc_in, stored = ([sem(f"at_{n}{s}") for s in range(4)] for n in ("bc_in", "stored"))
            hdT_p, rp, sum_p, attT_p, o_p = bank[0], [bank[1], bank[2]], bank[3], bank[4], [bank[5], bank[6]]

            def count8(g, s, dmas):
                return (g - s) * (2 * dmas) + 16 * dmas

            def count4(g, s):
                return (g - s % 4) * 4 + 16

            with nc.Block() as block:
                @block.gpsimd
                def _(pool):
                    pool.wait_ge(set_up, 1)

                    def src_used(g, s):
                        hold("pool", pool, h_ready, g + 1)

                    def dst_used(g, s):
                        hold("pool", pool, row_link, g + 1)

                    def rows(g, s):
                        at = s % 4
                        nc.gpsimd.tensor_copy(ix[:, at, 0:G], srcI[:, bass.ds(g * G, G)])
                        nc.gpsimd.tensor_copy(ix[:, at, G:2 * G], dstI[:, bass.ds(g * G, G)]).then_inc(ix_ready, 1)
                        hold("pool", pool, ix_ready, g + 1)
                        for j in range(G):
                            gather(pool, xs[:, at, j, :], x1_d, ix[:, at, j:j + 1], rows_in[s])
                            gather(pool, xd[:, s, j, :], x1_d, ix[:, at, G + j:G + j + 1], rows_in[s])

                    def rows_summed(g, s):
                        hold("pool", pool, summed, g + 1)

                    def attended_summed(g, s):
                        hold("pool", pool, summed2, g + 1)

                    def scales(k, s):
                        layer_all(pool, st[:, s, :, :], tmp[:, s % 2, :, :], rs[:, s, :], nb[:, s, :], 3 * G, pool_link,
                                  scaled, k)
                    pipeline(pool, NGE, [(src_used, 4), (dst_used, S8), (rows, 0), (rows_summed, 1),
                                         (attended_summed, 1 + last_norm), (scales, 1, last_norm)], S8)

                @block.sync
                def _(sp):
                    def bc_used(g, s):
                        sp.wait_ge(same_ready, g + 1)

                    def load_bc(g, s):
                        sp.dma_start(bc[:, s % 4, :], t["dst"][bass.ds(g * (G * P), G * P)].partition_broadcast(P)).then_inc(
                            bc_in[s % 4], 16)

                    def store(g, s):
                        sp.wait_ge(x2_ready, g + 1)
                        sp.dma_start(rows_of(x2_d, g, D, NN), x2[:, s % 4, :, :]).then_inc(stored[s % 4], 16)
                    pipeline(sp, NGE, [(bc_used, 5), (load_bc, 1), (store, 9)], S8)
                    for s in range(4):
                        sp.wait_ge(stored[s], 16 * ((NGE - s + 3) // 4) + 16)

                @block.vector
                def _(dve):
                    nc.vector.memset(hs[:, :, :, D:D + 1], 1.0)
                    nc.vector.memset(st[:, :, :, :], 0.0)
                    nc.vector.memset(sums[:, 3, G - 1, :], 0.0).then_inc(sum_in, 1)
                    dve.wait_ge(sum_in, 1)
                    dve.sem_inc(set_up, 1)
                    dve.sem_inc(score_ready, 1)
                    dve.sem_inc(o_used, 2)
                    for s in range(4):
                        dve.sem_inc(stored[s], 16)

                    def last_edge(g, s):
                        dve.wait_ge(rows_in[s], count8(g, s, 2 * G))
                        for x in (xs[:, s % 4, :, :], xd[:, s, :, :]):
                            for j in range(G):
                                last = nc.vector.scalar_tensor_tensor(
                                    out=x[:, j, 0:D], in0=he_last[1][:, :], scalar=x[:, j, D + M_CHIGH:D + M_CHIGH + 1],
                                    in1=x[:, j, 0:D], op0=ALU.mult, op1=ALU.add)
                        last.then_inc(x_link, 1)
                        nc.vector.tensor_copy(table_src[:, bass.ds(g * G, G)], xs[:, s % 4, :, D + M_INDEX])
                        nc.vector.tensor_copy(table_dst[:, bass.ds(g * G, G)], xd[:, s, :, D + M_INDEX])
                        nc.vector.tensor_copy(ginv_dst[:, bass.ds(g * G, G)], xd[:, s, :, D + M_GINV])

                    def stats(g, s):
                        dve.wait_ge(x_link, g + 1)
                        for j in range(G):
                            nc.vector.bn_stats(st[:, s, j, :], xs[:, s % 4, j, 0:D])
                        for j in range(G):
                            last = nc.vector.bn_stats(st[:, s, G + j, :], xd[:, s, j, 0:D])
                        last.then_inc(summed, 1)

                    def scores(g, s):
                        dve.wait_ge(r_ps, g + 1)
                        for j in range(G):
                            last = nc.vector.scalar_tensor_tensor(
                                out=junk[:, j, :], in0=rp[j // 2][:, (j % 2) * TW:(j % 2) * TW + D + 1], scalar=float(D) ** -0.5,
                                in1=hs[:, s % 4, j, 0:D + 1], op0=ALU.mult, op1=ALU.mult, accum_out=score[:, s, j:j + 1])
                        last.then_inc(clip_link, 1)
                        dve.wait_ge(clip_link, g + 1)
                        nc.vector.tensor_scalar(score[:, s, :], score[:, s, :], 5.0, -5.0, ALU.min, ALU.max).then_inc(score_ready, 1)

                    def sames(g, s):
                        dve.wait_ge(bc_in[s % 4], count4(g, s))
                        for j in range(G):
                            nc.vector.tensor_scalar(carry[:, s % 4, j, :], bc[:, s % 4, j * P:(j + 1) * P],
                                                    dstF[:, bass.ds(g * G + j, 1)], last_row, ALU.is_equal, ALU.mult)
                        dve.wait_ge(e_ready, g + 1)
                        for j in range(G):
                            last = nc.vector.tensor_scalar(same[:, s % 4, j, :], bc[:, s % 4, j * P:(j + 1) * P],
                                                           dstF[:, bass.ds(g * G + (j + 1), 1)], e[:, s, j:j + 1],
                                                           ALU.is_equal, ALU.mult)
                        last.then_inc(same_ready, 1)

                    def denominator(g, s):
                        dve.wait_ge(o_ps, g + 1)
                        nc.vector.reciprocal(rden[:, s, :], sums[:, s % 4, :, D]).then_inc(rden_ready, 1)

                    def attended(g, s):
                        dve.wait_ge(rden_ready, g + 1)
                        for j in range(G):
                            last = nc.vector.scalar_tensor_tensor(
                                out=hd[:, s, j, :], in0=o_p[s % 2][:, j * P:(j + 1) * P], scalar=rden[:, s, j:j + 1],
                                in1=hd[:, s, j, :], op0=ALU.mult, op1=ALU.add)
                        last.then_inc(o_used, 1)

                    def biased(g, s):
                        dve.wait_ge(stored[s % 4], count4(g, s))
                        nc.vector.tensor_tensor(x2[:, s % 4, :, :], xd[:, s, :, 0:D],
                                                R["beta"][:, :].unsqueeze(1).to_broadcast([P, G, D]), ALU.add)
                        dve.wait_ge(o_used, g + 3)
                        nc.vector.tensor_tensor(hd[:, s, :, :], hd[:, s, :, :],
                                                R["bvo"][:, :].unsqueeze(1).to_broadcast([P, G, D]), ALU.add).then_inc(row_link, 1)

                    def stats2(g, s):
                        dve.wait_ge(row_link, g + 1)
                        for j in range(G):
                            last = nc.vector.bn_stats(st[:, (s + last_norm) % S8, 2 * G + j, :], hd[:, s, j, :])
                        last.then_inc(summed2, 1)

                    def times_gamma(g, s):
                        dve.wait_ge(z_ready, g + 1)
                        nc.vector.tensor_tensor(hd[:, s, :, :], hd[:, s, :, :],
                                                R["gamma"][:, :].unsqueeze(1).to_broadcast([P, G, D]), ALU.mult).then_inc(x2_link, 1)

                    def added(g, s):
                        dve.wait_ge(x2_link, g + 1)
                        nc.vector.tensor_tensor(x2[:, s % 4, :, :], x2[:, s % 4, :, :], hd[:, s, :, :], ALU.add).then_inc(x2_ready, 1)
                    pipeline(dve, NGE, [(denominator, 7), (last_edge, 1), (attended, 7), (sames, 4), (biased, 7), (stats, 1),
                                        (stats2, 7), (times_gamma, 8), (scores, 3), (added, 8)], S8)

                @block.scalar
                def _(act):
                    act.preload_act_table(ACT.Exp)
                    act.wait_ge(set_up, 1)

                    def relus(g, s):
                        act.wait_ge(scaled, g + 1)
                        for k, x, h in ((G, xd[:, s, :, :], hd[:, s, :, :]), (0, xs[:, s % 4, :, :], hs[:, s % 4, :, :])):
                            for j in range(G):
                                last = nc.scalar.activation(h[:, j, 0:D], x[:, j, 0:D], ACT.Relu, bias=nb[:, s, k + j:k + j + 1],
                                                            scale=rs[:, s, k + j:k + j + 1])
                        last.then_inc(h_ready, 1)

                    def hdT_copy(g, s):
                        act.wait_ge(hdT_ps, g + 1)
                        nc.scalar.activation(hdT[:, s % 2, :], hdT_p[:, :], ACT.Copy).then_inc(hdT_in, 1)

                    def exps(g, s):
                        act.wait_ge(score_ready, g + 2)
                        nc.scalar.activation(e[:, s, :], score[:, s, :], ACT.Exp).then_inc(e_ready, 1)

                    def total(j):
                        def part(g, s):
                            act.wait_ge(sum_ps, g * G + j + 1)
                            nc.scalar.activation(sums[:, s % 4, j, 0:D + 1], sum_p[:, 0:D + 1], ACT.Copy).then_inc(sum_in, 1)
                        return part

                    def attT_copy(g, s):
                        act.wait_ge(attT_ps, g + 1)
                        nc.scalar.activation(attT[:, s % 2, :], attT_p[:, :], ACT.Copy).then_inc(attT_in, 1)

                    def normed(g, s):
                        act.wait_ge(scaled, g + last_norm + 1)
                        at = (s + last_norm) % S8
                        for j in range(G):
                            last = nc.scalar.activation(hd[:, s, j, :], hd[:, s, j, :], ACT.Identity,
                                                        bias=nb[:, at, 2 * G + j:2 * G + j + 1],
                                                        scale=rs[:, at, 2 * G + j:2 * G + j + 1])
                        last.then_inc(z_ready, 1)
                    pipeline(act, NGE, [(hdT_copy, 3), (total(0), 5), (exps, 4), (normed, 8), (total(1), 5), (relus, 2),
                                        (total(2), 5), (attT_copy, 6), (total(3), 5)], S8)

                @block.tensor
                def _(pe):
                    pe.wait_ge(set_up, 1)

                    def transposes(g, s):
                        pe.wait_ge(h_ready, g + 1)
                        for j in range(G):
                            last = nc.tensor.transpose(hdT_p[:, j * P:(j + 1) * P], hd[:, s, j, :], ident)
                        last.then_inc(hdT_ps, 1)

                    def product(g, s):
                        pe.wait_ge(score_ready, g + 1)
                        pe.wait_ge(hdT_in, g + 1)
                        for j in range(G):
                            out = rp[j // 2][:, (j % 2) * TW:(j % 2) * TW + D + 1]
                            nc.tensor.matmul(out, hdT[:, s % 2, j * P:(j + 1) * P], Wscore[:, :], start=True, stop=False)
                            last = nc.tensor.matmul(out, ones[0:1, :], urow[:, 0:D + 1], start=False, stop=True)
                        last.then_inc(r_ps, 1)

                    def total(j):
                        def part(g, s):
                            if j == 0:
                                pe.wait_ge(same_ready, g + 1)
                            before = sums[:, s % 4, j - 1, 0:D + 1] if j else sums[:, (s - 1) % 4, G - 1, 0:D + 1]
                            pe.wait_ge(sum_in, g * G + j + 1)
                            nc.tensor.matmul(sum_p[:, 0:D + 1], same[:, s % 4, j, :], hs[:, s % 4, j, 0:D + 1], start=True, stop=False)
                            nc.tensor.matmul(sum_p[:, 0:D + 1], carry[:, s % 4, j, :], before, start=False,
                                             stop=True).then_inc(sum_ps, 1)
                        return part

                    def attended(g, s):
                        pe.wait_ge(sum_in, g * G + G + 1)
                        for j in range(G):
                            last = nc.tensor.transpose(attT_p[:, j * P:(j + 1) * P], sums[:, s % 4, j, 0:D], ident)
                        last.then_inc(attT_ps, 1)

                    def output(g, s):
                        pe.wait_ge(attT_in, g + 1)
                        pe.wait_ge(o_used, g + 1)
                        for j in range(G):
                            last = nc.tensor.matmul(o_p[s % 2][:, j * P:(j + 1) * P], attT[:, s % 2, j * P:(j + 1) * P],
                                                    W["Wvo"][:, :], start=True, stop=True)
                        last.then_inc(o_ps, 1)
                    pipeline(pe, NGE, [(total(0), 5), (product, 3), (total(1), 5), (attended, 6), (total(2), 5),
                                       (transposes, 2), (total(3), 5), (output, 6)], S8)

        def update(edges):
            n = NGE if edges else NGN
            norms = 2 if edges else 4
            late = 2 * (norms - 1)
            S = 8

            def slot_count(g, s, dmas):
                return (g - s) * (16 // S * dmas) + 16 * dmas

            with phase() as c:
                x1 = sb("x1", [P, S, G, XW], F32, c)
                h = sb("h", [P, S, G, D], F32, c)
                x2 = sb("x2", [P, S, G, D], F32, c)
                st = sb("st", [P, 2, norms * G, 6], F32, c)
                tmp = sb("tmp", [P, 2, 3, norms * G], F32, c)
                rs, nb = (sb(k, [P, S, norms * G], F32, c) for k in ("rs", "nb"))
                summed = [sem(f"up_summed{i}") for i in range(norms)]
                scaled, pool_link, st_clear = sem("up_scaled"), sem("up_pool_link"), sem("up_st_clear")
                x_ready, h_ready, hb_link, z_ready, x2_link, x2_ready = (sem(f"up_{k}") for k in (
                    "x_ready", "h_ready", "hb_link", "z_ready", "x2_link", "x2_ready"))
                used = sem("up_used")
                rows_in = [sem(f"up_rows_in{s}") for s in range(S)]
                stored, r_stored = ([sem(f"up_{k}{s}") for s in range(S)] for k in ("stored", "r_stored"))
                if edges:
                    att = sb("att", [P, S, G, TW], F32, c)
                    attT = sb("attT", [P, S, G * P], F32, c)
                    rden = sb("rden", [P, S, G], F32, c)
                    attT_ps, attT_in, o_ps, rden_ready, o_used = (sem(f"up_{k}") for k in (
                        "attT_ps", "attT_in", "o_ps", "rden_ready", "o_used"))
                else:
                    h2 = sb("h2", [P, S, G, D], F32, c)
                    r = sb("r", [P, S, G, RW], F32, c)
                    u = sb("u", [P, S, G, D + 2], F32, c)
                    h2_ready, x3_ready, h3_ready, u_ready, gram_done, gram_zero = (sem(f"up_{k}") for k in (
                        "h2_ready", "x3_ready", "h3_ready", "u_ready", "gram_done", "gram_zero"))
                n_in = 2 if edges else 1

                with nc.Block() as block:
                    @block.sync
                    def _(sp):
                        sp.sem_inc(used, S)

                        def load(g, s):
                            sp.wait_ge(used, g + 1)
                            if edges:
                                sp.dma_start(x1[:, s, :, :], rows_of(xd_d, g, XW)).then_inc(rows_in[s], 16)
                                sp.dma_start(att[:, s, :, 0:D + 1], rows_of(att_d, g, D + 1)).then_inc(rows_in[s], 16)
                            else:
                                sp.dma_start(x1[:, s, :, :], node_rows_of(x1_d, g, XW)).then_inc(rows_in[s], 16)

                        def store(g, s):
                            sp.wait_ge(x2_ready, g + 1)
                            if edges:
                                sp.dma_start(rows_of(x2_d, g, D, NN), x2[:, s, :, :]).then_inc(stored[s], 16)
                            else:
                                sp.dma_start(node_rows_of(x2_d, g, D), x2[:, s, :, :]).then_inc(stored[s], 16)

                        def store_r(g, s):
                            sp.wait_ge(gram_done, g + 1)
                            sp.dma_start(node_rows_of(r_d, g, RW), r[:, s, :, :]).then_inc(r_stored[s], 16)
                        pipeline(sp, n, [(load, 0), (store, 6)] if edges else [(load, 0), (store, 6), (store_r, 8)], S)
                        for s in range(S):
                            sp.wait_ge(stored[s], 16 * ((n - s + S - 1) // S) + 16)
                            if not edges:
                                sp.wait_ge(r_stored[s], 16 * ((n - s + S - 1) // S) + 16)

                    @block.gpsimd
                    def _(pool):
                        pool.wait_ge(st_clear, 1)

                        def summed_rows(i):
                            def part(g, s):
                                hold("pool", pool, summed[i], g + 1)
                            return part

                        def scales(k, s):
                            layer_all(pool, st[:, s % 2, :, :], tmp[:, s % 2, :, :], rs[:, s, :], nb[:, s, :], norms * G, pool_link,
                                      scaled, k)
                        pipeline(pool, n, [(summed_rows(i), 2 * i) for i in range(norms)] + [(scales, 0, late)], S)

                    @block.vector
                    def _(dve):
                        nc.vector.memset(st[:, :, :, :], 0.0).then_inc(st_clear, 1)
                        dve.wait_ge(st_clear, 1)
                        for s in range(S):
                            dve.sem_inc(stored[s], 16)
                            dve.sem_inc(r_stored[s], 16)
                        if edges:
                            dve.sem_inc(o_used, 4)
                        else:
                            nc.vector.memset(bank[0][:, :], 0.0)
                            nc.vector.memset(bank[1][:, :], 0.0).then_inc(gram_zero, 1)
                            nc.vector.memset(r[:, :, :, 2 * D:2 * D + 1], 1.0)
                            nc.vector.memset(r[:, :, :, 2 * D + 2:RW], 0.0)

                        def sums_of(i, tiles, g, s):
                            for j, x in enumerate(tiles):
                                last = nc.vector.bn_stats(st[:, s % 2, i * G + j, :], x)
                            last.then_inc(summed[i], 1)

                        def first(g, s):
                            dve.wait_ge(rows_in[s], slot_count(g, s, n_in))
                            if edges:
                                nc.vector.reciprocal(rden[:, s, :], att[:, s, :, D]).then_inc(rden_ready, 1)
                            else:
                                for j in range(G):
                                    last = nc.vector.scalar_tensor_tensor(
                                        out=x1[:, s, j, 0:D], in0=he_last[1][:, :],
                                        scalar=x1[:, s, j, D + M_CHIGH:D + M_CHIGH + 1], in1=x1[:, s, j, 0:D],
                                        op0=ALU.mult, op1=ALU.add)
                                last.then_inc(x_ready, 1)
                                dve.wait_ge(x_ready, g + 1)
                            sums_of(0, [x1[:, s, j, 0:D] for j in range(G)], g, s)

                        def second(g, s):
                            dve.wait_ge(h_ready, g + 1)
                            row = R["bvo"] if edges else R["bo"]
                            if edges:
                                dve.wait_ge(o_ps, g + 1)
                                dve.wait_ge(rden_ready, g + 1)
                                for j in range(G):
                                    last = nc.vector.scalar_tensor_tensor(
                                        out=h[:, s, j, :], in0=bank[2 + s % 4][:, j * P:(j + 1) * P], scalar=rden[:, s, j:j + 1],
                                        in1=h[:, s, j, :], op0=ALU.mult, op1=ALU.add)
                                last.then_inc(o_used, 1)
                                dve.wait_ge(o_used, g + 5)
                            nc.vector.tensor_tensor(h[:, s, :, :], h[:, s, :, :],
                                                    row[:, :].unsqueeze(1).to_broadcast([P, G, D]), ALU.add).then_inc(hb_link, 1)
                            dve.wait_ge(hb_link, g + 1)
                            sums_of(1, [h[:, s, j, :] for j in range(G)], g, s)

                        def third(g, s):
                            dve.wait_ge(z_ready, g + 1)
                            dve.wait_ge(stored[s], slot_count(g, s, 1))
                            nc.vector.tensor_tensor(x2[:, s, :, :], h[:, s, :, :],
                                                    R["gamma"][:, :].unsqueeze(1).to_broadcast([P, G, D]), ALU.mult)
                            nc.vector.tensor_tensor(x1[:, s, :, 0:D], x1[:, s, :, 0:D],
                                                    R["beta"][:, :].unsqueeze(1).to_broadcast([P, G, D]), ALU.add).then_inc(x2_link, 1)
                            dve.wait_ge(x2_link, g + 1)
                            nc.vector.tensor_tensor(x2[:, s, :, :], x2[:, s, :, :], x1[:, s, :, 0:D], ALU.add).then_inc(x2_ready, 1)
                            if edges:
                                dve.wait_ge(x2_ready, g + 1)
                                dve.sem_inc(used, 1)
                            else:
                                dve.wait_ge(x2_ready, g + 1)
                                sums_of(2, [x2[:, s, j, :] for j in range(G)], g, s)

                        def fourth(g, s):
                            dve.wait_ge(h2_ready, g + 1)
                            dve.wait_ge(r_stored[s], slot_count(g, s, 1))
                            nc.vector.tensor_tensor(r[:, s, :, 0:D], x2[:, s, :, :], h2[:, s, :, :], ALU.add)
                            nc.vector.tensor_copy(r[:, s, :, 2 * D + 1], x1[:, s, :, D + M_GINV])
                            nc.vector.tensor_copy(u[:, s, :, D], x1[:, s, :, D + M_Q])
                            nc.vector.tensor_copy(u[:, s, :, D + 1], x1[:, s, :, D + M_BARE]).then_inc(x3_ready, 1)
                            dve.wait_ge(x3_ready, g + 1)
                            sums_of(3, [r[:, s, j, 0:D] for j in range(G)], g, s)
                        pipeline(dve, n, [(third, 4), (second, 2), (first, 0)] if edges else
                                 [(fourth, 6), (third, 4), (second, 2), (first, 0)], S)
                        if not edges:
                            dve.wait_ge(gram_done, n)
                            nc.vector.tensor_copy(gram1[:, :], bank[0][:, 0:D + 2])
                            nc.vector.tensor_copy(gram2[:, :], bank[1][0:2, 0:D + 2])

                    @block.scalar
                    def _(act):
                        act.preload_act_table(ACT.Relu)

                        def normed(i, out, x, func, ready):
                            def part(g, s):
                                act.wait_ge(scaled, g + 2 * i + 1)
                                at = (s + 2 * i) % S
                                for j in range(i * G, i * G + G):
                                    last = nc.scalar.activation(out(s, j - i * G), x(s, j - i * G), func,
                                                                bias=nb[:, at, j:j + 1], scale=rs[:, at, j:j + 1])
                                last.then_inc(ready, 1)
                            return part

                        def transposed(g, s):
                            act.wait_ge(attT_ps, g + 1)
                            nc.scalar.activation(attT[:, s, :], bank[s % 2][:, :], ACT.Copy).then_inc(attT_in, 1)

                        def weighted(g, s):
                            act.wait_ge(h3_ready, g + 1)
                            for j in range(G):
                                last = nc.scalar.activation(u[:, s, j, 0:D], r[:, s, j, D:2 * D], ACT.Copy,
                                                            scale=x1[:, s, j, D + M_Q:D + M_Q + 1])
                            last.then_inc(u_ready, 1)
                            act.wait_ge(u_ready, g + 1)
                            act.sem_inc(used, 1)

                        h1 = normed(0, lambda s, j: h[:, s, j, :], lambda s, j: x1[:, s, j, 0:D], ACT.Relu, h_ready)
                        z = normed(1, lambda s, j: h[:, s, j, :], lambda s, j: h[:, s, j, :], ACT.Identity, z_ready)
                        if edges:
                            pipeline(act, n, [(z, 2), (transposed, 0), (h1, 0)], S)
                        else:
                            second_h = normed(2, lambda s, j: h2[:, s, j, :], lambda s, j: x2[:, s, j, :], ACT.Relu, h2_ready)
                            third_h = normed(3, lambda s, j: r[:, s, j, D:2 * D], lambda s, j: r[:, s, j, 0:D], ACT.Relu, h3_ready)
                            pipeline(act, n, [(third_h, 6), (weighted, 6), (second_h, 4), (z, 2), (h1, 0)], S)

                    @block.tensor
                    def _(pe):
                        def outputs(g, s):
                            pe.wait_ge(rows_in[s], slot_count(g, s, n_in))
                            for j in range(G):
                                last = nc.tensor.transpose(bank[s % 2][:, j * P:(j + 1) * P], att[:, s, j, 0:D], ident)
                            last.then_inc(attT_ps, 1)
                            pe.wait_ge(attT_in, g + 1)
                            pe.wait_ge(o_used, g + 1)
                            for j in range(G):
                                last = nc.tensor.matmul(bank[2 + s % 4][:, j * P:(j + 1) * P], attT[:, s, j * P:(j + 1) * P],
                                                        W["Wvo"][:, :], start=True, stop=True)
                            last.then_inc(o_ps, 1)

                        def moments(g, s):
                            pe.wait_ge(u_ready, g + 1)
                            for j in range(G):
                                nc.tensor.matmul(bank[0][:, 0:D + 2], u[:, s, j, 0:D], u[:, s, j, :], start=False,
                                                 stop=False, skip_group_check=True)
                                last = nc.tensor.matmul(bank[1][0:2, 0:D + 2], u[:, s, j, D:D + 2], u[:, s, j, :],
                                                        start=False, stop=False, skip_group_check=True)
                            last.then_inc(gram_done, 1)
                        if not edges:
                            pe.wait_ge(gram_zero, 1)
                        pipeline(pe, n, [(outputs, 0)] if edges else [(moments, 0)], S)

        update(False)
        with phase() as c:
            S8 = 8
            last_norm = 6
            ix = sb("ix", [P, 4, 2 * G], I32, c)
            xs, hs, sums = (sb(n, [P, 4, G, D], F32, c) for n in ("xs", "hs", "sums"))
            xd, hd = (sb(n, [P, S8, G, D], F32, c) for n in ("xd", "hd"))
            efT = sb("efT", [64, 4, G * P], F32, c)
            bc = sb("bc", [P, 4, G * P], I32, c)
            st = sb("st", [P, S8, 3 * G, 6], F32, c)
            tmp = sb("tmp", [P, 2, 3, 3 * G], F32, c)
            rs, nb = (sb(n, [P, S8, 3 * G], F32, c) for n in ("rs", "nb"))
            hsT, hdT = (sb(n, [P, 2, G * P], F32, c) for n in ("hsT", "hdT"))
            hid = sb("hid", [32, 2, G * P], F32, c)
            msg = sb("msg", [P, 2, G * P], F32, c)
            nhid = sb("nhid", [65, 2, G * P], F32, c)
            nmsg = sb("nmsg", [P, 2, G, D], F32, c)
            same, carry = (sb(n, [P, 2, G, P], F32, c) for n in ("same", "carry"))
            r = sb("r", [P, 4, G, RW], F32, c)
            ix_ready, pool_link, summed, summed3, scaled, h_ready, hT_ps, hsT_in, hdT_in, hid_ps, hid_in, msg_ps, msg_in, \
                nhid_ps, nhid_in, nmsg_ps, nmsg_in, same_ready, sum_ps, sum_in, set_up, r_link, x3_ready, h3_ready = (
                    sem(f"mlp_{n}") for n in (
                        "ix_ready", "pool_link", "summed", "summed3", "scaled", "h_ready", "hT_ps", "hsT_in", "hdT_in",
                        "hid_ps", "hid_in", "msg_ps", "msg_in", "nhid_ps", "nhid_in", "nmsg_ps", "nmsg_in", "same_ready",
                        "sum_ps", "sum_in", "set_up", "r_link", "x3_ready", "h3_ready"))
            rows_in = [sem(f"mlp_rows_in{s}") for s in range(S8)]
            ef_in, bc_in, stored = ([sem(f"mlp_{n}{s}") for s in range(4)] for n in ("ef_in", "bc_in", "stored"))
            hs_p, hd_p, hid_p, msg_p, nhid_p, nmsg_p, sum_p = bank[0], bank[1], bank[2], bank[3], bank[4], bank[5], bank[6]

            def count8(g, s, dmas):
                return (g - s) * (2 * dmas) + 16 * dmas

            def count4(g, s):
                return (g - s % 4) * 4 + 16

            with nc.Block() as block:
                @block.gpsimd
                def _(pool):
                    pool.wait_ge(set_up, 1)

                    def src_used(g, s):
                        hold("pool", pool, h_ready, g + 1)

                    def dst_used(g, s):
                        hold("pool", pool, x3_ready, g + 1)

                    def rows(g, s):
                        at = s % 4
                        nc.gpsimd.tensor_copy(ix[:, at, 0:G], table_src[:, bass.ds(g * G, G)])
                        nc.gpsimd.tensor_copy(ix[:, at, G:2 * G], table_dst[:, bass.ds(g * G, G)]).then_inc(ix_ready, 1)
                        hold("pool", pool, ix_ready, g + 1)
                        for j in range(G):
                            gather(pool, xs[:, at, j, :], x2_d, ix[:, at, j:j + 1], rows_in[s])
                            gather(pool, xd[:, s, j, :], x2_d, ix[:, at, G + j:G + j + 1], rows_in[s])

                    def rows_summed(g, s):
                        hold("pool", pool, summed, g + 1)

                    def x3_summed(g, s):
                        hold("pool", pool, summed3, g + 1)

                    def scales(k, s):
                        layer_all(pool, st[:, s, :, :], tmp[:, s % 2, :, :], rs[:, s, :], nb[:, s, :], 3 * G, pool_link,
                                  scaled, k)
                    pipeline(pool, NGE, [(src_used, 4), (dst_used, S8), (rows, 0), (rows_summed, 1),
                                         (x3_summed, 1 + last_norm), (scales, 1, last_norm)], S8)

                @block.sync
                def _(sp):
                    def ef_used(g, s):
                        sp.wait_ge(hid_ps, g + 1)

                    def load_ef(g, s):
                        sp.dma_start(efT[:, s % 4, :], t["edge_attr_T"][:, bass.ds(g * (G * P), G * P)]).then_inc(ef_in[s % 4], 16)

                    def bc_used(g, s):
                        sp.wait_ge(same_ready, g + 1)

                    def load_bc(g, s):
                        sp.dma_start(bc[:, s % 4, :], t["dst"][bass.ds(g * (G * P), G * P)].partition_broadcast(P)).then_inc(
                            bc_in[s % 4], 16)

                    def store(g, s):
                        sp.wait_ge(h3_ready, g + 1)
                        sp.dma_start(rows_of(r_d, g, RW, NN), r[:, s % 4, :, :]).then_inc(stored[s % 4], 16)
                    pipeline(sp, NGE, [(ef_used, 4), (load_ef, 0), (bc_used, 5), (load_bc, 1), (store, 9)], S8)
                    for s in range(4):
                        sp.wait_ge(stored[s], 16 * ((NGE - s + 3) // 4) + 16)

                @block.vector
                def _(dve):
                    nc.vector.memset(nhid[64:65, :, :], 1.0)
                    nc.vector.memset(r[:, :, :, 2 * D:2 * D + 1], 1.0)
                    nc.vector.memset(r[:, :, :, 2 * D + 2:RW], 0.0)
                    nc.vector.memset(st[:, :, :, :], 0.0)
                    nc.vector.memset(sums[:, 3, G - 1, :], 0.0).then_inc(sum_in, 1)
                    dve.wait_ge(sum_in, 1)
                    dve.sem_inc(set_up, 1)
                    for s in range(4):
                        dve.sem_inc(stored[s], 16)

                    def stats(g, s):
                        dve.wait_ge(rows_in[s], count8(g, s, 2 * G))
                        for j in range(G):
                            nc.vector.bn_stats(st[:, s, j, :], xs[:, s % 4, j, :])
                        for j in range(G):
                            last = nc.vector.bn_stats(st[:, s, G + j, :], xd[:, s, j, :])
                        last.then_inc(summed, 1)

                    def hdT_copy(g, s):
                        dve.wait_ge(hT_ps, g + 1)
                        nc.vector.tensor_copy(hdT[:, s % 2, :], hd_p[:, :]).then_inc(hdT_in, 1)

                    def sames(g, s):
                        dve.wait_ge(bc_in[s % 4], count4(g, s))
                        for j in range(G):
                            to = bc[:, s % 4, j * P:(j + 1) * P]
                            nc.vector.tensor_scalar(same[:, s % 2, j, :], to, dstF[:, bass.ds(g * G + (j + 1), 1)], None,
                                                    ALU.is_equal)
                            last = nc.vector.tensor_scalar(carry[:, s % 2, j, :], to, dstF[:, bass.ds(g * G + j, 1)],
                                                           last_row, ALU.is_equal, ALU.mult)
                        last.then_inc(same_ready, 1)

                    def own(g, s):
                        dve.wait_ge(stored[s % 4], count4(g, s))
                        nc.vector.tensor_tensor(r[:, s % 4, :, 0:D], xd[:, s, :, :], hd[:, s, :, :], ALU.add)
                        nc.vector.tensor_copy(r[:, s % 4, :, 2 * D + 1], ginv_dst[:, bass.ds(g * G, G)]).then_inc(r_link, 1)

                    def x3(g, s):
                        dve.wait_ge(r_link, g + 1)
                        dve.wait_ge(sum_in, g * G + G + 1)
                        nc.vector.tensor_tensor(r[:, s % 4, :, 0:D], r[:, s % 4, :, 0:D], sums[:, s % 4, :, :],
                                                ALU.add).then_inc(x3_ready, 1)

                    def stats3(g, s):
                        dve.wait_ge(x3_ready, g + 1)
                        for j in range(G):
                            last = nc.vector.bn_stats(st[:, (s + last_norm) % S8, 2 * G + j, :], r[:, s % 4, j, 0:D])
                        last.then_inc(summed3, 1)
                    pipeline(dve, NGE, [(hdT_copy, 4), (own, 7), (x3, 7), (sames, 5), (stats, 1), (stats3, 7)], S8)

                @block.scalar
                def _(act):
                    act.preload_act_table(ACT.Relu)
                    act.wait_ge(set_up, 1)

                    def relus(g, s):
                        act.wait_ge(scaled, g + 1)
                        for k, x, h in ((0, xs[:, s % 4, :, :], hs[:, s % 4, :, :]), (G, xd[:, s, :, :], hd[:, s, :, :])):
                            for j in range(G):
                                last = nc.scalar.activation(h[:, j, :], x[:, j, :], ACT.Relu, bias=nb[:, s, k + j:k + j + 1],
                                                            scale=rs[:, s, k + j:k + j + 1])
                        last.then_inc(h_ready, 1)

                    def hsT_copy(g, s):
                        act.wait_ge(hT_ps, g + 1)
                        nc.scalar.activation(hsT[:, s % 2, :], hs_p[:, :], ACT.Copy).then_inc(hsT_in, 1)

                    def hidden(g, s):
                        act.wait_ge(hid_ps, g + 1)
                        nc.scalar.activation(hid[:, s % 2, :], hid_p[0:32, :], ACT.Relu, bias=C["be1"][0:32, :]).then_inc(hid_in, 1)

                    def message(g, s):
                        act.wait_ge(msg_ps, g + 1)
                        nc.scalar.activation(msg[:, s % 2, :], msg_p[:, :], ACT.Relu, bias=C["be2"][:, :]).then_inc(msg_in, 1)

                    def nhidden(g, s):
                        act.wait_ge(nhid_ps, g + 1)
                        nc.scalar.activation(nhid[0:64, s % 2, :], nhid_p[0:64, :], ACT.Relu, bias=C["bn1"][0:64, :]).then_inc(nhid_in, 1)

                    def nmessage(g, s):
                        act.wait_ge(nmsg_ps, g + 1)
                        nc.scalar.activation(nmsg[:, s % 2, :, :].rearrange("p j f -> p (j f)"), nmsg_p[:, :],
                                             ACT.Relu).then_inc(nmsg_in, 1)

                    def total(j):
                        def part(g, s):
                            act.wait_ge(sum_ps, g * G + j + 1)
                            nc.scalar.activation(sums[:, s % 4, j, :], sum_p[:, 0:D], ACT.Copy).then_inc(sum_in, 1)
                        return part

                    def h3(g, s):
                        act.wait_ge(scaled, g + last_norm + 1)
                        at = (s + last_norm) % S8
                        for j in range(G):
                            last = nc.scalar.activation(r[:, s % 4, j, D:2 * D], r[:, s % 4, j, 0:D], ACT.Relu,
                                                        bias=nb[:, at, 2 * G + j:2 * G + j + 1],
                                                        scale=rs[:, at, 2 * G + j:2 * G + j + 1])
                        last.then_inc(h3_ready, 1)
                    pipeline(act, NGE, [(hsT_copy, 4), (total(0), 6), (h3, 8), (nhidden, 5), (total(1), 6), (hidden, 4),
                                        (total(2), 6), (relus, 2), (nmessage, 5), (message, 4), (total(3), 6)], S8)

                @block.tensor
                def _(pe):
                    pe.wait_ge(set_up, 1)

                    def transposes(g, s):
                        pe.wait_ge(h_ready, g + 1)
                        for x, p in ((hs[:, s % 4, :, :], hs_p), (hd[:, s, :, :], hd_p)):
                            for j in range(G):
                                last = nc.tensor.transpose(p[:, j * P:(j + 1) * P], x[:, j, :], ident)
                        last.then_inc(hT_ps, 1)

                    def hidden(g, s):
                        pe.wait_ge(hsT_in, g + 1)
                        nc.tensor.matmul(hid_p[0:32, :], W["We1a"][:, 0:32], hsT[:, s % 2, :], start=True, stop=False)
                        pe.wait_ge(hdT_in, g + 1)
                        nc.tensor.matmul(hid_p[0:32, :], W["We1b"][:, 0:32], hdT[:, s % 2, :], start=False, stop=False)
                        hold("pe", pe, ef_in[s % 4], count4(g, s))
                        nc.tensor.matmul(hid_p[0:32, :], W["We1c"][0:64, 0:32], efT[:, s % 4, :], start=False,
                                         stop=True).then_inc(hid_ps, 1)

                    def message(g, s):
                        pe.wait_ge(hid_in, g + 1)
                        nc.tensor.matmul(msg_p[:, :], W["We2"][0:32, :], hid[:, s % 2, :], start=True, stop=True).then_inc(msg_ps, 1)

                    def nhidden(g, s):
                        nc.tensor.matmul(nhid_p[0:64, :], W["Wn1a"][:, 0:64], hdT[:, s % 2, :], start=True, stop=False)
                        pe.wait_ge(msg_in, g + 1)
                        nc.tensor.matmul(nhid_p[0:64, :], W["Wn1b"][:, 0:64], msg[:, s % 2, :], start=False,
                                         stop=True).then_inc(nhid_ps, 1)

                    def nmessage(g, s):
                        pe.wait_ge(nhid_in, g + 1)
                        for j in range(G):
                            last = nc.tensor.matmul(nmsg_p[:, j * P:(j + 1) * P], nhid[:, s % 2, j * P:(j + 1) * P],
                                                    W["Wn2"][0:65, :], start=True, stop=True)
                        last.then_inc(nmsg_ps, 1)

                    def total(j):
                        def part(g, s):
                            if j == 0:
                                pe.wait_ge(same_ready, g + 1)
                                pe.wait_ge(nmsg_in, g + 1)
                            before = sums[:, s % 4, j - 1, :] if j else sums[:, (s - 1) % 4, G - 1, :]
                            pe.wait_ge(sum_in, g * G + j + 1)
                            nc.tensor.matmul(sum_p[:, 0:D], same[:, s % 2, j, :], nmsg[:, s % 2, j, :], start=True, stop=False)
                            nc.tensor.matmul(sum_p[:, 0:D], carry[:, s % 2, j, :], before, start=False, stop=True).then_inc(sum_ps, 1)
                        return part
                    pipeline(pe, NGE, [(total(0), 6), (nhidden, 5), (total(1), 6), (hidden, 4), (total(2), 6), (nmessage, 5),
                                       (message, 4), (total(3), 6), (transposes, 3)], S8)

        with phase() as c:
            S8 = 8
            ix = sb("ix", [P, S8, 2 * G], I32, c)
            rs_, rd = (sb(n, [P, S8, G, RW], F32, c) for n in ("rs_", "rd"))
            bc = sb("bc", [P, 4, G * P], I32, c)
            wt, rg, q = (sb(n, [P, S8, G], F32, c) for n in ("wt", "rg", "q"))
            same, carry = (sb(n, [P, 4, G, P], F32, c) for n in ("same", "carry"))
            sums = sb("sums", [P, 4, G, TW], F32, c)
            u = sb("u", [P, 4, G, D + 2], F32, c)
            ix_ready, wt_link, q_link, same_ready, sum_ps, sum_in, w_ready, u_ready, gram_done, gram_zero = (
                sem(f"gc_{n}") for n in ("ix_ready", "wt_link", "q_link", "same_ready", "sum_ps", "sum_in", "w_ready",
                                         "u_ready", "gram_done", "gram_zero"))
            src_in, dst_in, scattered = ([sem(f"gc_{n}{s}") for s in range(S8)] for n in ("src_in", "dst_in", "scattered"))
            bc_in = [sem(f"gc_bc_in{s}") for s in range(4)]
            sum_p = bank[4]

            def count8(g, s, dmas):
                return (g - s) * (2 * dmas) + 16 * dmas

            with nc.Block() as block:
                @block.gpsimd
                def _(pool):
                    def written(g, s):
                        hold("pool", pool, scattered[s], count8(g, s, G))
                        hold("pool", pool, u_ready, g + 1)

                    def rows(g, s):
                        nc.gpsimd.tensor_copy(ix[:, s, 0:G], table_src[:, bass.ds(g * G, G)])
                        nc.gpsimd.tensor_copy(ix[:, s, G:2 * G], out_row[:, bass.ds(g * G, G)]).then_inc(ix_ready, 1)
                        hold("pool", pool, ix_ready, g + 1)
                        for j in range(G):
                            gather(pool, rs_[:, s, j, :], r_d, ix[:, s, j:j + 1], src_in[s])

                    def scatter(g, s):
                        hold("pool", pool, w_ready, g + 1)
                        for j in range(G):
                            pool.indirect_dma_start(out=r_d, out_offset=bass.IndirectOffsetOnAxis(ap=ix[:, s, G + j:G + j + 1], axis=0),
                                                    in_=rd[:, s, j, :], in_offset=None).then_inc(scattered[s], 16)
                    pipeline(pool, NGE, [(written, S8), (rows, 0), (scatter, 5)], S8)

                @block.sync
                def _(sp):
                    def load(g, s):
                        sp.wait_ge(ix_ready, g + 1)
                        sp.dma_start(rd[:, s, :, :], rows_of(r_d, g, RW, NN)).then_inc(dst_in[s], 16)

                    def bc_used(g, s):
                        sp.wait_ge(same_ready, g + 1)

                    def load_bc(g, s):
                        sp.dma_start(bc[:, s % 4, :], t["dst"][bass.ds(g * (G * P), G * P)].partition_broadcast(P)).then_inc(
                            bc_in[s % 4], 16)
                    pipeline(sp, NGE, [(bc_used, 4), (load_bc, 0), (load, 0)], S8)

                @block.vector
                def _(dve):
                    nc.vector.memset(bank[0][:, :], 0.0)
                    nc.vector.memset(bank[1][:, :], 0.0).then_inc(gram_zero, 1)
                    nc.vector.memset(sums[:, 3, G - 1, :], 0.0).then_inc(sum_in, 1)
                    dve.sem_inc(gram_done, 4)

                    def weights(g, s):
                        dve.wait_ge(src_in[s], count8(g, s, G))
                        nc.vector.tensor_tensor(wt[:, s, :], rs_[:, s, :, 2 * D + 1], ew[:, bass.ds(g * G, G)], ALU.mult)
                        dve.wait_ge(dst_in[s], count8(g, s, 1))
                        nc.vector.reciprocal(rg[:, s, :], rd[:, s, :, 2 * D + 1])
                        nc.vector.tensor_tensor(q[:, s, :], rd[:, s, :, 2 * D + 1], rd[:, s, :, 2 * D + 1],
                                                ALU.mult).then_inc(wt_link, 1)

                    def ends(g, s):
                        dve.wait_ge(wt_link, g + 1)
                        nc.vector.tensor_tensor(q[:, s, :], q[:, s, :], seg_end[:, bass.ds(g * G, G)], ALU.mult).then_inc(q_link, 1)

                    def sames(g, s):
                        dve.wait_ge(bc_in[s % 4], (g - s % 4) * 4 + 16)
                        for j in range(G):
                            to = bc[:, s % 4, j * P:(j + 1) * P]
                            nc.vector.tensor_scalar(same[:, s % 4, j, :], to, dstF[:, bass.ds(g * G + (j + 1), 1)],
                                                    wt[:, s, j:j + 1], ALU.is_equal, ALU.mult)
                            last = nc.vector.tensor_scalar(carry[:, s % 4, j, :], to, dstF[:, bass.ds(g * G + j, 1)],
                                                           last_row, ALU.is_equal, ALU.mult)
                        last.then_inc(same_ready, 1)

                    def own(g, s):
                        hold("dve", dve, gram_done, g + 1)
                        nc.vector.tensor_copy(u[:, s % 4, :, D + 1], seg_end[:, bass.ds(g * G, G)])
                        dve.wait_ge(sum_in, g * G + G + 1)
                        dve.wait_ge(q_link, g + 1)
                        for j in range(G):
                            last = nc.vector.scalar_tensor_tensor(
                                out=rd[:, s, j, D:2 * D + 1], in0=sums[:, s % 4, j, 0:D + 1], scalar=rg[:, s, j:j + 1],
                                in1=rd[:, s, j, D:2 * D + 1], op0=ALU.mult, op1=ALU.add)
                        last.then_inc(w_ready, 1)
                    pipeline(dve, NGE, [(weights, 1), (own, 4), (ends, 1), (sames, 1)], S8)
                    dve.wait_ge(gram_done, NGE + 4)
                    nc.vector.tensor_tensor(gram1[:, :], gram1[:, :], bank[0][:, 0:D + 2], ALU.add)
                    nc.vector.tensor_tensor(gram2[:, :], gram2[:, :], bank[1][0:2, 0:D + 2], ALU.add)

                @block.scalar
                def _(act):
                    act.preload_act_table(ACT.Copy)

                    def total(j):
                        def part(g, s):
                            act.wait_ge(sum_ps, g * G + j + 1)
                            nc.scalar.activation(sums[:, s % 4, j, 0:D + 1], sum_p[:, 0:D + 1], ACT.Copy).then_inc(sum_in, 1)
                        return part

                    def weighted(j):
                        def part(g, s):
                            act.wait_ge(w_ready, g + 1)
                            ins = nc.scalar.activation(u[:, s % 4, j, 0:D + 1], rd[:, s, j, D:2 * D + 1], ACT.Copy,
                                                       scale=q[:, s, j:j + 1])
                            if j == G - 1:
                                ins.then_inc(u_ready, 1)
                        return part
                    pipeline(act, NGE, [p for j in range(G) for p in ((total(j), 2), (weighted(j), 5))], S8)

                @block.tensor
                def _(pe):
                    pe.wait_ge(gram_zero, 1)

                    def total(j):
                        def part(g, s):
                            if j == 0:
                                pe.wait_ge(same_ready, g + 1)
                            before = sums[:, s % 4, j - 1, 0:D + 1] if j else sums[:, (s - 1) % 4, G - 1, 0:D + 1]
                            pe.wait_ge(sum_in, g * G + j + 1)
                            nc.tensor.matmul(sum_p[:, 0:D + 1], same[:, s % 4, j, :], rs_[:, s, j, D:2 * D + 1], start=True, stop=False)
                            nc.tensor.matmul(sum_p[:, 0:D + 1], carry[:, s % 4, j, :], before, start=False,
                                             stop=True).then_inc(sum_ps, 1)
                        return part

                    def moments(j):
                        def part(g, s):
                            if j == 0:
                                pe.wait_ge(u_ready, g + 1)
                            v = u[:, s % 4, j, :]
                            nc.tensor.matmul(bank[0][:, 0:D + 2], v[:, 0:D], v, start=False, stop=False, skip_group_check=True)
                            last = nc.tensor.matmul(bank[1][0:2, 0:D + 2], v[:, D:D + 2], v, start=False, stop=False,
                                                    skip_group_check=True)
                            if j == G - 1:
                                last.then_inc(gram_done, 1)
                        return part
                    pipeline(pe, NGE, [p for j in range(G) for p in ((total(j), 2), (moments(j), 6))], S8)

        Wbn = sb("Wbn", [P, D])
        bbn = sb("bbn", [P, D])
        tbn = sb("tbn", [P, D])
        with phase() as c:
            y1, z1, var_, sc, half = (sb(n, [P, D], F32, c) for n in ("y1", "z1", "var_", "sc", "half"))
            y2, z2 = (sb(n, [2, D], F32, c) for n in ("y2", "z2"))
            mean = sb("mean", [P, D], F32, c)
            y_ps, z_ready, e_ps, link, var_ready, pow_done = (sem(f"bn_{n}") for n in ("y_ps", "z_ready", "e_ps", "link", "var_ready", "pow_done"))
            with nc.Block() as block:
                @block.tensor
                def _(pe):
                    nc.tensor.matmul(bank[0][:, 0:D], gram1[:, 0:D], W["W3"][:, :], start=True, stop=False)
                    nc.tensor.matmul(bank[0][:, 0:D], gram2[:, 0:D], wb[:, :], start=False, stop=True)
                    nc.tensor.matmul(bank[1][0:2, 0:D], gram1[:, D:D + 2], W["W3"][:, :], start=True, stop=False)
                    nc.tensor.matmul(bank[1][0:2, 0:D], gram2[:, D:D + 2], wb[:, :], start=False, stop=True).then_inc(y_ps, 1)
                    pe.wait_ge(z_ready, 1)
                    nc.tensor.matmul(bank[2][:, 0:D], ones, z1[:, :], start=True, stop=False)
                    nc.tensor.matmul(bank[2][:, 0:D], ones[0:2, :], z2[:, :], start=False, stop=True)
                    nc.tensor.matmul(bank[3][:, 0:D], K[0:2, K_ROW1:K_ROW1 + P], y2[:, :], start=True, stop=True).then_inc(e_ps, 1)

                @block.gpsimd
                def _(pool):
                    nc.gpsimd.memset(half[:, :], -0.5).then_inc(pow_done, 1)
                    pool.wait_ge(pow_done, 1)
                    pool.wait_ge(var_ready, 1)
                    nc.gpsimd.tensor_tensor(sc[:, :], var_[:, :], half[:, :], ALU.pow).then_inc(pow_done, 1)

                @block.vector
                def _(dve):
                    k = [0]

                    def chain(ins):
                        k[0] += 1
                        ins.then_inc(link, 1)
                        dve.wait_ge(link, k[0])

                    dve.wait_ge(y_ps, 1)
                    chain(nc.vector.tensor_tensor(z1[:, :], W["W3"][:, :], bank[0][:, 0:D], ALU.mult))
                    chain(nc.vector.tensor_copy(y2[:, :], bank[1][0:2, 0:D]))
                    nc.vector.tensor_tensor(z2[:, :], wb[:, :], y2[:, :], ALU.mult).then_inc(z_ready, 1)
                    dve.wait_ge(e_ps, 1)
                    chain(nc.vector.tensor_scalar(mean[:, :], bank[3][:, 0:D], 1.0 / N, None, ALU.mult))
                    chain(nc.vector.tensor_tensor(z1[:, :], mean[:, :], mean[:, :], ALU.mult))
                    chain(nc.vector.tensor_scalar(y1[:, :], bank[2][:, 0:D], 1.0 / N, EPS, ALU.mult, ALU.add))
                    chain(nc.vector.tensor_tensor(y1[:, :], y1[:, :], z1[:, :], ALU.subtract))
                    nc.vector.tensor_scalar(var_[:, :], y1[:, :], EPS, None, ALU.max).then_inc(var_ready, 1)
                    dve.wait_ge(pow_done, 2)
                    chain(nc.vector.tensor_tensor(sc[:, :], sc[:, :], R["bgamma"][:, :], ALU.mult))
                    chain(nc.vector.tensor_tensor(Wbn[:, :], W["W3"][:, :], sc[:, :], ALU.mult))
                    chain(nc.vector.tensor_tensor(bbn[:, :], R["b3"][:, :], sc[:, :], ALU.mult))
                    chain(nc.vector.tensor_tensor(z1[:, :], mean[:, :], sc[:, :], ALU.mult))
                    chain(nc.vector.tensor_tensor(tbn[:, :], R["bbeta"][:, :], z1[:, :], ALU.subtract))

        with phase() as c:
            r = sb("r", [P, S, G, RW], F32, c)
            wT = sb("wT", [P, S, G * P], F32, c)
            y = sb("y", [P, S, G, D], F32, c)
            g2 = sb("g2", [P, S, G], F32, c)
            wT_ps, wT_in, y_ps, y_used, link, link2, y_ready = (sem(f"out_{n}") for n in (
                "wT_ps", "wT_in", "y_ps", "y_used", "link", "link2", "y_ready"))
            rows_in = [sem(f"out_rows_in{s}") for s in range(S)]
            stored = [sem(f"out_stored{s}") for s in range(S)]

            with nc.Block() as block:
                @block.sync
                def _(sp):
                    for s in range(S):
                        sp.sem_inc(stored[s], 16)

                    def load(g, s):
                        sp.wait_ge(stored[s], slot_count(g, s, 1))
                        sp.dma_start(r[:, s, :, :], node_rows_of(r_d, g, RW)).then_inc(rows_in[s], 16)
                    pipeline(sp, NGN, [(load, 0)], S)

                @block.tensor
                def _(pe):
                    def transposes(g, s):
                        pe.wait_ge(rows_in[s], slot_count(g, s, 1))
                        for j in range(G):
                            last = nc.tensor.transpose(bank[s % 2][:, j * P:(j + 1) * P], r[:, s, j, D:2 * D], ident)
                        last.then_inc(wT_ps, 1)

                    def products(g, s):
                        pe.wait_ge(wT_in, g + 1)
                        pe.wait_ge(y_used, g + 1)
                        for j in range(G):
                            last = nc.tensor.matmul(bank[2 + s % 2][:, j * P:(j + 1) * P], wT[:, s, j * P:(j + 1) * P],
                                                    Wbn[:, :], start=True, stop=True)
                        last.then_inc(y_ps, 1)
                    pipeline(pe, NGN, [(transposes, 0), (products, 1)], S)

                @block.scalar
                def _(act):
                    act.preload_act_table(ACT.Copy)

                    def to_sbuf(g, s):
                        act.wait_ge(wT_ps, g + 1)
                        nc.scalar.activation(wT[:, s, :], bank[s % 2][:, :], ACT.Copy).then_inc(wT_in, 1)

                    def store(g, s):
                        act.wait_ge(y_ready, g + 1)
                        act.dma_start(node_rows_of(t["out"], g, D), y[:, s, :, :]).then_inc(stored[s], 16)
                    pipeline(act, NGN, [(to_sbuf, 0), (store, 2)], S)
                    for s in range(S):
                        act.wait_ge(stored[s], 16 * ((NGN - s + S - 1) // S) + 16)

                @block.vector
                def _(dve):
                    dve.sem_inc(y_used, 2)

                    def part(g, s):
                        dve.wait_ge(y_ps, g + 1)
                        for j in range(G):
                            last = nc.vector.scalar_tensor_tensor(
                                out=y[:, s, j, :], in0=bbn[:, :], scalar=r[:, s, j, 2 * D:2 * D + 1],
                                in1=bank[2 + s % 2][:, j * P:(j + 1) * P], op0=ALU.mult, op1=ALU.add)
                        last.then_inc(y_used, 1)
                        nc.vector.tensor_tensor(g2[:, s, :], r[:, s, :, 2 * D + 1], r[:, s, :, 2 * D + 1], ALU.mult).then_inc(link, 1)
                        dve.wait_ge(link, g + 1)
                        for j in range(G):
                            last = nc.vector.scalar_tensor_tensor(out=y[:, s, j, :], in0=y[:, s, j, :], scalar=g2[:, s, j:j + 1],
                                                                  in1=tbn[:, :], op0=ALU.mult, op1=ALU.add)
                        last.then_inc(link2, 1)
                        dve.wait_ge(link2, g + 1)
                        nc.vector.scalar_tensor_tensor(out=y[:, s, :, :], in0=y[:, s, :, :], scalar=0.0, in1=r[:, s, :, 0:D],
                                                       op0=ALU.max, op1=ALU.add).then_inc(y_ready, 1)
                    pipeline(dve, NGN, [(part, 0)], S)
    return


_FLOATS = ["x", "edge_attr_64", "L0_gnn_W1", "L0_gnn_b1", "L0_gnn_W2", "L0_gnn_b2", "L1_gnn_Wqk", "L1_gnn_bqk",
           "L1_gnn_Wv", "L1_gnn_bv", "L1_gnn_Wo", "L1_gnn_bo", "L1_gnn_gamma", "L1_gnn_beta", "L2_gnn_We1",
           "L2_gnn_be1", "L2_gnn_We2", "L2_gnn_be2", "L2_gnn_Wn1", "L2_gnn_bn1", "L2_gnn_Wn2", "L2_gnn_bn2",
           "L3_gnn_W", "L3_gnn_b", "L3_gnn_gamma", "L3_gnn_beta"]
DEBUG = False


def constants():
    import numpy as np

    k = np.zeros((P, K_COLS), np.float32)
    p = np.arange(P)
    k[:, K_ID:K_ID + P] = np.eye(P)
    k[:, K_AFTER:K_AFTER + P] = p[None, :] > p[:, None]
    k[:, K_IOTA:K_IOTA + NLO] = np.arange(NLO)
    for b in range(2):
        k[:HB, K_NODE + b * NLO:K_NODE + (b + 1) * NLO] = (b * HB + np.arange(HB))[:, None] * NLO + np.arange(NLO)
    k[:, K_EDGE:K_EDGE + NT] = np.arange(NT) * P + p[:, None]
    k[P - 1, K_LAST] = 1
    k[:, K_DUMP] = NN + p
    k[:, K_ONE:K_ONE + P] = 1
    k[1, K_ROW1:K_ROW1 + P] = 1
    return k


def kernel(**inputs):
    import numpy as np
    import concourse.bacc as bacc
    from concourse.bass_utils import run_bass_kernel_spmd

    def padded(v, rows, fill):
        v = np.asarray(v)
        out = np.full((rows,) + v.shape[1:], fill, v.dtype)
        out[:len(v)] = v
        return out

    arrays = {n: np.ascontiguousarray(np.asarray(inputs[n])) for n in _FLOATS}
    arrays["x"] = padded(arrays["x"], NN, 0)
    arrays["edge_attr_T"] = np.ascontiguousarray(padded(arrays.pop("edge_attr_64"), EP, 0).T)
    arrays["src"] = padded(inputs["src"], EP, N)
    arrays["dst"] = padded(inputs["dst"], EP, N)
    arrays["next_dst"] = padded(arrays["dst"][1:], EP, N + 1)
    arrays["edge_weight"] = padded(inputs["edge_weight"], EP, 0)
    arrays["consts"] = constants()
    nc = bacc.Bacc("TRN2", target_bir_lowering=False, num_devices=1)
    t = {n: nc.dram_tensor(n, a.shape, mybir.dt.from_np(a.dtype), kind="ExternalInput").ap() for n, a in arrays.items()}
    t["out"] = nc.dram_tensor("out", (NN, D), F32, kind="ExternalOutput").ap()
    build(nc, t, DEBUG)
    r = run_bass_kernel_spmd(nc, [arrays], core_ids=[0])
    return r.results[0]["out"][:N]
```

```python
from contextlib import ExitStack, contextmanager

import concourse.bass as bass
from concourse import mybir

F32 = mybir.dt.float32
BF16 = mybir.dt.bfloat16
I32 = mybir.dt.int32
ALU = mybir.AluOpType
ACT = mybir.ActivationFunctionType
AX_X = mybir.AxisListType.X

P = 128
D = 128
N = 50000
E = 25000
HEDGES = 10000
G = 4
NT = 200
EP = NT * P
NGE = NT // G
LOW_STEP = 2 * G * P
NHI, NLO = 196, 256
HB = NHI // 2
NN = NHI * NLO
NGN = NN // (P * G)
XW = 136
TW = 132
RW = 260
EPS = 1e-5
M_DINV, M_CHIGH, M_GINV, M_INDEX, M_BINV, M_GINV2, M_BARE, M_Q = range(8)
K_ID = 0
K_AFTER = K_ID + P
K_IOTA = K_AFTER + P
K_NODE = K_IOTA + NLO
K_EDGE = K_NODE + 2 * NLO
K_LAST = K_EDGE + NT
K_DUMP = K_LAST + 1
K_ONE = K_DUMP + 1
K_ROW1 = K_ONE + P
K_COLS = K_ROW1 + P


def pipeline(eng, n, parts, slots=2):
    parts = [(p + (0,))[:3] for p in parts]
    deep = max(lag for _, lag, _ in parts)
    looped = (n - deep) // slots * slots

    def step(k):
        for part, lag, more in parts:
            if 0 <= k - lag < n + more:
                part(k - lag, (k - lag) % slots)

    for k in range(deep):
        step(k)
    with eng.Fori(0, looped - slots + 1, slots) as i:
        for k in range(deep, deep + slots):
            for part, lag, _ in parts:
                part(i + (k - lag), (k - lag) % slots)
    for k in range(deep + looped, max(n + lag + more for _, lag, more in parts)):
        step(k)


def bounded(eng, count, *parts):
    with eng.Fori(0, count - 1, 2) as i:
        for part in parts:
            part(i, 0)
            part(i + 1, 1)


def build(nc, t, debug):
    root = ExitStack()
    with root:
        def dram(name, shape):
            return nc.dram_tensor(name, shape, F32, kind="ExternalOutput" if debug else "Internal").ap()

        meta_d = dram("meta_d", (NN, 8))
        sum1_d = dram("sum1_d", (NN + P, D))
        x1_d = dram("x1_d", (NN + P, XW))
        he_d = dram("he_d", (EP + P, D))
        x2_d = dram("x2_d", (NN + EP, D))
        r_d = dram("r_d", (NN + EP, RW))

        stage = [0]

        def sb(name, shape, dt=F32, ctx=root):
            return ctx.enter_context(nc.sbuf_tensor(f"{name}_{stage[0]}", shape, dt))

        def sem(name):
            return nc.alloc_semaphore(f"{name}_{stage[0]}")

        @contextmanager
        def phase():
            stage[0] += 1
            with nc.cleanup_on_exit(), ExitStack() as c:
                yield c

        K = sb("K", [P, K_COLS])
        ident = K[:, K_ID:K_ID + P]
        after = K[:, K_AFTER:K_AFTER + P]
        last_row = K[:, K_LAST:K_LAST + 1]
        dump_row = K[:, K_DUMP:K_DUMP + 1]
        edge_no = K[:, K_EDGE:K_EDGE + NT]
        ones = K[:, K_ONE:K_ONE + P]
        srcF = sb("srcF", [P, NT])
        dstF = sb("dstF", [P, NT + 1])
        ew = sb("ew", [P, NT])
        srcI = sb("srcI", [P, NT], I32)
        dstI = sb("dstI", [P, NT], I32)
        low = sb("low", [P, NT])
        seg_end = sb("seg_end", [P, NT])
        out_row = sb("out_row", [P, NT], I32)
        he_index = sb("he_index", [P, NT], I32)
        meta_src = sb("meta_src", [P, NT, 8])
        meta_dst = sb("meta_dst", [P, NT, 8])
        table_src = sb("table_src", [P, NT], I32)
        table_dst = sb("table_dst", [P, NT], I32)
        ginv_dst = sb("ginv_dst", [P, NT])
        he_last = [sb("he_last0", [P, D]), sb("he_last1", [P, D])]
        low_groups = sb("low_groups", [P, 1], I32)
        minus_half = sb("minus_half", [P, 16])
        W = {n: sb("w_" + n, [P, D]) for n in
             ("W1", "W2", "Wvo", "We1a", "We1b", "We1c", "We2", "Wn1a", "Wn1b", "Wn2", "W3")}
        Wscore = sb("Wscore", [P, D + 1])
        urow = sb("urow", [1, 2 * TW])
        R = {n: sb("r_" + n, [P, D]) for n in ("b1", "b2", "bo", "bvo", "gamma", "beta", "bgamma", "bbeta", "b3")}
        C = {n: sb("c_" + n, [P, 1]) for n in ("be1", "be2", "bn1", "bqk", "bv")}
        wb = sb("wb", [2, D])
        gram1 = sb("gram1", [P, D + 2])
        gram2 = sb("gram2", [2, D + 2])
        bank = [root.enter_context(nc.psum_tensor(f"bank{i}", [P, 512], F32)) for i in range(8)]
        passed = {n: sem("passed_" + n) for n in ("pool", "dve", "act", "pe", "sp")}

        x1_meta = sem("x1_meta")

        def hold(name, eng, s, value):
            eng.wait_ge(s, value)
            eng.sem_inc(passed[name], 1)

        def rows_of(table, g, width, first=0):
            return table[bass.ds(g * (G * P) + first, G * P), 0:width].rearrange("(j p) f -> p j f", p=P)

        def node_rows_of(table, g, width):
            return table[bass.ds(g * (G * P), G * P), 0:width].rearrange("(p j) f -> p j f", p=P)

        with phase() as c:
            rows = sb("rows", [NT // 2, 3, 2, P], I32, c)
            rowsF = sb("rowsF", [NT // 2, 4, 2, P], F32, c)
            zeros = sb("zeros", [P, 28 * D], F32, c)
            wq, wv, wo, wqT, wvT = (sb(f"ld_{n}", [P, D], F32, c) for n in ("q", "v", "o", "qT", "vT"))
            tmpF, nextF, high = (sb(n, [P, NT], F32, c) for n in ("tmpF", "nextF", "high"))
            tmpI = sb("tmpI", [P, NT], I32, c)
            split = {n: sb("sp_" + n, [P, NT], F32, c) for n in ("hs", "ls", "hd", "ld")}
            cnt = sb("cnt", [P, 1], F32, c)
            iota = sb("iota_b", [P, NLO], BF16, c)
            hot_s = sb("hot_s", [P, 2, NHI + 2 * NLO], BF16, c)
            hot_d = sb("hot_d", [P, 2, NHI + NLO], BF16, c)
            deg = {n: sb("deg_" + n, [HB, 2 * NLO], F32, c) for n in ("s", "h", "d")}
            a = {n: sb("a_" + n, [HB, 2 * NLO], F32, c) for n in ("x", "y", "z", "w", "root")}
            totals = sb("totals", [HB, 2], F32, c)
            xt = sb("xt", [P, 4, 8, D], F32, c)
            chunk = 8 * P
            chunks = NN // chunk
            xt_added = sem("xt_added")
            xt_in, xt_out = ([sem(f"{n}{s}") for s in range(4)] for n in ("xt_in", "xt_out"))

            def chunk_of(table, g):
                return table[bass.ds(g * chunk, chunk), 0:D].rearrange("(p j) f -> p j f", p=P)
            meta = sb("meta", [HB, 2 * NLO, 8], F32, c)
            loads, zeroed, zero_ready, vec, columns_ps, columns_in, weights_ps, hot_ready, hot_used, \
                counts_ps, deg_ready, root_ready, totals_ready, offsets_ps, meta_ready, meta_out, act_link = (sem(n) for n in (
                    "loads", "zeroed", "zero_ready", "vec", "columns_ps", "columns_in", "weights_ps", "hot_ready",
                    "hot_used", "counts_ps", "deg_ready", "root_ready", "totals_ready", "offsets_ps", "meta_ready",
                    "meta_out", "act_link"))

            def as_col(ap):
                return ap.rearrange("(n a) -> n a", a=1)

            plan = [(K[:, :], t["consts"])]
            plan += [(rows[:, k, :, :], t[n].rearrange("(a r p) -> r a p", a=2, p=P)) for k, n in
                     enumerate(("src", "dst", "next_dst"))]
            plan += [(rowsF[:, 3, :, :], t["edge_weight"].rearrange("(a r p) -> r a p", a=2, p=P))]
            plan += [(wq[:, :], t["L1_gnn_Wqk"]), (wv[:, :], t["L1_gnn_Wv"]), (wo[:, :], t["L1_gnn_Wo"]),
                     (W["W1"][:, :], t["L0_gnn_W1"]), (W["W2"][:, :], t["L0_gnn_W2"]), (W["W3"][:, :], t["L3_gnn_W"]),
                     (W["We1a"][:, 0:32], t["L2_gnn_We1"][0:D, :]), (W["We1b"][:, 0:32], t["L2_gnn_We1"][D:2 * D, :]),
                     (W["We1c"][0:64, 0:32], t["L2_gnn_We1"][2 * D:2 * D + 64, :]), (W["We2"][0:32, :], t["L2_gnn_We2"]),
                     (W["Wn1a"][:, 0:64], t["L2_gnn_Wn1"][0:D, :]), (W["Wn1b"][:, 0:64], t["L2_gnn_Wn1"][D:2 * D, :]),
                     (W["Wn2"][0:64, :], t["L2_gnn_Wn2"]),
                     (W["Wn2"][64:65, :], t["L2_gnn_bn2"].rearrange("(a n) -> a n", a=1)),
                     (C["be1"][0:32, :], as_col(t["L2_gnn_be1"])), (C["be2"][:, :], as_col(t["L2_gnn_be2"])),
                     (C["bn1"][0:64, :], as_col(t["L2_gnn_bn1"])), (C["bqk"][:, :], as_col(t["L1_gnn_bqk"])),
                     (C["bv"][:, :], as_col(t["L1_gnn_bv"])),
                     (wb[0:1, :], t["L3_gnn_b"].rearrange("(a n) -> a n", a=1)),
                     (wb[1:2, :], t["consts"][0:1, K_ROW1:K_ROW1 + P])]
            plan += [(R[dst][:, :], t[n].partition_broadcast(P)) for dst, n in
                     (("b1", "L0_gnn_b1"), ("b2", "L0_gnn_b2"), ("bo", "L1_gnn_bo"), ("gamma", "L1_gnn_gamma"),
                      ("beta", "L1_gnn_beta"), ("bgamma", "L3_gnn_gamma"), ("bbeta", "L3_gnn_beta"), ("b3", "L3_gnn_b"))]
            count = [0]

            with nc.Block() as block:
                @block.sync
                def _(sp):
                    for dst, src in plan:
                        sp.dma_start(dst, src).then_inc(loads, 16)
                    sp.wait_ge(zero_ready, 1)
                    for k in range(NN // (P * 28)):
                        sp.dma_start(sum1_d[k * P * 28:(k + 1) * P * 28, :].rearrange("(p r) f -> p (r f)", p=P),
                                     zeros[:, :]).then_inc(zeroed, 16)
                    for k in range(EP // (P * 25)):
                        sp.dma_start(he_d[k * P * 25:(k + 1) * P * 25, :].rearrange("(p r) f -> p (r f)", p=P),
                                     zeros[:, 0:25 * D]).then_inc(zeroed, 16)
                    for part in (sum1_d[NN:NN + P, :], he_d[EP:EP + P, :]):
                        sp.dma_start(part, zeros[:, 0:D]).then_inc(zeroed, 16)
                    sp.dma_start(x1_d[NN:NN + P, :], zeros[:, 0:XW]).then_inc(zeroed, 16)

                    def load(g, s):
                        sp.wait_ge(xt_out[s], g * 4 - 4 * s + 16)
                        sp.dma_start(xt[:, s, :, :], chunk_of(t["x"], g)).then_inc(xt_in[s], 16)
                    for s in range(4):
                        sp.sem_inc(xt_out[s], 16)
                    pipeline(sp, chunks, [(load, 0)], 4)
                    sp.wait_ge(meta_ready, 1)
                    sp.dma_start(meta_d.rearrange("(a p l) m -> p a (l m)", a=2, p=HB),
                                 meta[:, :, :].rearrange("p (a l) m -> p a (l m)", a=2)).then_inc(meta_out, 16)
                    sp.wait_ge(meta_out, 16)
                    sp.dma_start(x1_d[0:NN, D:XW], meta_d).then_inc(x1_meta, 16)
                    sp.wait_ge(zeroed, 16 * (NN // (P * 28) + EP // (P * 25) + 3))

                @block.gpsimd
                def _(pool):
                    nc.gpsimd.memset(zeros[:, :], 0.0).then_inc(zero_ready, 1)
                    nc.gpsimd.memset(minus_half[:, :], -0.5)
                    pool.wait_ge(loads, 16 * len(plan))

                    def add(g, s):
                        hold("pool", pool, xt_in[s], g * 4 - 4 * s + 16)
                        nc.gpsimd.tensor_tensor(xt[:, s, :, :], xt[:, s, :, :],
                                                R["b2"][:, :].unsqueeze(1).to_broadcast([P, 8, D]), ALU.add).then_inc(xt_added, 1)
                    pipeline(pool, chunks, [(add, 0)], 4)

                @block.tensor
                def _(pe):
                    pe.wait_ge(loads, 16 * len(plan))
                    nc.tensor.transpose(bank[4][:, 0:D], wq[:, :], ident)
                    nc.tensor.transpose(bank[4][:, D:2 * D], wv[:, :], ident).then_inc(weights_ps, 1)
                    pe.wait_ge(columns_in, 1)
                    for k in range(4):
                        for b in range(2):
                            last = nc.tensor.transpose(bank[k][:, b * (NT // 2):(b + 1) * (NT // 2)], rowsF[:, k, b, :],
                                                       K[0:NT // 2, K_ID:K_ID + NT // 2])
                    last.then_inc(columns_ps, 1)
                    pe.wait_ge(act_link, 1)
                    nc.tensor.matmul(bank[5][:, 0:D], wqT[:, :], wqT[:, :], start=True, stop=True)
                    nc.tensor.matmul(bank[5][:, D:D + 1], wqT[:, :], C["bqk"][:, :], start=True, stop=True)
                    nc.tensor.matmul(bank[6][0:1, 0:D], C["bqk"][:, :], wqT[:, :], start=True, stop=True)
                    nc.tensor.matmul(bank[6][0:1, D:D + 1], C["bqk"][:, :], C["bqk"][:, :], start=True, stop=True)
                    nc.tensor.matmul(bank[7][:, 0:D], wvT[:, :], wo[:, :], start=True, stop=True)
                    nc.tensor.matmul(bank[7][:, D:2 * D], C["bv"][:, :].to_broadcast([P, P]), wo[:, :], start=True,
                                     stop=True).then_inc(weights_ps, 1)
                    pe.wait_ge(columns_in, 3)
                    nc.tensor.matmul(bank[4][:, 0:1], ones, cnt[:, :], start=True, stop=True).then_inc(weights_ps, 1)

                    def counts(g, s):
                        pe.wait_ge(hot_ready, g + 1)
                        for b in range(2):
                            nc.tensor.matmul(bank[b][0:HB, :], hot_s[:, s, b * HB:(b + 1) * HB],
                                             hot_s[:, s, NHI:], start=False, stop=False, skip_group_check=True)
                            last = nc.tensor.matmul(bank[2 + b][0:HB, 0:NLO], hot_d[:, s, b * HB:(b + 1) * HB],
                                                    hot_d[:, s, NHI:], start=False, stop=False, skip_group_check=True)
                        last.then_inc(hot_used, 1)
                    pipeline(pe, NT, [(counts, 0)])
                    pe.wait_ge(totals_ready, 1)
                    nc.tensor.matmul(bank[4][0:HB, 0:2], K[0:HB, K_AFTER:K_AFTER + HB], totals[:, :], start=True, stop=True)
                    nc.tensor.matmul(bank[4][0:HB, 2:3], ones[0:HB, 0:HB], totals[:, 0:1], start=True,
                                     stop=True).then_inc(offsets_ps, 1)

                @block.scalar
                def _(act):
                    act.wait_ge(weights_ps, 1)
                    nc.scalar.activation(wqT[:, :], bank[4][:, 0:D], ACT.Copy)
                    nc.scalar.activation(wvT[:, :], bank[4][:, D:2 * D], ACT.Copy).then_inc(act_link, 1)
                    act.wait_ge(weights_ps, 2)
                    nc.scalar.activation(Wscore[:, :], bank[5][:, 0:D + 1], ACT.Copy)
                    for j in range(2):
                        nc.scalar.activation(urow[:, j * TW:j * TW + D + 1], bank[6][0:1, 0:D + 1], ACT.Copy)
                    nc.scalar.activation(W["Wvo"][:, :], bank[7][:, 0:D], ACT.Copy).then_inc(act_link, 1)

                    def store(g, s):
                        act.wait_ge(xt_added, g + 1)
                        act.dma_start(chunk_of(x1_d, g), xt[:, s, :, :]).then_inc(xt_out[s], 16)
                    pipeline(act, chunks, [(store, 0)], 4)
                    act.wait_ge(deg_ready, 1)
                    nc.scalar.activation(a["root"][:, :], a["w"][:, :], ACT.Sqrt).then_inc(root_ready, 1)
                    for s in range(4):
                        act.wait_ge(xt_out[s], 16 * ((chunks + 3 - s) // 4) + 16)

                @block.vector
                def _(dve):
                    def link(ins):
                        count[0] += 1
                        ins.then_inc(vec, 1)
                        dve.wait_ge(vec, count[0])

                    dve.wait_ge(loads, 16 * len(plan))
                    nc.vector.tensor_copy(rowsF[:, 0:3, :, :], rows[:, :, :, :]).then_inc(columns_in, 1)
                    dve.wait_ge(columns_ps, 1)
                    for k, dst in enumerate((srcF[:, :], dstF[:, 1:NT + 1], nextF[:, :], ew[:, :])):
                        link(nc.vector.tensor_copy(dst, bank[k][:, 0:NT]))
                    for k in range(4):
                        link(nc.vector.memset(bank[k][:, :], 0.0))
                    link(nc.vector.memset(dstF[:, 0:1], -1.0))
                    link(nc.vector.tensor_copy(srcI[:, :], srcF[:, :]))
                    link(nc.vector.tensor_copy(dstI[:, :], dstF[:, 1:NT + 1]))
                    for whole, hi, lo in ((srcI, "hs", "ls"), (dstI, "hd", "ld")):
                        link(nc.vector.tensor_single_scalar(tmpI[:, :], whole[:, :], 8, ALU.arith_shift_right))
                        link(nc.vector.tensor_copy(split[hi][:, :], tmpI[:, :]))
                        link(nc.vector.tensor_single_scalar(tmpI[:, :], whole[:, :], NLO - 1, ALU.bitwise_and))
                        link(nc.vector.tensor_copy(split[lo][:, :], tmpI[:, :]))
                    link(nc.vector.tensor_scalar(high[:, :], dstF[:, 1:NT + 1], float(HEDGES), None, ALU.is_ge))
                    link(nc.vector.tensor_scalar(low[:, :], dstF[:, 1:NT + 1], float(HEDGES), None, ALU.is_lt))
                    link(nc.vector.tensor_copy(iota[:, :], K[:, K_IOTA:K_IOTA + NLO]))
                    link(nc.vector.tensor_reduce(cnt[:, :], low[:, :], AX_X, ALU.add))
                    link(nc.vector.tensor_tensor(seg_end[:, :], dstF[:, 1:NT + 1], nextF[:, :], ALU.not_equal))
                    link(nc.vector.tensor_scalar(tmpF[:, :], edge_no, float(NN), None, ALU.add))
                    link(nc.vector.tensor_tensor(nextF[:, :], dstF[:, 1:NT + 1], tmpF[:, :], ALU.subtract))
                    link(nc.vector.tensor_tensor(nextF[:, :], nextF[:, :], seg_end[:, :], ALU.mult))
                    link(nc.vector.tensor_tensor(nextF[:, :], nextF[:, :], tmpF[:, :], ALU.add))
                    link(nc.vector.tensor_copy(out_row[:, :], nextF[:, :]))
                    link(nc.vector.tensor_scalar(tmpF[:, :], dstF[:, 1:NT + 1], float(N), None, ALU.is_lt))
                    link(nc.vector.tensor_tensor(seg_end[:, :], seg_end[:, :], tmpF[:, :], ALU.mult))
                    for m in (meta_src, meta_dst):
                        link(nc.vector.memset(m[:, :, :], 0.0))
                    dve.wait_ge(act_link, 2)
                    nc.vector.tensor_tensor(R["bvo"][:, :], bank[7][:, D:2 * D], R["bo"][:, :], ALU.add).then_inc(columns_in, 2)
                    dve.wait_ge(weights_ps, 3)
                    link(nc.vector.tensor_scalar(cnt[:, :], bank[4][:, 0:1], 1.0, float(LOW_STEP - 1), ALU.max, ALU.add))
                    link(nc.vector.tensor_copy(low_groups[:, :], cnt[:, :]))
                    link(nc.vector.tensor_single_scalar(low_groups[:, :], low_groups[:, :], 10, ALU.arith_shift_right))
                    link(nc.vector.tensor_copy(cnt[:, :], low_groups[:, :]))
                    link(nc.vector.tensor_scalar(cnt[:, :], cnt[:, :], 2.0, None, ALU.mult))
                    link(nc.vector.tensor_copy(low_groups[:, :], cnt[:, :]))

                    dve.sem_inc(hot_used, 2)

                    def hots(g, s):
                        at = bass.ds(g, 1)
                        dve.wait_ge(hot_used, g + 1)
                        for out, hi, lo in ((hot_s, "hs", "ls"), (hot_d, "hd", "ld")):
                            nc.vector.tensor_scalar(out[:, s, 0:NHI], iota[:, 0:NHI], split[hi][:, at], None, ALU.is_equal)
                            nc.vector.tensor_scalar(out[:, s, NHI:NHI + NLO], iota[:, :], split[lo][:, at], None,
                                                    ALU.is_equal)
                        nc.vector.tensor_scalar(hot_s[:, s, NHI + NLO:NHI + 2 * NLO], iota[:, :], split["ls"][:, at],
                                                high[:, at], ALU.is_equal, ALU.mult).then_inc(hot_ready, 1)
                    pipeline(dve, NT, [(hots, 0)])

                    dve.wait_ge(hot_used, NT + 2)
                    for b in range(2):
                        cols = slice(b * NLO, (b + 1) * NLO)
                        link(nc.vector.tensor_copy(deg["s"][:, cols], bank[b][0:HB, 0:NLO]))
                        link(nc.vector.tensor_copy(deg["h"][:, cols], bank[b][0:HB, NLO:2 * NLO]))
                        link(nc.vector.tensor_copy(deg["d"][:, cols], bank[2 + b][0:HB, 0:NLO]))
                    nc.vector.tensor_scalar(a["w"][:, :], deg["s"][:, :], 1.0, None, ALU.add).then_inc(deg_ready, 1)
                    node = K[0:HB, K_NODE:K_NODE + 2 * NLO]
                    link(nc.vector.tensor_scalar(a["x"][:, :], deg["s"][:, :], 1.0, None, ALU.max))
                    link(nc.vector.reciprocal(a["x"][:, :], a["x"][:, :]))
                    link(nc.vector.tensor_scalar(a["y"][:, :], deg["s"][:, :], 1.0, None, ALU.min))
                    link(nc.vector.tensor_tensor(a["x"][:, :], a["x"][:, :], a["y"][:, :], ALU.mult))
                    link(nc.vector.tensor_copy(meta[:, :, M_DINV], a["x"][:, :]))
                    link(nc.vector.tensor_tensor(meta[:, :, M_CHIGH], a["x"][:, :], deg["h"][:, :], ALU.mult))
                    link(nc.vector.tensor_scalar(a["x"][:, :], deg["d"][:, :], 1.0, None, ALU.max))
                    link(nc.vector.reciprocal(meta[:, :, M_BINV], a["x"][:, :]))
                    link(nc.vector.memset(a["y"][:, :], 1.0))
                    for b in range(2):
                        cols = slice(b * NLO, (b + 1) * NLO)
                        link(nc.vector.tensor_tensor_scan(a["z"][:, cols], a["y"][:, cols], deg["d"][:, cols], 0.0,
                                                          ALU.mult, ALU.add))
                        link(nc.vector.tensor_copy(totals[:, b:b + 1], a["z"][:, (b + 1) * NLO - 1:(b + 1) * NLO]))
                    dve.sem_inc(totals_ready, 1)
                    dve.wait_ge(offsets_ps, 1)
                    link(nc.vector.tensor_copy(a["x"][:, 0:3], bank[4][0:HB, 0:3]))
                    link(nc.vector.tensor_tensor(a["x"][:, 1:2], a["x"][:, 1:2], a["x"][:, 2:3], ALU.add))
                    for b in range(2):
                        cols = slice(b * NLO, (b + 1) * NLO)
                        link(nc.vector.tensor_scalar(a["z"][:, cols], a["z"][:, cols], a["x"][:, b:b + 1], None, ALU.add))
                    link(nc.vector.tensor_scalar(a["z"][:, :], a["z"][:, :], float(NN - 1), None, ALU.add))
                    link(nc.vector.tensor_tensor(a["z"][:, :], a["z"][:, :], node, ALU.subtract))
                    link(nc.vector.tensor_scalar(a["y"][:, :], deg["d"][:, :], 1.0, None, ALU.min))
                    link(nc.vector.tensor_tensor(a["z"][:, :], a["z"][:, :], a["y"][:, :], ALU.mult))
                    link(nc.vector.tensor_tensor(meta[:, :, M_INDEX], a["z"][:, :], node, ALU.add))
                    link(nc.vector.tensor_scalar(a["x"][:, :], node, float(N), None, ALU.is_lt))
                    link(nc.vector.tensor_scalar(a["y"][:, :], a["y"][:, :], -1.0, 1.0, ALU.mult, ALU.add))
                    link(nc.vector.tensor_tensor(a["x"][:, :], a["x"][:, :], a["y"][:, :], ALU.mult))
                    link(nc.vector.tensor_copy(meta[:, :, M_BARE], a["x"][:, :]))
                    dve.wait_ge(root_ready, 1)
                    link(nc.vector.reciprocal(a["root"][:, :], a["root"][:, :]))
                    link(nc.vector.tensor_tensor(a["w"][:, :], a["w"][:, :], a["root"][:, :], ALU.mult))
                    link(nc.vector.tensor_tensor(a["w"][:, :], a["w"][:, :], a["root"][:, :], ALU.mult))
                    link(nc.vector.tensor_scalar(a["w"][:, :], a["w"][:, :], -0.5, 1.5, ALU.mult, ALU.add))
                    link(nc.vector.tensor_tensor(a["w"][:, :], a["w"][:, :], a["root"][:, :], ALU.mult))
                    link(nc.vector.tensor_copy(meta[:, :, M_GINV], a["w"][:, :]))
                    link(nc.vector.tensor_tensor(a["w"][:, :], a["w"][:, :], a["w"][:, :], ALU.mult))
                    link(nc.vector.tensor_copy(meta[:, :, M_GINV2], a["w"][:, :]))
                    nc.vector.tensor_tensor(meta[:, :, M_Q], a["w"][:, :], a["x"][:, :], ALU.mult).then_inc(meta_ready, 1)

        def layer_sums(dve, tiles, st, tmp, neg, var, link, ready, g):
            n = len(tiles)
            for j, x in enumerate(tiles):
                last = nc.vector.bn_stats(st[:, j, :], x)
            last.then_inc(link, 1)
            dve.wait_ge(link, g * 4 + 1)
            nc.vector.tensor_tensor(tmp[:, 0, 0:n], st[:, 0:n, 1], st[:, 0:n, 4], ALU.add)
            nc.vector.tensor_tensor(tmp[:, 1, 0:n], st[:, 0:n, 1], st[:, 0:n, 4], ALU.subtract)
            nc.vector.tensor_tensor(tmp[:, 2, 0:n], st[:, 0:n, 2], st[:, 0:n, 5], ALU.add).then_inc(link, 1)
            dve.wait_ge(link, g * 4 + 2)
            nc.vector.tensor_scalar(neg, tmp[:, 0, 0:n], -0.5, None, ALU.mult)
            nc.vector.tensor_tensor(tmp[:, 1, 0:n], tmp[:, 1, 0:n], tmp[:, 1, 0:n], ALU.mult).then_inc(link, 1)
            dve.wait_ge(link, g * 4 + 3)
            nc.vector.scalar_tensor_tensor(out=tmp[:, 2, 0:n], in0=tmp[:, 1, 0:n], scalar=D / 4.0, in1=tmp[:, 2, 0:n],
                                           op0=ALU.mult, op1=ALU.add).then_inc(link, 1)
            dve.wait_ge(link, g * 4 + 4)
            nc.vector.tensor_scalar(var, tmp[:, 2, 0:n], 1.0 / D, EPS, ALU.mult, ALU.add).then_inc(ready, 1)

        def layer_scale(pool, neg, var, rs, nb, n, summed, link, ready, g):
            pool.wait_ge(summed, g + 1)
            nc.gpsimd.tensor_tensor(rs, var, minus_half[:, 0:n], ALU.pow).then_inc(link, 1)
            pool.wait_ge(link, g + 1)
            nc.gpsimd.tensor_tensor(nb, neg, rs, ALU.mult).then_inc(ready, 1)

        def summing_parts(dve, st, tmp, neg, var, link, ready):
            def differences(k, s):
                nc.vector.tensor_tensor(tmp[:, s % 2, 0, :], st[:, s, :, 1], st[:, s, :, 4], ALU.add)
                nc.vector.tensor_tensor(tmp[:, s % 2, 1, :], st[:, s, :, 1], st[:, s, :, 4], ALU.subtract)
                nc.vector.tensor_tensor(tmp[:, s % 2, 2, :], st[:, s, :, 2], st[:, s, :, 5], ALU.add).then_inc(link, 1)

            def squares(k, s):
                dve.wait_ge(link, k * 3 + 1)
                nc.vector.tensor_scalar(neg[:, s, :], tmp[:, s % 2, 0, :], -0.5, None, ALU.mult)
                nc.vector.tensor_tensor(tmp[:, s % 2, 1, :], tmp[:, s % 2, 1, :], tmp[:, s % 2, 1, :], ALU.mult).then_inc(link, 1)

            def total(k, s):
                dve.wait_ge(link, k * 3 + 2)
                nc.vector.scalar_tensor_tensor(out=tmp[:, s % 2, 2, :], in0=tmp[:, s % 2, 1, :], scalar=D / 4.0,
                                               in1=tmp[:, s % 2, 2, :], op0=ALU.mult, op1=ALU.add).then_inc(link, 1)

            def variance(k, s):
                dve.wait_ge(link, k * 3 + 3)
                nc.vector.tensor_scalar(var[:, s, :], tmp[:, s % 2, 2, :], 1.0 / D, EPS, ALU.mult, ALU.add).then_inc(ready, 1)
            return differences, squares, total, variance

        def gather(pool, out, table, index, s):
            pool.indirect_dma_start(out=out, out_offset=None, in_=table,
                                    in_offset=bass.IndirectOffsetOnAxis(ap=index, axis=0)).then_inc(s, 16)

        def groups_of_low(eng):
            return eng.value_load(low_groups[0:1, 0:1], min_val=2, max_val=NGE)

        def hyperedges(conv):
            with phase() as c:
                ix = sb("ix", [P, 2, 2 * G], I32, c)
                col = sb("col", [P, 2, G + 1], F32, c)
                rows = sb("rows", [P, 2, G, D], F32, c)
                ms, md = (sb(n, [P, 2, G, 8], F32, c) for n in ("ms", "md"))
                st = sb("st", [P, G, 6], F32, c)
                tmp = sb("tmp", [P, 3, G], F32, c)
                neg, var, rs, nb = (sb(n, [P, 2, G], F32, c) for n in ("neg", "var", "rs", "nb"))
                h = sb("h", [P, 2, G, D], F32, c)
                same, carry, sumT, out = (sb(n, [P, 2, G, P], F32, c) for n in ("same", "carry", "sumT", "out"))
                whole = sb("whole", [P, 2, G, D], F32, c)
                cols_ready, pool_link, summed, scaled, link, h_ready, bc_ps, same_ready, sumT_ps, sumT_in, he_ps, \
                    whole_in, out_ready, meta_kept, front = (sem(f"he_{n}") for n in (
                        "cols_ready", "pool_link", "summed", "scaled", "link", "h_ready", "bc_ps", "same_ready",
                        "sumT_ps", "sumT_in", "he_ps", "whole_in", "out_ready", "meta_kept", "front"))
                rows_in = [sem("he_rows_in0"), sem("he_rows_in1")]
                stored = [sem("he_stored0"), sem("he_stored1")]
                bc, sT, hps = bank[0], bank[1], [bank[2], bank[3]]
                weight = W["W1"] if conv == 0 else W["W2"]
                n_in = 16 * G * (3 if conv == 0 else 1)

                with nc.Block() as block:
                    @block.gpsimd
                    def _(pool):
                        n = groups_of_low(pool)

                        def part(g, s):
                            hold("pool", pool, stored[s], (g - s) * 8 + 16)
                            nc.gpsimd.tensor_copy(ix[:, s, 0:G], srcI[:, bass.ds(g * G, G)])
                            if conv == 0:
                                nc.gpsimd.tensor_copy(ix[:, s, G:2 * G], dstI[:, bass.ds(g * G, G)])
                            else:
                                nc.gpsimd.tensor_copy(ms[:, s, :, :], meta_src[:, bass.ds(g * G, G), :])
                                nc.gpsimd.tensor_copy(md[:, s, :, :], meta_dst[:, bass.ds(g * G, G), :])
                            nc.gpsimd.tensor_copy(col[:, s, :], dstF[:, bass.ds(g * G, G + 1)]).then_inc(cols_ready, 1)
                            hold("pool", pool, cols_ready, g + 1)
                            for j in range(G):
                                gather(pool, rows[:, s, j, :], t["x"] if conv == 0 else sum1_d, ix[:, s, j:j + 1], rows_in[s])
                                if conv == 0:
                                    gather(pool, ms[:, s, j, :], meta_d, ix[:, s, j:j + 1], rows_in[s])
                                    gather(pool, md[:, s, j, :], meta_d, ix[:, s, G + j:G + j + 1], rows_in[s])

                        def scale(g, s):
                            if conv == 0:
                                layer_scale(pool, neg[:, s, :], var[:, s, :], rs[:, s, :], nb[:, s, :], G, summed,
                                            pool_link, scaled, g)
                        bounded(pool, n, part, scale)

                    @block.vector
                    def _(dve):
                        n = groups_of_low(dve)
                        nc.vector.memset(whole[:, 1, G - 1, :], 0.0).then_inc(whole_in, 1)

                        def part(g, s):
                            dve.wait_ge(rows_in[s], ((g - s) // 2) * n_in + n_in)
                            if conv == 0:
                                layer_sums(dve, [rows[:, s, j, :] for j in range(G)], st, tmp, neg[:, s, :], var[:, s, :],
                                           link, summed, g)
                                nc.vector.tensor_copy(meta_src[:, bass.ds(g * G, G), :], ms[:, s, :, :])
                                nc.vector.tensor_copy(meta_dst[:, bass.ds(g * G, G), :], md[:, s, :, :])
                            else:
                                for j in range(G):
                                    last = nc.vector.scalar_tensor_tensor(
                                        out=rows[:, s, j, :], in0=rows[:, s, j, :], scalar=ms[:, s, j, M_DINV:M_DINV + 1],
                                        in1=R["b1"][:, :], op0=ALU.mult, op1=ALU.add)
                                last.then_inc(link, 1)
                                dve.wait_ge(link, g + 1)
                                for j in range(G):
                                    last = nc.vector.scalar_tensor_tensor(
                                        out=rows[:, s, j, :], in0=he_last[0][:, :], scalar=ms[:, s, j, M_CHIGH:M_CHIGH + 1],
                                        in1=rows[:, s, j, :], op0=ALU.mult, op1=ALU.add)
                                last.then_inc(scaled, 1)
                            dve.wait_ge(bc_ps, g + 1)
                            for j in range(G):
                                nc.vector.tensor_scalar(same[:, s, j, :], bc[:, j * P:(j + 1) * P], col[:, s, j + 1:j + 2],
                                                        None, ALU.is_equal)
                                last = nc.vector.tensor_scalar(carry[:, s, j, :], bc[:, j * P:(j + 1) * P], col[:, s, j:j + 1],
                                                               last_row, ALU.is_equal, ALU.mult)
                            last.then_inc(same_ready, 1)
                            dve.wait_ge(whole_in, g * G + G + 1)
                            for j in range(G):
                                last = nc.vector.tensor_scalar(out[:, s, j, :], whole[:, s, j, :],
                                                               md[:, s, j, M_BINV:M_BINV + 1], None, ALU.mult)
                            last.then_inc(out_ready, 1)
                        bounded(dve, n, part)

                    @block.scalar
                    def _(act):
                        act.preload_act_table(ACT.Relu)
                        n = groups_of_low(act)

                        def part(g, s):
                            act.wait_ge(scaled, g + 1)
                            if conv == 0:
                                for j in range(G):
                                    last = nc.scalar.activation(h[:, s, j, :], rows[:, s, j, :], ACT.Relu,
                                                                bias=nb[:, s, j:j + 1], scale=rs[:, s, j:j + 1])
                            else:
                                last = nc.scalar.activation(h[:, s, :, :], rows[:, s, :, :], ACT.Relu)
                            last.then_inc(h_ready, 1)
                            act.wait_ge(sumT_ps, g + 1)
                            nc.scalar.activation(sumT[:, s, :, :], sT[:, :].rearrange("p (j f) -> p j f", j=G),
                                                 ACT.Copy).then_inc(sumT_in, 1)
                            for j in range(G):
                                act.wait_ge(he_ps, g * G + j + 1)
                                nc.scalar.activation(whole[:, s, j, :], hps[j % 2][:, 0:D], ACT.Copy).then_inc(whole_in, 1)
                        bounded(act, n, part)

                    @block.tensor
                    def _(pe):
                        n = groups_of_low(pe)
                        pe.sem_inc(same_ready, 1)

                        def part(g, s):
                            pe.wait_ge(cols_ready, g + 1)
                            pe.wait_ge(same_ready, g + 1)
                            for j in range(G):
                                last = nc.tensor.transpose(bc[:, j * P:(j + 1) * P],
                                                           col[:, s, j + 1:j + 2].to_broadcast([P, P]), ident)
                            last.then_inc(bc_ps, 1)
                            pe.wait_ge(h_ready, g + 1)
                            pe.wait_ge(same_ready, g + 2)
                            for j in range(G):
                                last = nc.tensor.matmul(sT[:, j * P:(j + 1) * P], h[:, s, j, :], same[:, s, j, :],
                                                        start=True, stop=True)
                            last.then_inc(sumT_ps, 1)
                            pe.wait_ge(sumT_in, g + 1)
                            for j in range(G):
                                before = whole[:, s, j - 1, :] if j else whole[:, 1 - s, G - 1, :]
                                nc.tensor.matmul(hps[j % 2][:, 0:D], sumT[:, s, j, :], weight[:, :], start=True, stop=False)
                                pe.wait_ge(whole_in, g * G + j + 1)
                                nc.tensor.matmul(hps[j % 2][:, 0:D], carry[:, s, j, :], before, start=False,
                                                 stop=True).then_inc(he_ps, 1)
                        bounded(pe, n, part)

                    @block.sync
                    def _(sp):
                        n = groups_of_low(sp)
                        for s in range(2):
                            sp.sem_inc(stored[s], 16)

                        def part(g, s):
                            sp.wait_ge(out_ready, g + 1)
                            sp.dma_start(rows_of(he_d, g, D), out[:, s, :, :]).then_inc(stored[s], 16)
                            hold("sp", sp, stored[s], (g - s) * 8 + 32)
                        bounded(sp, n, part)

        def last_hyperedge(conv):
            with phase() as c:
                m = sb("m", [P, 8], F32, c)
                v = sb("v", [P, 4], F32, c)
                vi = sb("vi", [P, 1], I32, c)
                e = sb("e", [P, NT], F32, c)
                m_in, link, v_ready, row_in = (sem(f"last_{n}") for n in ("m_in", "link", "v_ready", "row_in"))
                with nc.Block() as block:
                    @block.sync
                    def _(sp):
                        sp.dma_start(m[:, :], meta_d[HEDGES - 1, :].partition_broadcast(P)).then_inc(m_in, 16)

                    @block.vector
                    def _(dve):
                        k = [0]

                        def chain(ins):
                            k[0] += 1
                            ins.then_inc(link, 1)
                            dve.wait_ge(link, k[0])

                        dve.wait_ge(m_in, 16)
                        chain(nc.vector.tensor_scalar(v[:, 0:1], m[:, M_INDEX:M_INDEX + 1], float(NN), None, ALU.is_ge))
                        chain(nc.vector.tensor_scalar(v[:, 1:2], m[:, M_INDEX:M_INDEX + 1], float(-NN - EP), None, ALU.add))
                        chain(nc.vector.tensor_tensor(v[:, 2:3], v[:, 0:1], v[:, 1:2], ALU.mult))
                        chain(nc.vector.tensor_scalar(v[:, 3:4], v[:, 2:3], float(EP), None, ALU.add))
                        nc.vector.tensor_copy(vi[:, :], v[:, 3:4]).then_inc(v_ready, 1)
                        if conv == 0:
                            chain(nc.vector.tensor_tensor(e[:, :], meta_dst[:, :, M_INDEX], edge_no, ALU.subtract))
                            chain(nc.vector.tensor_scalar(e[:, :], e[:, :], float(-NN), None, ALU.add))
                            chain(nc.vector.tensor_tensor(e[:, :], e[:, :], low[:, :], ALU.mult))
                            chain(nc.vector.tensor_tensor(e[:, :], e[:, :], edge_no, ALU.add))
                            chain(nc.vector.tensor_copy(he_index[:, :], e[:, :]))

                    @block.gpsimd
                    def _(pool):
                        pool.wait_ge(v_ready, 1)
                        gather(pool, he_last[conv][:, :], he_d, vi[:, :], row_in)
                        pool.wait_ge(row_in, 16)

        def to_sources(conv):
            with phase() as c:
                width = D if conv == 0 else XW
                ix = sb("ix", [P, 2, G], I32, c)
                col = sb("col", [P, 2, G], F32, c)
                lo = sb("lo", [P, 2, G], F32, c)
                dinv = sb("dinv", [P, 2, G], F32, c)
                rows = sb("rows", [P, 2, G, D], F32, c)
                same = sb("same", [P, 2, G, P], F32, c)
                junk = sb("junk", [P, P], F32, c)
                later = sb("later", [P, 3, G], F32, c)
                to = sb("to", [P, 2, G], I32, c)
                add = sb("add", [P, 2, G, width], F32, c)
                cols_ready, bc_ps, same_ready, comb_ps, add_ready, to_ready, link, added, cleared, comb_free = (
                    sem(f"ts_{n}") for n in ("cols_ready", "bc_ps", "same_ready", "comb_ps", "add_ready", "to_ready",
                                             "link", "added", "cleared", "comb_free"))
                rows_in = [sem("ts_rows_in0"), sem("ts_rows_in1")]
                bc, comb = [bank[0], bank[1]], [bank[2], bank[3]]
                table = sum1_d if conv == 0 else x1_d

                with nc.Block() as block:
                    @block.gpsimd
                    def _(pool):
                        n = groups_of_low(pool)
                        nc.gpsimd.memset(add[:, :, :, :], 0.0).then_inc(cleared, 1)
                        if conv == 1:
                            pool.wait_ge(x1_meta, 16)

                        def part(g, s):
                            nc.gpsimd.tensor_copy(ix[:, s, :], he_index[:, bass.ds(g * G, G)])
                            nc.gpsimd.tensor_copy(col[:, s, :], srcF[:, bass.ds(g * G, G)])
                            nc.gpsimd.tensor_copy(dinv[:, s, :], meta_src[:, bass.ds(g * G, G), M_DINV])
                            nc.gpsimd.tensor_copy(lo[:, s, :], low[:, bass.ds(g * G, G)]).then_inc(cols_ready, 1)
                            hold("pool", pool, cols_ready, g + 1)
                            for j in range(G):
                                gather(pool, rows[:, s, j, :], he_d, ix[:, s, j:j + 1], rows_in[s])

                        def scatter(g, s):
                            hold("pool", pool, to_ready, g + 1)
                            hold("pool", pool, add_ready, g + 1)
                            for j in range(G):
                                pool.indirect_dma_start(out=table, out_offset=bass.IndirectOffsetOnAxis(ap=to[:, s, j:j + 1], axis=0),
                                                        in_=add[:, s, j, :], in_offset=None, compute_op=ALU.add).then_inc(added, 16)
                                hold("pool", pool, added, (g * G + j) * 16 + 16)
                        bounded(pool, n, part, scatter)

                    @block.tensor
                    def _(pe):
                        n = groups_of_low(pe)

                        def part(g, s):
                            pe.wait_ge(cols_ready, g + 1)
                            for j in range(G):
                                last = nc.tensor.transpose(bc[s][:, j * P:(j + 1) * P], col[:, s, j:j + 1].to_broadcast([P, P]), ident)
                            last.then_inc(bc_ps, 1)
                            pe.wait_ge(same_ready, g + 1)
                            hold("pe", pe, rows_in[s], (g - s) * (8 * G) + 16 * G)
                            for j in range(G):
                                last = nc.tensor.matmul(comb[s][:, j * P:(j + 1) * P], same[:, s, j, :], rows[:, s, j, :],
                                                        start=True, stop=True)
                            last.then_inc(comb_ps, 1)
                        bounded(pe, n, part)

                    @block.vector
                    def _(dve):
                        n = groups_of_low(dve)

                        def part(g, s):
                            dve.wait_ge(bc_ps, g + 1)
                            for j in range(G):
                                nc.vector.tensor_scalar(same[:, s, j, :], bc[s][:, j * P:(j + 1) * P], col[:, s, j:j + 1],
                                                        lo[:, s, j:j + 1], ALU.is_equal, ALU.mult)
                                last = nc.vector.scalar_tensor_tensor(out=junk[:, :], in0=bc[s][:, j * P:(j + 1) * P],
                                                                      scalar=col[:, s, j:j + 1], in1=after, op0=ALU.is_equal,
                                                                      op1=ALU.mult, accum_out=later[:, 0, j:j + 1])
                                last.then_inc(link, 1)
                                dve.wait_ge(link, g * (G + 3) + j + 1)
                            dve.sem_inc(same_ready, 1)
                            nc.vector.tensor_scalar(later[:, 1, :], later[:, 0, :], 1.0, None, ALU.min)
                            nc.vector.tensor_scalar(later[:, 2, :], col[:, s, :], -1.0, dump_row, ALU.mult, ALU.add).then_inc(link, 1)
                            dve.wait_ge(link, g * (G + 3) + G + 1)
                            nc.vector.tensor_tensor(later[:, 1, :], later[:, 1, :], later[:, 2, :], ALU.mult).then_inc(link, 1)
                            dve.wait_ge(link, g * (G + 3) + G + 2)
                            nc.vector.tensor_tensor(later[:, 2, :], later[:, 1, :], col[:, s, :], ALU.add).then_inc(link, 1)
                            dve.wait_ge(link, g * (G + 3) + G + 3)
                            nc.vector.tensor_copy(to[:, s, :], later[:, 2, :]).then_inc(to_ready, 1)
                            dve.wait_ge(to_ready, g + 1)
                        bounded(dve, n, part)

                    @block.scalar
                    def _(act):
                        act.preload_act_table(ACT.Copy)
                        act.wait_ge(cleared, 1)
                        n = groups_of_low(act)

                        def part(g, s):
                            act.wait_ge(comb_ps, g + 1)
                            for j in range(G):
                                if conv == 0:
                                    last = nc.scalar.activation(add[:, s, j, 0:D], comb[s][:, j * P:(j + 1) * P], ACT.Copy)
                                else:
                                    last = nc.scalar.activation(add[:, s, j, 0:D], comb[s][:, j * P:(j + 1) * P], ACT.Copy,
                                                                scale=dinv[:, s, j:j + 1])
                            last.then_inc(add_ready, 1)
                        bounded(act, n, part)

        for conv in range(2):
            hyperedges(conv)
            last_hyperedge(conv)
            to_sources(conv)
        S = 4

        def slot_count(g, s, dmas):
            return (g - s) * (16 // S * dmas) + 16 * dmas

        with phase() as c:
            S8 = 8
            last_norm = 6
            ix = sb("ix", [P, 4, 2 * G], I32, c)
            xs = sb("xs", [P, 4, G, XW], F32, c)
            xd = sb("xd", [P, S8, G, XW], F32, c)
            hs = sb("hs", [P, 4, G, TW], F32, c)
            hd = sb("hd", [P, S8, G, D], F32, c)
            x2 = sb("x2", [P, 4, G, D], F32, c)
            bc = sb("bc", [P, 4, G * P], I32, c)
            st = sb("st", [P, S8, 3 * G, 6], F32, c)
            tmp = sb("tmp", [P, 2, 3, 3 * G], F32, c)
            neg, var, rs, nb = (sb(n, [P, S8, 3 * G], F32, c) for n in ("neg", "var", "rs", "nb"))
            sum_link, mixed = sem("at_sum_link"), sem("at_mixed")
            hdT, attT = (sb(n, [P, 2, G * P], F32, c) for n in ("hdT", "attT"))
            junk = sb("junk", [P, G, D + 1], F32, c)
            score, e, rden = (sb(n, [P, S8, G], F32, c) for n in ("score", "e", "rden"))
            same, carry = (sb(n, [P, 4, G, P], F32, c) for n in ("same", "carry"))
            sums = sb("sums", [P, 4, G, TW], F32, c)
            ix_ready, pool_link, summed, summed2, scaled, x_link, h_ready, hdT_ps, hdT_in, r_ps, clip_link, score_ready, \
                e_ready, same_ready, sum_ps, sum_in, set_up, attT_ps, attT_in, o_ps, o_used, rden_ready, row_link, z_ready, \
                x2_link, x2_ready = (sem(f"at_{n}") for n in (
                    "ix_ready", "pool_link", "summed", "summed2", "scaled", "x_link", "h_ready", "hdT_ps", "hdT_in", "r_ps",
                    "clip_link", "score_ready", "e_ready", "same_ready", "sum_ps", "sum_in", "set_up", "attT_ps",
                    "attT_in", "o_ps", "o_used", "rden_ready", "row_link", "z_ready", "x2_link", "x2_ready"))
            rows_in = [sem(f"at_rows_in{s}") for s in range(S8)]
            bc_in, stored = ([sem(f"at_{n}{s}") for s in range(4)] for n in ("bc_in", "stored"))
            hdT_p, rp, sum_p, attT_p, o_p = bank[0], [bank[1], bank[2]], bank[3], bank[4], [bank[5], bank[6]]

            def count8(g, s, dmas):
                return (g - s) * (2 * dmas) + 16 * dmas

            def count4(g, s):
                return (g - s % 4) * 4 + 16

            with nc.Block() as block:
                @block.gpsimd
                def _(pool):
                    pool.wait_ge(set_up, 1)

                    def src_used(g, s):
                        hold("pool", pool, h_ready, g + 1)

                    def dst_used(g, s):
                        hold("pool", pool, row_link, g + 1)

                    def rows(g, s):
                        at = s % 4
                        nc.gpsimd.tensor_copy(ix[:, at, 0:G], srcI[:, bass.ds(g * G, G)])
                        nc.gpsimd.tensor_copy(ix[:, at, G:2 * G], dstI[:, bass.ds(g * G, G)]).then_inc(ix_ready, 1)
                        hold("pool", pool, ix_ready, g + 1)
                        for j in range(G):
                            gather(pool, xs[:, at, j, :], x1_d, ix[:, at, j:j + 1], rows_in[s])
                            gather(pool, xd[:, s, j, :], x1_d, ix[:, at, G + j:G + j + 1], rows_in[s])

                    def scales(k, s):
                        layer_scale(pool, neg[:, s, :], var[:, s, :], rs[:, s, :], nb[:, s, :], 3 * G, mixed, pool_link,
                                    scaled, k)
                    pipeline(pool, NGE, [(src_used, 4), (dst_used, S8), (rows, 0), (scales, 1, last_norm)], S8)

                @block.sync
                def _(sp):
                    def bc_used(g, s):
                        sp.wait_ge(same_ready, g + 1)

                    def load_bc(g, s):
                        sp.dma_start(bc[:, s % 4, :], t["dst"][bass.ds(g * (G * P), G * P)].partition_broadcast(P)).then_inc(
                            bc_in[s % 4], 16)

                    def store(g, s):
                        sp.wait_ge(x2_ready, g + 1)
                        sp.dma_start(rows_of(x2_d, g, D, NN), x2[:, s % 4, :, :]).then_inc(stored[s % 4], 16)
                    pipeline(sp, NGE, [(bc_used, 5), (load_bc, 1), (store, 9)], S8)
                    for s in range(4):
                        sp.wait_ge(stored[s], 16 * ((NGE - s + 3) // 4) + 16)

                @block.vector
                def _(dve):
                    nc.vector.memset(hs[:, :, :, D:D + 1], 1.0)
                    nc.vector.memset(st[:, :, :, :], 0.0)
                    nc.vector.memset(sums[:, 3, G - 1, :], 0.0).then_inc(sum_in, 1)
                    dve.wait_ge(sum_in, 1)
                    dve.sem_inc(set_up, 1)
                    dve.sem_inc(score_ready, 1)
                    dve.sem_inc(o_used, 2)
                    for s in range(4):
                        dve.sem_inc(stored[s], 16)

                    def last_edge(g, s):
                        dve.wait_ge(rows_in[s], count8(g, s, 2 * G))
                        for x in (xs[:, s % 4, :, :], xd[:, s, :, :]):
                            for j in range(G):
                                last = nc.vector.scalar_tensor_tensor(
                                    out=x[:, j, 0:D], in0=he_last[1][:, :], scalar=x[:, j, D + M_CHIGH:D + M_CHIGH + 1],
                                    in1=x[:, j, 0:D], op0=ALU.mult, op1=ALU.add)
                        last.then_inc(x_link, 1)
                        nc.vector.tensor_copy(table_src[:, bass.ds(g * G, G)], xs[:, s % 4, :, D + M_INDEX])
                        nc.vector.tensor_copy(table_dst[:, bass.ds(g * G, G)], xd[:, s, :, D + M_INDEX])
                        nc.vector.tensor_copy(ginv_dst[:, bass.ds(g * G, G)], xd[:, s, :, D + M_GINV])

                    def stats(g, s):
                        dve.wait_ge(x_link, g + 1)
                        for j in range(G):
                            nc.vector.bn_stats(st[:, s, j, :], xs[:, s % 4, j, 0:D])
                        for j in range(G):
                            last = nc.vector.bn_stats(st[:, s, G + j, :], xd[:, s, j, 0:D])
                        last.then_inc(summed, 1)

                    def scores(g, s):
                        dve.wait_ge(r_ps, g + 1)
                        for j in range(G):
                            last = nc.vector.scalar_tensor_tensor(
                                out=junk[:, j, :], in0=rp[j // 2][:, (j % 2) * TW:(j % 2) * TW + D + 1], scalar=float(D) ** -0.5,
                                in1=hs[:, s % 4, j, 0:D + 1], op0=ALU.mult, op1=ALU.mult, accum_out=score[:, s, j:j + 1])
                        last.then_inc(clip_link, 1)
                        dve.wait_ge(clip_link, g + 1)
                        nc.vector.tensor_scalar(score[:, s, :], score[:, s, :], 5.0, -5.0, ALU.min, ALU.max).then_inc(score_ready, 1)

                    def carries(g, s):
                        dve.wait_ge(bc_in[s % 4], count4(g, s))
                        for j in range(G):
                            nc.vector.tensor_scalar(carry[:, s % 4, j, :], bc[:, s % 4, j * P:(j + 1) * P],
                                                    dstF[:, bass.ds(g * G + j, 1)], last_row, ALU.is_equal, ALU.mult)

                    def sames(g, s):
                        dve.wait_ge(e_ready, g + 1)
                        for j in range(G):
                            last = nc.vector.tensor_scalar(same[:, s % 4, j, :], bc[:, s % 4, j * P:(j + 1) * P],
                                                           dstF[:, bass.ds(g * G + (j + 1), 1)], e[:, s, j:j + 1],
                                                           ALU.is_equal, ALU.mult)
                        last.then_inc(same_ready, 1)

                    def denominator(g, s):
                        dve.wait_ge(o_ps, g + 1)
                        nc.vector.reciprocal(rden[:, s, :], sums[:, s % 4, :, D]).then_inc(rden_ready, 1)

                    def attended(g, s):
                        dve.wait_ge(rden_ready, g + 1)
                        for j in range(G):
                            last = nc.vector.scalar_tensor_tensor(
                                out=hd[:, s, j, :], in0=o_p[s % 2][:, j * P:(j + 1) * P], scalar=rden[:, s, j:j + 1],
                                in1=hd[:, s, j, :], op0=ALU.mult, op1=ALU.add)
                        last.then_inc(o_used, 1)

                    def biased(g, s):
                        dve.wait_ge(stored[s % 4], count4(g, s))
                        nc.vector.tensor_tensor(x2[:, s % 4, :, :], xd[:, s, :, 0:D],
                                                R["beta"][:, :].unsqueeze(1).to_broadcast([P, G, D]), ALU.add)
                        dve.wait_ge(o_used, g + 3)
                        nc.vector.tensor_tensor(hd[:, s, :, :], hd[:, s, :, :],
                                                R["bvo"][:, :].unsqueeze(1).to_broadcast([P, G, D]), ALU.add).then_inc(row_link, 1)

                    def stats2(g, s):
                        dve.wait_ge(row_link, g + 1)
                        for j in range(G):
                            last = nc.vector.bn_stats(st[:, (s + last_norm) % S8, 2 * G + j, :], hd[:, s, j, :])
                        last.then_inc(summed2, 1)

                    def times_gamma(g, s):
                        dve.wait_ge(z_ready, g + 1)
                        nc.vector.tensor_tensor(hd[:, s, :, :], hd[:, s, :, :],
                                                R["gamma"][:, :].unsqueeze(1).to_broadcast([P, G, D]), ALU.mult).then_inc(x2_link, 1)

                    def added(g, s):
                        dve.wait_ge(x2_link, g + 1)
                        nc.vector.tensor_tensor(x2[:, s % 4, :, :], x2[:, s % 4, :, :], hd[:, s, :, :], ALU.add).then_inc(x2_ready, 1)
                    def rows_summed(g, s):
                        dve.wait_ge(summed, g + 1)

                    def attended_summed(g, s):
                        dve.wait_ge(summed2, g + 1)
                    differences, squares, total, variance = summing_parts(dve, st, tmp, neg, var, sum_link, mixed)
                    pipeline(dve, NGE, [(denominator, 7), (last_edge, 1), (attended, 7), (carries, 4), (biased, 7), (stats, 1),
                                        (stats2, 7), (rows_summed, 1), (attended_summed, 1 + last_norm),
                                        (differences, 1, last_norm), (sames, 4), (squares, 1, last_norm), (times_gamma, 8),
                                        (total, 1, last_norm), (scores, 3), (variance, 1, last_norm), (added, 8)], S8)

                @block.scalar
                def _(act):
                    act.preload_act_table(ACT.Exp)
                    act.wait_ge(set_up, 1)

                    def relus(g, s):
                        act.wait_ge(scaled, g + 1)
                        for k, x, h in ((G, xd[:, s, :, :], hd[:, s, :, :]), (0, xs[:, s % 4, :, :], hs[:, s % 4, :, :])):
                            for j in range(G):
                                last = nc.scalar.activation(h[:, j, 0:D], x[:, j, 0:D], ACT.Relu, bias=nb[:, s, k + j:k + j + 1],
                                                            scale=rs[:, s, k + j:k + j + 1])
                        last.then_inc(h_ready, 1)

                    def hdT_copy(g, s):
                        act.wait_ge(hdT_ps, g + 1)
                        nc.scalar.activation(hdT[:, s % 2, :], hdT_p[:, :], ACT.Copy).then_inc(hdT_in, 1)

                    def exps(g, s):
                        act.wait_ge(score_ready, g + 2)
                        nc.scalar.activation(e[:, s, :], score[:, s, :], ACT.Exp).then_inc(e_ready, 1)

                    def total(j):
                        def part(g, s):
                            act.wait_ge(sum_ps, g * G + j + 1)
                            nc.scalar.activation(sums[:, s % 4, j, 0:D + 1], sum_p[:, 0:D + 1], ACT.Copy).then_inc(sum_in, 1)
                        return part

                    def attT_copy(g, s):
                        act.wait_ge(attT_ps, g + 1)
                        nc.scalar.activation(attT[:, s % 2, :], attT_p[:, :], ACT.Copy).then_inc(attT_in, 1)

                    def normed(g, s):
                        act.wait_ge(scaled, g + last_norm + 1)
                        at = (s + last_norm) % S8
                        for j in range(G):
                            last = nc.scalar.activation(hd[:, s, j, :], hd[:, s, j, :], ACT.Identity,
                                                        bias=nb[:, at, 2 * G + j:2 * G + j + 1],
                                                        scale=rs[:, at, 2 * G + j:2 * G + j + 1])
                        last.then_inc(z_ready, 1)
                    pipeline(act, NGE, [(hdT_copy, 3), (total(0), 5), (exps, 4), (normed, 8), (total(1), 5), (relus, 2),
                                        (total(2), 5), (attT_copy, 6), (total(3), 5)], S8)

                @block.tensor
                def _(pe):
                    pe.wait_ge(set_up, 1)

                    def transposes(g, s):
                        pe.wait_ge(h_ready, g + 1)
                        for j in range(G):
                            last = nc.tensor.transpose(hdT_p[:, j * P:(j + 1) * P], hd[:, s, j, :], ident)
                        last.then_inc(hdT_ps, 1)

                    def product(g, s):
                        pe.wait_ge(score_ready, g + 1)
                        pe.wait_ge(hdT_in, g + 1)
                        for j in range(G):
                            out = rp[j // 2][:, (j % 2) * TW:(j % 2) * TW + D + 1]
                            nc.tensor.matmul(out, hdT[:, s % 2, j * P:(j + 1) * P], Wscore[:, :], start=True, stop=False)
                            last = nc.tensor.matmul(out, ones[0:1, :], urow[:, 0:D + 1], start=False, stop=True)
                        last.then_inc(r_ps, 1)

                    def total(j):
                        def part(g, s):
                            if j == 0:
                                pe.wait_ge(same_ready, g + 1)
                            before = sums[:, s % 4, j - 1, 0:D + 1] if j else sums[:, (s - 1) % 4, G - 1, 0:D + 1]
                            pe.wait_ge(sum_in, g * G + j + 1)
                            nc.tensor.matmul(sum_p[:, 0:D + 1], same[:, s % 4, j, :], hs[:, s % 4, j, 0:D + 1], start=True, stop=False)
                            nc.tensor.matmul(sum_p[:, 0:D + 1], carry[:, s % 4, j, :], before, start=False,
                                             stop=True).then_inc(sum_ps, 1)
                        return part

                    def attended(g, s):
                        pe.wait_ge(sum_in, g * G + G + 1)
                        for j in range(G):
                            last = nc.tensor.transpose(attT_p[:, j * P:(j + 1) * P], sums[:, s % 4, j, 0:D], ident)
                        last.then_inc(attT_ps, 1)

                    def output(g, s):
                        pe.wait_ge(attT_in, g + 1)
                        pe.wait_ge(o_used, g + 1)
                        for j in range(G):
                            last = nc.tensor.matmul(o_p[s % 2][:, j * P:(j + 1) * P], attT[:, s % 2, j * P:(j + 1) * P],
                                                    W["Wvo"][:, :], start=True, stop=True)
                        last.then_inc(o_ps, 1)
                    pipeline(pe, NGE, [(total(0), 5), (product, 3), (total(1), 5), (attended, 6), (total(2), 5),
                                       (transposes, 2), (total(3), 5), (output, 6)], S8)

        def bare_nodes():
            n = NGN
            norms = 4
            late = 2 * (norms - 1)
            S = 8

            def slot_count(g, s):
                return (g - s) * 2 + 16

            with phase() as c:
                x1 = sb("x1", [P, S, G, XW], F32, c)
                h = sb("h", [P, S, G, D], F32, c)
                x2 = sb("x2", [P, S, G, D], F32, c)
                st = sb("st", [P, S, norms * G, 6], F32, c)
                tmp = sb("tmp", [P, 2, 3, norms * G], F32, c)
                neg, var, rs, nb = (sb(k, [P, S, norms * G], F32, c) for k in ("neg", "var", "rs", "nb"))
                sum_link, mixed = sem("up_sum_link"), sem("up_mixed")
                summed = [sem(f"up_summed{i}") for i in range(norms)]
                scaled, pool_link, st_clear = sem("up_scaled"), sem("up_pool_link"), sem("up_st_clear")
                x1_added = sem("up_x1_added")
                x_ready, h_ready, hb_link, z_ready, x2_link, x2_ready = (sem(f"up_{k}") for k in (
                    "x_ready", "h_ready", "hb_link", "z_ready", "x2_link", "x2_ready"))
                used = sem("up_used")
                rows_in = [sem(f"up_rows_in{s}") for s in range(S)]
                stored, r_stored = ([sem(f"up_{k}{s}") for s in range(S)] for k in ("stored", "r_stored"))
                m = sb("m", [P, S, G, 8], F32, c)
                h2 = sb("h2", [P, S, G, D], F32, c)
                r = sb("r", [P, S, G, RW], F32, c)
                u = sb("u", [P, S, G, D + 2], F32, c)
                h2_ready, x3_ready, h3_ready, u_ready, gram_done, gram_zero = (sem(f"up_{k}") for k in (
                    "h2_ready", "x3_ready", "h3_ready", "u_ready", "gram_done", "gram_zero"))

                with nc.Block() as block:
                    @block.sync
                    def _(sp):
                        sp.sem_inc(used, S)

                        def load(g, s):
                            sp.wait_ge(used, g + 1)
                            sp.dma_start(x1[:, s, :, :], node_rows_of(x1_d, g, XW)).then_inc(rows_in[s], 16)

                        def store(g, s):
                            sp.wait_ge(x2_ready, g + 1)
                            sp.dma_start(node_rows_of(x2_d, g, D), x2[:, s, :, :]).then_inc(stored[s], 16)

                        def store_r(g, s):
                            sp.wait_ge(gram_done, g + 1)
                            sp.dma_start(node_rows_of(r_d, g, RW), r[:, s, :, :]).then_inc(r_stored[s], 16)
                        pipeline(sp, n, [(load, 0), (store, 6), (store_r, 8)], S)
                        for s in range(S):
                            sp.wait_ge(stored[s], 16 * ((n - s + S - 1) // S) + 16)
                            sp.wait_ge(r_stored[s], 16 * ((n - s + S - 1) // S) + 16)

                    @block.gpsimd
                    def _(pool):
                        pool.wait_ge(st_clear, 1)

                        def scales(k, s):
                            layer_scale(pool, neg[:, s, :], var[:, s, :], rs[:, s, :], nb[:, s, :], norms * G, mixed,
                                        pool_link, scaled, k)

                        def rows_added(g, s):
                            pool.wait_ge(h_ready, g + 1)
                            nc.gpsimd.tensor_tensor(x1[:, s, :, 0:D], x1[:, s, :, 0:D],
                                                    R["beta"][:, :].unsqueeze(1).to_broadcast([P, G, D]), ALU.add).then_inc(x1_added, 1)
                        pipeline(pool, n, [(scales, 0, late), (rows_added, 1)], S)

                    @block.vector
                    def _(dve):
                        nc.vector.memset(st[:, :, :, :], 0.0).then_inc(st_clear, 1)
                        dve.wait_ge(st_clear, 1)
                        for s in range(S):
                            dve.sem_inc(stored[s], 16)
                            dve.sem_inc(r_stored[s], 16)
                        nc.vector.memset(bank[0][:, :], 0.0)
                        nc.vector.memset(bank[1][:, :], 0.0).then_inc(gram_zero, 1)
                        nc.vector.memset(r[:, :, :, 2 * D:2 * D + 1], 1.0)
                        nc.vector.memset(r[:, :, :, 2 * D + 2:RW], 0.0)

                        def sums_of(i, tiles, g, s):
                            for j, x in enumerate(tiles):
                                last = nc.vector.bn_stats(st[:, (s + 2 * i) % S, i * G + j, :], x)
                            last.then_inc(summed[i], 1)

                        def first(g, s):
                            dve.wait_ge(rows_in[s], slot_count(g, s))
                            for j in range(G):
                                last = nc.vector.scalar_tensor_tensor(
                                    out=x1[:, s, j, 0:D], in0=he_last[1][:, :],
                                    scalar=x1[:, s, j, D + M_CHIGH:D + M_CHIGH + 1], in1=x1[:, s, j, 0:D],
                                    op0=ALU.mult, op1=ALU.add)
                            last.then_inc(x_ready, 1)

                        def first_sums(g, s):
                            dve.wait_ge(x_ready, g + 1)
                            sums_of(0, [x1[:, s, j, 0:D] for j in range(G)], g, s)

                        def bias_added(g, s):
                            dve.wait_ge(h_ready, g + 1)
                            nc.vector.tensor_tensor(h[:, s, :, :], h[:, s, :, :],
                                                    R["bo"][:, :].unsqueeze(1).to_broadcast([P, G, D]), ALU.add).then_inc(hb_link, 1)

                        def summed_rows(i):
                            def part(g, s):
                                dve.wait_ge(summed[i], g + 1)
                            return part
                        differences, squares, total, variance = summing_parts(dve, st, tmp, neg, var, sum_link, mixed)

                        def second(g, s):
                            dve.wait_ge(hb_link, g + 1)
                            sums_of(1, [h[:, s, j, :] for j in range(G)], g, s)

                        def third(g, s):
                            dve.wait_ge(z_ready, g + 1)
                            dve.wait_ge(x1_added, g + 1)
                            nc.vector.tensor_copy(m[:, s, :, :], x1[:, s, :, D:XW])
                            dve.wait_ge(stored[s], slot_count(g, s))
                            nc.vector.tensor_tensor(x2[:, s, :, :], h[:, s, :, :],
                                                    R["gamma"][:, :].unsqueeze(1).to_broadcast([P, G, D]), ALU.mult).then_inc(x2_link, 1)

                        def third_sums(g, s):
                            dve.wait_ge(x2_ready, g + 1)
                            dve.sem_inc(used, 1)
                            sums_of(2, [x2[:, s, j, :] for j in range(G)], g, s)

                        def third_added(g, s):
                            dve.wait_ge(x2_link, g + 1)
                            nc.vector.tensor_tensor(x2[:, s, :, :], x2[:, s, :, :], x1[:, s, :, 0:D], ALU.add).then_inc(x2_ready, 1)

                        def fourth_sums(g, s):
                            dve.wait_ge(x3_ready, g + 1)
                            sums_of(3, [r[:, s, j, 0:D] for j in range(G)], g, s)

                        def fourth(g, s):
                            dve.wait_ge(h2_ready, g + 1)
                            dve.wait_ge(r_stored[s], slot_count(g, s))
                            nc.vector.tensor_tensor(r[:, s, :, 0:D], x2[:, s, :, :], h2[:, s, :, :], ALU.add)
                            nc.vector.tensor_copy(r[:, s, :, 2 * D + 1], m[:, s, :, M_GINV])
                            nc.vector.tensor_copy(u[:, s, :, D], m[:, s, :, M_Q])
                            nc.vector.tensor_copy(u[:, s, :, D + 1], m[:, s, :, M_BARE]).then_inc(x3_ready, 1)
                        pipeline(dve, n, [(first, 0), (fourth, 6), (third, 4), (first_sums, 0), (third_added, 4),
                                          (bias_added, 2), (fourth_sums, 6), (second, 2), (third_sums, 4)] +
                                 [(summed_rows(i), 2 * i) for i in range(norms)] +
                                 [(part, 0, late) for part in (differences, squares, total, variance)], S)
                        dve.wait_ge(gram_done, n)
                        nc.vector.tensor_copy(gram1[:, :], bank[0][:, 0:D + 2])
                        nc.vector.tensor_copy(gram2[:, :], bank[1][0:2, 0:D + 2])

                    @block.scalar
                    def _(act):
                        act.preload_act_table(ACT.Relu)

                        def normed(i, out, x, func, ready):
                            def part(g, s):
                                act.wait_ge(scaled, g + 2 * i + 1)
                                at = (s + 2 * i) % S
                                for j in range(i * G, i * G + G):
                                    last = nc.scalar.activation(out(s, j - i * G), x(s, j - i * G), func,
                                                                bias=nb[:, at, j:j + 1], scale=rs[:, at, j:j + 1])
                                last.then_inc(ready, 1)
                            return part

                        def weighted(g, s):
                            act.wait_ge(h3_ready, g + 1)
                            for j in range(G):
                                last = nc.scalar.activation(u[:, s, j, 0:D], r[:, s, j, D:2 * D], ACT.Copy,
                                                            scale=m[:, s, j, M_Q:M_Q + 1])
                            last.then_inc(u_ready, 1)

                        h1 = normed(0, lambda s, j: h[:, s, j, :], lambda s, j: x1[:, s, j, 0:D], ACT.Relu, h_ready)
                        z = normed(1, lambda s, j: h[:, s, j, :], lambda s, j: h[:, s, j, :], ACT.Identity, z_ready)
                        second_h = normed(2, lambda s, j: h2[:, s, j, :], lambda s, j: x2[:, s, j, :], ACT.Relu, h2_ready)
                        third_h = normed(3, lambda s, j: r[:, s, j, D:2 * D], lambda s, j: r[:, s, j, 0:D], ACT.Relu, h3_ready)
                        pipeline(act, n, [(second_h, 4), (z, 2), (h1, 0), (third_h, 6), (weighted, 6)], S)

                    @block.tensor
                    def _(pe):
                        def moments(g, s):
                            pe.wait_ge(u_ready, g + 1)
                            for j in range(G):
                                nc.tensor.matmul(bank[0][:, 0:D + 2], u[:, s, j, 0:D], u[:, s, j, :], start=False,
                                                 stop=False, skip_group_check=True)
                                last = nc.tensor.matmul(bank[1][0:2, 0:D + 2], u[:, s, j, D:D + 2], u[:, s, j, :],
                                                        start=False, stop=False, skip_group_check=True)
                            last.then_inc(gram_done, 1)
                        pe.wait_ge(gram_zero, 1)
                        pipeline(pe, n, [(moments, 0)], S)

        bare_nodes()
        with phase() as c:
            S8 = 8
            last_norm = 6
            ix = sb("ix", [P, 4, 2 * G], I32, c)
            xs, hs, sums = (sb(n, [P, 4, G, D], F32, c) for n in ("xs", "hs", "sums"))
            xd, hd = (sb(n, [P, S8, G, D], F32, c) for n in ("xd", "hd"))
            efT = sb("efT", [64, 4, G * P], F32, c)
            bc = sb("bc", [P, 4, G * P], I32, c)
            st = sb("st", [P, S8, 3 * G, 6], F32, c)
            tmp = sb("tmp", [P, 2, 3, 3 * G], F32, c)
            neg, var, rs, nb = (sb(n, [P, S8, 3 * G], F32, c) for n in ("neg", "var", "rs", "nb"))
            sum_link, mixed = sem("mlp_sum_link"), sem("mlp_mixed")
            hsT, hdT = (sb(n, [P, 2, G * P], F32, c) for n in ("hsT", "hdT"))
            hid = sb("hid", [32, 2, G * P], F32, c)
            msg = sb("msg", [P, 2, G * P], F32, c)
            nhid = sb("nhid", [65, 2, G * P], F32, c)
            nmsg = sb("nmsg", [P, 2, G, D], F32, c)
            same, carry = (sb(n, [P, 2, G, P], F32, c) for n in ("same", "carry"))
            r = sb("r", [P, 4, G, RW], F32, c)
            ix_ready, pool_link, summed, summed3, scaled, h_ready, hT_ps, hsT_in, hdT_in, hid_ps, hid_in, msg_ps, msg_in, \
                nhid_ps, nhid_in, nmsg_ps, nmsg_in, same_ready, sum_ps, sum_in, set_up, r_link, x3_ready, h3_ready = (
                    sem(f"mlp_{n}") for n in (
                        "ix_ready", "pool_link", "summed", "summed3", "scaled", "h_ready", "hT_ps", "hsT_in", "hdT_in",
                        "hid_ps", "hid_in", "msg_ps", "msg_in", "nhid_ps", "nhid_in", "nmsg_ps", "nmsg_in", "same_ready",
                        "sum_ps", "sum_in", "set_up", "r_link", "x3_ready", "h3_ready"))
            rows_in = [sem(f"mlp_rows_in{s}") for s in range(S8)]
            ef_in, bc_in, stored = ([sem(f"mlp_{n}{s}") for s in range(4)] for n in ("ef_in", "bc_in", "stored"))
            hs_p, hd_p, hid_p, msg_p, nhid_p, nmsg_p, sum_p = bank[0], bank[1], bank[2], bank[3], bank[4], bank[5], bank[6]

            def count8(g, s, dmas):
                return (g - s) * (2 * dmas) + 16 * dmas

            def count4(g, s):
                return (g - s % 4) * 4 + 16

            with nc.Block() as block:
                @block.gpsimd
                def _(pool):
                    pool.wait_ge(set_up, 1)

                    def src_used(g, s):
                        hold("pool", pool, h_ready, g + 1)

                    def dst_used(g, s):
                        hold("pool", pool, x3_ready, g + 1)

                    def rows(g, s):
                        at = s % 4
                        nc.gpsimd.tensor_copy(ix[:, at, 0:G], table_src[:, bass.ds(g * G, G)])
                        nc.gpsimd.tensor_copy(ix[:, at, G:2 * G], table_dst[:, bass.ds(g * G, G)]).then_inc(ix_ready, 1)
                        hold("pool", pool, ix_ready, g + 1)
                        for j in range(G):
                            gather(pool, xs[:, at, j, :], x2_d, ix[:, at, j:j + 1], rows_in[s])
                            gather(pool, xd[:, s, j, :], x2_d, ix[:, at, G + j:G + j + 1], rows_in[s])

                    def scales(k, s):
                        layer_scale(pool, neg[:, s, :], var[:, s, :], rs[:, s, :], nb[:, s, :], 3 * G, mixed, pool_link,
                                    scaled, k)
                    pipeline(pool, NGE, [(src_used, 4), (dst_used, S8), (rows, 0), (scales, 1, last_norm)], S8)

                @block.sync
                def _(sp):
                    def ef_used(g, s):
                        sp.wait_ge(hid_ps, g + 1)

                    def load_ef(g, s):
                        sp.dma_start(efT[:, s % 4, :], t["edge_attr_T"][:, bass.ds(g * (G * P), G * P)]).then_inc(ef_in[s % 4], 16)

                    def bc_used(g, s):
                        sp.wait_ge(same_ready, g + 1)

                    def load_bc(g, s):
                        sp.dma_start(bc[:, s % 4, :], t["dst"][bass.ds(g * (G * P), G * P)].partition_broadcast(P)).then_inc(
                            bc_in[s % 4], 16)

                    def store(g, s):
                        sp.wait_ge(h3_ready, g + 1)
                        sp.dma_start(rows_of(r_d, g, RW, NN), r[:, s % 4, :, :]).then_inc(stored[s % 4], 16)
                    pipeline(sp, NGE, [(ef_used, 4), (load_ef, 0), (bc_used, 5), (load_bc, 1), (store, 9)], S8)
                    for s in range(4):
                        sp.wait_ge(stored[s], 16 * ((NGE - s + 3) // 4) + 16)

                @block.vector
                def _(dve):
                    nc.vector.memset(nhid[64:65, :, :], 1.0)
                    nc.vector.memset(r[:, :, :, 2 * D:2 * D + 1], 1.0)
                    nc.vector.memset(r[:, :, :, 2 * D + 2:RW], 0.0)
                    nc.vector.memset(st[:, :, :, :], 0.0)
                    nc.vector.memset(sums[:, 3, G - 1, :], 0.0).then_inc(sum_in, 1)
                    dve.wait_ge(sum_in, 1)
                    dve.sem_inc(set_up, 1)
                    for s in range(4):
                        dve.sem_inc(stored[s], 16)

                    def stats(g, s):
                        dve.wait_ge(rows_in[s], count8(g, s, 2 * G))
                        for j in range(G):
                            nc.vector.bn_stats(st[:, s, j, :], xs[:, s % 4, j, :])
                        for j in range(G):
                            last = nc.vector.bn_stats(st[:, s, G + j, :], xd[:, s, j, :])
                        last.then_inc(summed, 1)

                    def hdT_copy(g, s):
                        dve.wait_ge(hT_ps, g + 1)
                        nc.vector.tensor_copy(hdT[:, s % 2, :], hd_p[:, :]).then_inc(hdT_in, 1)

                    def sames(g, s):
                        dve.wait_ge(bc_in[s % 4], count4(g, s))
                        for j in range(G):
                            to = bc[:, s % 4, j * P:(j + 1) * P]
                            nc.vector.tensor_scalar(same[:, s % 2, j, :], to, dstF[:, bass.ds(g * G + (j + 1), 1)], None,
                                                    ALU.is_equal)

                    def carries(g, s):
                        for j in range(G):
                            to = bc[:, s % 4, j * P:(j + 1) * P]
                            last = nc.vector.tensor_scalar(carry[:, s % 2, j, :], to, dstF[:, bass.ds(g * G + j, 1)],
                                                           last_row, ALU.is_equal, ALU.mult)
                        last.then_inc(same_ready, 1)

                    def own(g, s):
                        dve.wait_ge(stored[s % 4], count4(g, s))
                        nc.vector.tensor_tensor(r[:, s % 4, :, 0:D], xd[:, s, :, :], hd[:, s, :, :], ALU.add)
                        nc.vector.tensor_copy(r[:, s % 4, :, 2 * D + 1], ginv_dst[:, bass.ds(g * G, G)]).then_inc(r_link, 1)

                    def x3(g, s):
                        dve.wait_ge(r_link, g + 1)
                        dve.wait_ge(sum_in, g * G + G + 1)
                        nc.vector.tensor_tensor(r[:, s % 4, :, 0:D], r[:, s % 4, :, 0:D], sums[:, s % 4, :, :],
                                                ALU.add).then_inc(x3_ready, 1)

                    def stats3(g, s):
                        dve.wait_ge(x3_ready, g + 1)
                        for j in range(G):
                            last = nc.vector.bn_stats(st[:, (s + last_norm) % S8, 2 * G + j, :], r[:, s % 4, j, 0:D])
                        last.then_inc(summed3, 1)
                    def rows_summed(g, s):
                        dve.wait_ge(summed, g + 1)

                    def x3_summed(g, s):
                        dve.wait_ge(summed3, g + 1)
                    differences, squares, total, variance = summing_parts(dve, st, tmp, neg, var, sum_link, mixed)
                    pipeline(dve, NGE, [(hdT_copy, 4), (own, 7), (stats, 1), (x3, 7), (stats3, 7), (rows_summed, 1),
                                        (x3_summed, 1 + last_norm), (differences, 1, last_norm), (sames, 5),
                                        (squares, 1, last_norm), (carries, 5), (total, 1, last_norm),
                                        (variance, 1, last_norm)], S8)

                @block.scalar
                def _(act):
                    act.preload_act_table(ACT.Relu)
                    act.wait_ge(set_up, 1)

                    def relus(g, s):
                        act.wait_ge(scaled, g + 1)
                        for k, x, h in ((0, xs[:, s % 4, :, :], hs[:, s % 4, :, :]), (G, xd[:, s, :, :], hd[:, s, :, :])):
                            for j in range(G):
                                last = nc.scalar.activation(h[:, j, :], x[:, j, :], ACT.Relu, bias=nb[:, s, k + j:k + j + 1],
                                                            scale=rs[:, s, k + j:k + j + 1])
                        last.then_inc(h_ready, 1)

                    def hsT_copy(g, s):
                        act.wait_ge(hT_ps, g + 1)
                        nc.scalar.activation(hsT[:, s % 2, :], hs_p[:, :], ACT.Copy).then_inc(hsT_in, 1)

                    def hidden(g, s):
                        act.wait_ge(hid_ps, g + 1)
                        nc.scalar.activation(hid[:, s % 2, :], hid_p[0:32, :], ACT.Relu, bias=C["be1"][0:32, :]).then_inc(hid_in, 1)

                    def message(g, s):
                        act.wait_ge(msg_ps, g + 1)
                        nc.scalar.activation(msg[:, s % 2, :], msg_p[:, :], ACT.Relu, bias=C["be2"][:, :]).then_inc(msg_in, 1)

                    def nhidden(g, s):
                        act.wait_ge(nhid_ps, g + 1)
                        nc.scalar.activation(nhid[0:64, s % 2, :], nhid_p[0:64, :], ACT.Relu, bias=C["bn1"][0:64, :]).then_inc(nhid_in, 1)

                    def nmessage(g, s):
                        act.wait_ge(nmsg_ps, g + 1)
                        nc.scalar.activation(nmsg[:, s % 2, :, :].rearrange("p j f -> p (j f)"), nmsg_p[:, :],
                                             ACT.Relu).then_inc(nmsg_in, 1)

                    def total(j):
                        def part(g, s):
                            act.wait_ge(sum_ps, g * G + j + 1)
                            nc.scalar.activation(sums[:, s % 4, j, :], sum_p[:, 0:D], ACT.Copy).then_inc(sum_in, 1)
                        return part

                    def h3(g, s):
                        act.wait_ge(scaled, g + last_norm + 1)
                        at = (s + last_norm) % S8
                        for j in range(G):
                            last = nc.scalar.activation(r[:, s % 4, j, D:2 * D], r[:, s % 4, j, 0:D], ACT.Relu,
                                                        bias=nb[:, at, 2 * G + j:2 * G + j + 1],
                                                        scale=rs[:, at, 2 * G + j:2 * G + j + 1])
                        last.then_inc(h3_ready, 1)
                    pipeline(act, NGE, [(hsT_copy, 4), (total(0), 6), (h3, 8), (nhidden, 5), (total(1), 6), (hidden, 4),
                                        (total(2), 6), (relus, 2), (nmessage, 5), (message, 4), (total(3), 6)], S8)

                @block.tensor
                def _(pe):
                    pe.wait_ge(set_up, 1)

                    def transposes(g, s):
                        pe.wait_ge(h_ready, g + 1)
                        for x, p in ((hs[:, s % 4, :, :], hs_p), (hd[:, s, :, :], hd_p)):
                            for j in range(G):
                                last = nc.tensor.transpose(p[:, j * P:(j + 1) * P], x[:, j, :], ident)
                        last.then_inc(hT_ps, 1)

                    def hidden(g, s):
                        pe.wait_ge(hsT_in, g + 1)
                        nc.tensor.matmul(hid_p[0:32, :], W["We1a"][:, 0:32], hsT[:, s % 2, :], start=True, stop=False)
                        pe.wait_ge(hdT_in, g + 1)
                        nc.tensor.matmul(hid_p[0:32, :], W["We1b"][:, 0:32], hdT[:, s % 2, :], start=False, stop=False)
                        hold("pe", pe, ef_in[s % 4], count4(g, s))
                        nc.tensor.matmul(hid_p[0:32, :], W["We1c"][0:64, 0:32], efT[:, s % 4, :], start=False,
                                         stop=True).then_inc(hid_ps, 1)

                    def message(g, s):
                        pe.wait_ge(hid_in, g + 1)
                        nc.tensor.matmul(msg_p[:, :], W["We2"][0:32, :], hid[:, s % 2, :], start=True, stop=True).then_inc(msg_ps, 1)

                    def nhidden(g, s):
                        nc.tensor.matmul(nhid_p[0:64, :], W["Wn1a"][:, 0:64], hdT[:, s % 2, :], start=True, stop=False)
                        pe.wait_ge(msg_in, g + 1)
                        nc.tensor.matmul(nhid_p[0:64, :], W["Wn1b"][:, 0:64], msg[:, s % 2, :], start=False,
                                         stop=True).then_inc(nhid_ps, 1)

                    def nmessage(g, s):
                        pe.wait_ge(nhid_in, g + 1)
                        for j in range(G):
                            last = nc.tensor.matmul(nmsg_p[:, j * P:(j + 1) * P], nhid[:, s % 2, j * P:(j + 1) * P],
                                                    W["Wn2"][0:65, :], start=True, stop=True)
                        last.then_inc(nmsg_ps, 1)

                    def total(j):
                        def part(g, s):
                            if j == 0:
                                pe.wait_ge(same_ready, g + 1)
                                pe.wait_ge(nmsg_in, g + 1)
                            before = sums[:, s % 4, j - 1, :] if j else sums[:, (s - 1) % 4, G - 1, :]
                            pe.wait_ge(sum_in, g * G + j + 1)
                            nc.tensor.matmul(sum_p[:, 0:D], same[:, s % 2, j, :], nmsg[:, s % 2, j, :], start=True, stop=False)
                            nc.tensor.matmul(sum_p[:, 0:D], carry[:, s % 2, j, :], before, start=False, stop=True).then_inc(sum_ps, 1)
                        return part
                    pipeline(pe, NGE, [(total(0), 6), (nhidden, 5), (total(1), 6), (hidden, 4), (total(2), 6), (nmessage, 5),
                                       (message, 4), (total(3), 6), (transposes, 3)], S8)

        with phase() as c:
            S8 = 8
            ix = sb("ix", [P, S8, 2 * G], I32, c)
            rs_, rd = (sb(n, [P, S8, G, RW], F32, c) for n in ("rs_", "rd"))
            bc = sb("bc", [P, 4, G * P], I32, c)
            wt, rg, q = (sb(n, [P, S8, G], F32, c) for n in ("wt", "rg", "q"))
            same, carry = (sb(n, [P, 4, G, P], F32, c) for n in ("same", "carry"))
            sums = sb("sums", [P, 4, G, TW], F32, c)
            u = sb("u", [P, 4, G, D + 2], F32, c)
            ix_ready, wt_link, q_link, same_ready, sum_ps, sum_in, w_ready, u_ready, gram_done, gram_zero = (
                sem(f"gc_{n}") for n in ("ix_ready", "wt_link", "q_link", "same_ready", "sum_ps", "sum_in", "w_ready",
                                         "u_ready", "gram_done", "gram_zero"))
            src_in, dst_in, scattered = ([sem(f"gc_{n}{s}") for s in range(S8)] for n in ("src_in", "dst_in", "scattered"))
            bc_in = [sem(f"gc_bc_in{s}") for s in range(4)]
            sum_p = bank[4]

            def count8(g, s, dmas):
                return (g - s) * (2 * dmas) + 16 * dmas

            with nc.Block() as block:
                @block.gpsimd
                def _(pool):
                    def written(g, s):
                        hold("pool", pool, scattered[s], count8(g, s, G))
                        hold("pool", pool, u_ready, g + 1)

                    def rows(g, s):
                        nc.gpsimd.tensor_copy(ix[:, s, 0:G], table_src[:, bass.ds(g * G, G)])
                        nc.gpsimd.tensor_copy(ix[:, s, G:2 * G], out_row[:, bass.ds(g * G, G)]).then_inc(ix_ready, 1)
                        hold("pool", pool, ix_ready, g + 1)
                        for j in range(G):
                            gather(pool, rs_[:, s, j, :], r_d, ix[:, s, j:j + 1], src_in[s])

                    def scatter(g, s):
                        hold("pool", pool, w_ready, g + 1)
                        for j in range(G):
                            pool.indirect_dma_start(out=r_d, out_offset=bass.IndirectOffsetOnAxis(ap=ix[:, s, G + j:G + j + 1], axis=0),
                                                    in_=rd[:, s, j, :], in_offset=None).then_inc(scattered[s], 16)
                    pipeline(pool, NGE, [(written, S8), (rows, 0), (scatter, 5)], S8)

                @block.sync
                def _(sp):
                    def load(g, s):
                        sp.wait_ge(ix_ready, g + 1)
                        sp.dma_start(rd[:, s, :, :], rows_of(r_d, g, RW, NN)).then_inc(dst_in[s], 16)

                    def bc_used(g, s):
                        sp.wait_ge(same_ready, g + 1)

                    def load_bc(g, s):
                        sp.dma_start(bc[:, s % 4, :], t["dst"][bass.ds(g * (G * P), G * P)].partition_broadcast(P)).then_inc(
                            bc_in[s % 4], 16)
                    pipeline(sp, NGE, [(bc_used, 4), (load_bc, 0), (load, 0)], S8)

                @block.vector
                def _(dve):
                    nc.vector.memset(bank[0][:, :], 0.0)
                    nc.vector.memset(bank[1][:, :], 0.0).then_inc(gram_zero, 1)
                    nc.vector.memset(sums[:, 3, G - 1, :], 0.0).then_inc(sum_in, 1)
                    dve.sem_inc(gram_done, 4)

                    def weights(g, s):
                        dve.wait_ge(src_in[s], count8(g, s, G))
                        nc.vector.tensor_tensor(wt[:, s, :], rs_[:, s, :, 2 * D + 1], ew[:, bass.ds(g * G, G)], ALU.mult)
                        dve.wait_ge(dst_in[s], count8(g, s, 1))
                        nc.vector.reciprocal(rg[:, s, :], rd[:, s, :, 2 * D + 1])
                        nc.vector.tensor_tensor(q[:, s, :], rd[:, s, :, 2 * D + 1], rd[:, s, :, 2 * D + 1],
                                                ALU.mult).then_inc(wt_link, 1)

                    def ends(g, s):
                        dve.wait_ge(wt_link, g + 1)
                        nc.vector.tensor_tensor(q[:, s, :], q[:, s, :], seg_end[:, bass.ds(g * G, G)], ALU.mult).then_inc(q_link, 1)

                    def sames(g, s):
                        dve.wait_ge(bc_in[s % 4], (g - s % 4) * 4 + 16)
                        for j in range(G):
                            to = bc[:, s % 4, j * P:(j + 1) * P]
                            nc.vector.tensor_scalar(same[:, s % 4, j, :], to, dstF[:, bass.ds(g * G + (j + 1), 1)],
                                                    wt[:, s, j:j + 1], ALU.is_equal, ALU.mult)
                            last = nc.vector.tensor_scalar(carry[:, s % 4, j, :], to, dstF[:, bass.ds(g * G + j, 1)],
                                                           last_row, ALU.is_equal, ALU.mult)
                        last.then_inc(same_ready, 1)

                    def own(g, s):
                        hold("dve", dve, gram_done, g + 1)
                        nc.vector.tensor_copy(u[:, s % 4, :, D + 1], seg_end[:, bass.ds(g * G, G)])
                        dve.wait_ge(sum_in, g * G + G + 1)
                        dve.wait_ge(q_link, g + 1)
                        for j in range(G):
                            last = nc.vector.scalar_tensor_tensor(
                                out=rd[:, s, j, D:2 * D + 1], in0=sums[:, s % 4, j, 0:D + 1], scalar=rg[:, s, j:j + 1],
                                in1=rd[:, s, j, D:2 * D + 1], op0=ALU.mult, op1=ALU.add)
                        last.then_inc(w_ready, 1)
                    pipeline(dve, NGE, [(weights, 1), (own, 4), (ends, 1), (sames, 1)], S8)
                    dve.wait_ge(gram_done, NGE + 4)
                    nc.vector.tensor_tensor(gram1[:, :], gram1[:, :], bank[0][:, 0:D + 2], ALU.add)
                    nc.vector.tensor_tensor(gram2[:, :], gram2[:, :], bank[1][0:2, 0:D + 2], ALU.add)

                @block.scalar
                def _(act):
                    act.preload_act_table(ACT.Copy)

                    def total(j):
                        def part(g, s):
                            act.wait_ge(sum_ps, g * G + j + 1)
                            nc.scalar.activation(sums[:, s % 4, j, 0:D + 1], sum_p[:, 0:D + 1], ACT.Copy).then_inc(sum_in, 1)
                        return part

                    def weighted(j):
                        def part(g, s):
                            act.wait_ge(w_ready, g + 1)
                            ins = nc.scalar.activation(u[:, s % 4, j, 0:D + 1], rd[:, s, j, D:2 * D + 1], ACT.Copy,
                                                       scale=q[:, s, j:j + 1])
                            if j == G - 1:
                                ins.then_inc(u_ready, 1)
                        return part
                    pipeline(act, NGE, [p for j in range(G) for p in ((total(j), 2), (weighted(j), 5))], S8)

                @block.tensor
                def _(pe):
                    pe.wait_ge(gram_zero, 1)

                    def total(j):
                        def part(g, s):
                            if j == 0:
                                pe.wait_ge(same_ready, g + 1)
                            before = sums[:, s % 4, j - 1, 0:D + 1] if j else sums[:, (s - 1) % 4, G - 1, 0:D + 1]
                            pe.wait_ge(sum_in, g * G + j + 1)
                            nc.tensor.matmul(sum_p[:, 0:D + 1], same[:, s % 4, j, :], rs_[:, s, j, D:2 * D + 1], start=True, stop=False)
                            nc.tensor.matmul(sum_p[:, 0:D + 1], carry[:, s % 4, j, :], before, start=False,
                                             stop=True).then_inc(sum_ps, 1)
                        return part

                    def moments(j):
                        def part(g, s):
                            if j == 0:
                                pe.wait_ge(u_ready, g + 1)
                            v = u[:, s % 4, j, :]
                            nc.tensor.matmul(bank[0][:, 0:D + 2], v[:, 0:D], v, start=False, stop=False, skip_group_check=True)
                            last = nc.tensor.matmul(bank[1][0:2, 0:D + 2], v[:, D:D + 2], v, start=False, stop=False,
                                                    skip_group_check=True)
                            if j == G - 1:
                                last.then_inc(gram_done, 1)
                        return part
                    pipeline(pe, NGE, [p for j in range(G) for p in ((total(j), 2), (moments(j), 6))], S8)

        Wbn = sb("Wbn", [P, D])
        bbn = sb("bbn", [P, D])
        tbn = sb("tbn", [P, D])
        with phase() as c:
            y1, z1, var_, sc, half = (sb(n, [P, D], F32, c) for n in ("y1", "z1", "var_", "sc", "half"))
            y2, z2 = (sb(n, [2, D], F32, c) for n in ("y2", "z2"))
            mean = sb("mean", [P, D], F32, c)
            y_ps, z_ready, e_ps, link, var_ready, pow_done = (sem(f"bn_{n}") for n in ("y_ps", "z_ready", "e_ps", "link", "var_ready", "pow_done"))
            with nc.Block() as block:
                @block.tensor
                def _(pe):
                    nc.tensor.matmul(bank[0][:, 0:D], gram1[:, 0:D], W["W3"][:, :], start=True, stop=False)
                    nc.tensor.matmul(bank[0][:, 0:D], gram2[:, 0:D], wb[:, :], start=False, stop=True)
                    nc.tensor.matmul(bank[1][0:2, 0:D], gram1[:, D:D + 2], W["W3"][:, :], start=True, stop=False)
                    nc.tensor.matmul(bank[1][0:2, 0:D], gram2[:, D:D + 2], wb[:, :], start=False, stop=True).then_inc(y_ps, 1)
                    pe.wait_ge(z_ready, 1)
                    nc.tensor.matmul(bank[2][:, 0:D], ones, z1[:, :], start=True, stop=False)
                    nc.tensor.matmul(bank[2][:, 0:D], ones[0:2, :], z2[:, :], start=False, stop=True)
                    nc.tensor.matmul(bank[3][:, 0:D], K[0:2, K_ROW1:K_ROW1 + P], y2[:, :], start=True, stop=True).then_inc(e_ps, 1)

                @block.gpsimd
                def _(pool):
                    nc.gpsimd.memset(half[:, :], -0.5).then_inc(pow_done, 1)
                    pool.wait_ge(pow_done, 1)
                    pool.wait_ge(var_ready, 1)
                    nc.gpsimd.tensor_tensor(sc[:, :], var_[:, :], half[:, :], ALU.pow).then_inc(pow_done, 1)

                @block.vector
                def _(dve):
                    k = [0]

                    def chain(ins):
                        k[0] += 1
                        ins.then_inc(link, 1)
                        dve.wait_ge(link, k[0])

                    dve.wait_ge(y_ps, 1)
                    chain(nc.vector.tensor_tensor(z1[:, :], W["W3"][:, :], bank[0][:, 0:D], ALU.mult))
                    chain(nc.vector.tensor_copy(y2[:, :], bank[1][0:2, 0:D]))
                    nc.vector.tensor_tensor(z2[:, :], wb[:, :], y2[:, :], ALU.mult).then_inc(z_ready, 1)
                    dve.wait_ge(e_ps, 1)
                    chain(nc.vector.tensor_scalar(mean[:, :], bank[3][:, 0:D], 1.0 / N, None, ALU.mult))
                    chain(nc.vector.tensor_tensor(z1[:, :], mean[:, :], mean[:, :], ALU.mult))
                    chain(nc.vector.tensor_scalar(y1[:, :], bank[2][:, 0:D], 1.0 / N, EPS, ALU.mult, ALU.add))
                    chain(nc.vector.tensor_tensor(y1[:, :], y1[:, :], z1[:, :], ALU.subtract))
                    nc.vector.tensor_scalar(var_[:, :], y1[:, :], EPS, None, ALU.max).then_inc(var_ready, 1)
                    dve.wait_ge(pow_done, 2)
                    chain(nc.vector.tensor_tensor(sc[:, :], sc[:, :], R["bgamma"][:, :], ALU.mult))
                    chain(nc.vector.tensor_tensor(Wbn[:, :], W["W3"][:, :], sc[:, :], ALU.mult))
                    chain(nc.vector.tensor_tensor(bbn[:, :], R["b3"][:, :], sc[:, :], ALU.mult))
                    chain(nc.vector.tensor_tensor(z1[:, :], mean[:, :], sc[:, :], ALU.mult))
                    chain(nc.vector.tensor_tensor(tbn[:, :], R["bbeta"][:, :], z1[:, :], ALU.subtract))

        with phase() as c:
            S8 = 8
            r = sb("r", [P, S8, G, RW], F32, c)
            wT = sb("wT", [P, S8, G * P], F32, c)
            y = sb("y", [P, S8, G, D], F32, c)
            g2 = sb("g2", [P, S8, G], F32, c)
            wT_ps, wT_in, y_ps, y_used, link, link2, y_ready = (sem(f"out_{n}") for n in (
                "wT_ps", "wT_in", "y_ps", "y_used", "link", "link2", "y_ready"))
            rows_in = [sem(f"out_rows_in{s}") for s in range(S8)]
            stored = [sem(f"out_stored{s}") for s in range(S8)]

            with nc.Block() as block:
                @block.sync
                def _(sp):
                    for s in range(S8):
                        sp.sem_inc(stored[s], 16)

                    def load(g, s):
                        sp.wait_ge(stored[s], (g - s) * 2 + 16)
                        sp.dma_start(r[:, s, :, :], node_rows_of(r_d, g, RW)).then_inc(rows_in[s], 16)
                    pipeline(sp, NGN, [(load, 0)], S8)

                @block.tensor
                def _(pe):
                    def transposes(g, s):
                        pe.wait_ge(rows_in[s], (g - s) * 2 + 16)
                        for j in range(G):
                            last = nc.tensor.transpose(bank[s % 2][:, j * P:(j + 1) * P], r[:, s, j, D:2 * D], ident)
                        last.then_inc(wT_ps, 1)

                    def products(g, s):
                        pe.wait_ge(wT_in, g + 1)
                        pe.wait_ge(y_used, g + 1)
                        for j in range(G):
                            last = nc.tensor.matmul(bank[2 + s % 2][:, j * P:(j + 1) * P], wT[:, s, j * P:(j + 1) * P],
                                                    Wbn[:, :], start=True, stop=True)
                        last.then_inc(y_ps, 1)
                    pipeline(pe, NGN, [(transposes, 0), (products, 1)], S8)

                @block.scalar
                def _(act):
                    act.preload_act_table(ACT.Copy)

                    def to_sbuf(g, s):
                        act.wait_ge(wT_ps, g + 1)
                        nc.scalar.activation(wT[:, s, :], bank[s % 2][:, :], ACT.Copy).then_inc(wT_in, 1)

                    def store(g, s):
                        act.wait_ge(y_ready, g + 1)
                        act.dma_start(node_rows_of(t["out"], g, D), y[:, s, :, :]).then_inc(stored[s], 16)
                    pipeline(act, NGN, [(to_sbuf, 0), (store, 2)], S8)
                    for s in range(S8):
                        act.wait_ge(stored[s], 16 * ((NGN - s + S8 - 1) // S8) + 16)

                @block.vector
                def _(dve):
                    dve.sem_inc(y_used, 2)

                    def part(g, s):
                        dve.wait_ge(y_ps, g + 1)
                        for j in range(G):
                            last = nc.vector.scalar_tensor_tensor(
                                out=y[:, s, j, :], in0=bbn[:, :], scalar=r[:, s, j, 2 * D:2 * D + 1],
                                in1=bank[2 + s % 2][:, j * P:(j + 1) * P], op0=ALU.mult, op1=ALU.add)
                        last.then_inc(y_used, 1)
                        nc.vector.tensor_tensor(g2[:, s, :], r[:, s, :, 2 * D + 1], r[:, s, :, 2 * D + 1], ALU.mult).then_inc(link, 1)
                        dve.wait_ge(link, g + 1)
                        for j in range(G):
                            last = nc.vector.scalar_tensor_tensor(out=y[:, s, j, :], in0=y[:, s, j, :], scalar=g2[:, s, j:j + 1],
                                                                  in1=tbn[:, :], op0=ALU.mult, op1=ALU.add)
                        last.then_inc(link2, 1)
                        dve.wait_ge(link2, g + 1)
                        nc.vector.scalar_tensor_tensor(out=y[:, s, :, :], in0=y[:, s, :, :], scalar=0.0, in1=r[:, s, :, 0:D],
                                                       op0=ALU.max, op1=ALU.add).then_inc(y_ready, 1)
                    pipeline(dve, NGN, [(part, 0)], S8)
    return


_FLOATS = ["x", "edge_attr_64", "L0_gnn_W1", "L0_gnn_b1", "L0_gnn_W2", "L0_gnn_b2", "L1_gnn_Wqk", "L1_gnn_bqk",
           "L1_gnn_Wv", "L1_gnn_bv", "L1_gnn_Wo", "L1_gnn_bo", "L1_gnn_gamma", "L1_gnn_beta", "L2_gnn_We1",
           "L2_gnn_be1", "L2_gnn_We2", "L2_gnn_be2", "L2_gnn_Wn1", "L2_gnn_bn1", "L2_gnn_Wn2", "L2_gnn_bn2",
           "L3_gnn_W", "L3_gnn_b", "L3_gnn_gamma", "L3_gnn_beta"]
DEBUG = False


def constants():
    import numpy as np

    k = np.zeros((P, K_COLS), np.float32)
    p = np.arange(P)
    k[:, K_ID:K_ID + P] = np.eye(P)
    k[:, K_AFTER:K_AFTER + P] = p[None, :] > p[:, None]
    k[:, K_IOTA:K_IOTA + NLO] = np.arange(NLO)
    for b in range(2):
        k[:HB, K_NODE + b * NLO:K_NODE + (b + 1) * NLO] = (b * HB + np.arange(HB))[:, None] * NLO + np.arange(NLO)
    k[:, K_EDGE:K_EDGE + NT] = np.arange(NT) * P + p[:, None]
    k[P - 1, K_LAST] = 1
    k[:, K_DUMP] = NN + p
    k[:, K_ONE:K_ONE + P] = 1
    k[1, K_ROW1:K_ROW1 + P] = 1
    return k


def kernel(**inputs):
    import numpy as np
    import concourse.bacc as bacc
    from concourse.bass_utils import run_bass_kernel_spmd

    def padded(v, rows, fill):
        v = np.asarray(v)
        out = np.full((rows,) + v.shape[1:], fill, v.dtype)
        out[:len(v)] = v
        return out

    arrays = {n: np.ascontiguousarray(np.asarray(inputs[n])) for n in _FLOATS}
    arrays["x"] = padded(arrays["x"], NN, 0)
    arrays["edge_attr_T"] = np.ascontiguousarray(padded(arrays.pop("edge_attr_64"), EP, 0).T)
    arrays["src"] = padded(inputs["src"], EP, N)
    arrays["dst"] = padded(inputs["dst"], EP, N)
    arrays["next_dst"] = padded(arrays["dst"][1:], EP, N + 1)
    arrays["edge_weight"] = padded(inputs["edge_weight"], EP, 0)
    arrays["consts"] = constants()
    nc = bacc.Bacc("TRN2", target_bir_lowering=False, num_devices=1)
    t = {n: nc.dram_tensor(n, a.shape, mybir.dt.from_np(a.dtype), kind="ExternalInput").ap() for n, a in arrays.items()}
    t["out"] = nc.dram_tensor("out", (NN, D), F32, kind="ExternalOutput").ap()
    build(nc, t, DEBUG)
    r = run_bass_kernel_spmd(nc, [arrays], core_ids=[0])
    return r.results[0]["out"][:N]
```
